# Optimizing a Trainium2 kernel written in Bass

```python
import numpy as np
import jax
import jax.numpy as jnp

def _softmax(x, axis=-1):
    return jax.nn.softmax(x, axis=axis)

def _gelu(x):
    return jax.nn.gelu(x, approximate=True)

def _silu(x):
    return jax.nn.silu(x)

def _sigmoid(x):
    return jax.nn.sigmoid(x)

def _layernorm(x, axis=-1, eps=1e-05):
    m = jnp.mean(x, axis=axis, keepdims=True)
    v = jnp.var(x, axis=axis, keepdims=True)
    return (x - m) / jnp.sqrt(v + eps)

def _scatter_add(tgt, idx, src, axis=0):
    return tgt.at[idx].add(src)

def _segment_sum(src, seg, n):
    return jax.ops.segment_sum(src, seg, n)
kernel_name = 'mk_seq_postln_d1_jaxref_r4_b46bf4'

def setup_inputs(seed: int=0):
    np.random.seed(seed)
    _w = jnp.asarray

    def _L0_attn_setup():
        import jax, jax.numpy as jnp
        import numpy as np
        BATCH, SEQ, D_MODEL = (2, 1024, 256)
        N_HEADS = 16
        HEAD_DIM = D_MODEL // N_HEADS
        WINDOW = 128
        EPS = 1e-05

        def layer_norm(x, g, b):
            m = x.mean(-1, keepdims=True)
            v = ((x - m) ** 2).mean(-1, keepdims=True)
            return (x - m) * jax.lax.rsqrt(v + EPS) * g + b

        def sliding_window_attn(q, k, v, window, scale):
            B, H, S, D = q.shape
            W = window
            C = S // W
            qc = q.reshape(B, H, C, W, D)
            kc = k.reshape(B, H, C, W, D)
            vc = v.reshape(B, H, C, W, D)
            kprev = jnp.pad(kc, ((0, 0), (0, 0), (1, 0), (0, 0), (0, 0)))[:, :, :C]
            vprev = jnp.pad(vc, ((0, 0), (0, 0), (1, 0), (0, 0), (0, 0)))[:, :, :C]
            kcat = jnp.concatenate([kprev, kc], axis=3)
            vcat = jnp.concatenate([vprev, vc], axis=3)
            scores = jnp.einsum('bhcqd,bhckd->bhcqk', qc, kcat) * scale
            i = jnp.arange(W)[:, None]
            j = jnp.arange(2 * W)[None, :]
            band = (j >= i + 1) & (j <= i + W)
            cidx = jnp.arange(C)[:, None, None]
            valid = band[None] & ((cidx > 0) | (j[None] >= W))
            scores = jnp.where(valid[None, None], scores, -jnp.inf)
            attn = jax.nn.softmax(scores, axis=-1)
            out = jnp.einsum('bhcqk,bhckd->bhcqd', attn, vcat)
            return out.reshape(B, H, S, D)
        key = jax.random.key(seed)
        ks = jax.random.split(key, 8)
        s = 0.02
        d = D_MODEL
        return {'x': jax.random.normal(ks[0], (BATCH, SEQ, d), dtype=jnp.float32), 'w_qkv': jax.random.normal(ks[1], (3 * d, d), dtype=jnp.float32) * s, 'w_o': jax.random.normal(ks[2], (d, d), dtype=jnp.float32) * s, 'ln1_g': jnp.ones((d,), jnp.float32), 'ln1_b': jnp.zeros((d,), jnp.float32), 'ln2_g': jnp.ones((d,), jnp.float32), 'ln2_b': jnp.zeros((d,), jnp.float32), 'mlp_w1': jax.random.normal(ks[3], (4 * d, d), dtype=jnp.float32) * s, 'mlp_b1': jnp.zeros((4 * d,), jnp.float32), 'mlp_w2': jax.random.normal(ks[4], (d, 4 * d), dtype=jnp.float32) * s, 'mlp_b2': jnp.zeros((d,), jnp.float32)}
    _L0_attn_in = _L0_attn_setup()

    def _L0_ffn_setup():
        import jax, jax.numpy as jnp
        import numpy as np
        DIM = 256
        DEPTH = 2
        HEADS = 8
        DIM_HEAD = 64
        WINDOW = 128
        INNER = HEADS * DIM_HEAD
        HID = int(DIM * 4 * 2 / 3)
        B, N = (2, 2048)
        QK_SCALE = 8.0

        def shift_token(t):
            t1, t2 = jnp.split(t, 2, axis=-1)
            t2 = jnp.pad(t2, ((0, 0), (1, 0), (0, 0)))[:, :-1]
            return jnp.concatenate([t1, t2], axis=-1)

        def l2norm(t):
            return t / jnp.clip(jnp.linalg.norm(t, axis=-1, keepdims=True), 1e-12)

        def rotate_half(x):
            x1, x2 = jnp.split(x, 2, axis=-1)
            return jnp.concatenate([-x2, x1], axis=-1)

        def rotary_xpos(q, k):
            n = q.shape[-2]
            half_idx = jnp.arange(0, DIM_HEAD, 2, dtype=jnp.float32)
            inv_freq = 1.0 / 10000.0 ** (half_idx / DIM_HEAD)
            t = jnp.arange(n, dtype=jnp.float32)
            freqs = t[:, None] * inv_freq[None, :]
            freqs = jnp.concatenate([freqs, freqs], axis=-1)
            base = (half_idx + 0.4 * DIM_HEAD) / (1.4 * DIM_HEAD)
            power = (t - n // 2) / float(WINDOW // 2)
            scale = base[None, :] ** power[:, None]
            scale = jnp.concatenate([scale, scale], axis=-1)
            cos, sin = (jnp.cos(freqs), jnp.sin(freqs))
            q = q * cos * scale + rotate_half(q) * sin * scale
            k = k * cos / scale + rotate_half(k) * sin / scale
            return (q, k)

        def local_attention(q, k, v):
            b, h, n, d = q.shape
            w = n // WINDOW
            bq = q.reshape(b, h, w, WINDOW, d) * QK_SCALE
            bk = k.reshape(b, h, w, WINDOW, d)
            bv = v.reshape(b, h, w, WINDOW, d)

            def look_around(t):
                p = jnp.pad(t, ((0, 0), (0, 0), (1, 0), (0, 0), (0, 0)))
                return jnp.concatenate([p[:, :, :w], p[:, :, 1:]], axis=3)
            bk, bv = (look_around(bk), look_around(bv))
            bt = jnp.arange(n).reshape(w, WINDOW)
            btp = jnp.pad(bt, ((1, 0), (0, 0)), constant_values=-1)
            btk = jnp.concatenate([btp[:w], btp[1:]], axis=1)
            sim = jnp.einsum('bhwid,bhwjd->bhwij', bq, bk)
            i = bt[:, :, None]
            j = btk[:, None, :]
            mask = (i < j) | (i > j + WINDOW) | (j == -1)
            sim = jnp.where(mask, -jnp.finfo(sim.dtype).max, sim)
            attn = jax.nn.softmax(sim, axis=-1)
            out = jnp.einsum('bhwij,bhwjd->bhwid', attn, bv)
            return out.reshape(b, h, n, d)

        def _layer(x, wqkv, qs, ksc, wo, lg, lb, w1, b1, w2, b2):
            b, n, _ = x.shape
            h = shift_token(x)
            qkv = h @ wqkv
            q, k, v = jnp.split(qkv, 3, axis=-1)
            to_heads = lambda t: t.reshape(b, n, HEADS, DIM_HEAD).transpose(0, 2, 1, 3)
            q, k, v = (to_heads(q), to_heads(k), to_heads(v))
            q = l2norm(q) * qs
            k = l2norm(k) * ksc
            q, k = rotary_xpos(q, k)
            o = local_attention(q, k, v)
            o = o.transpose(0, 2, 1, 3).reshape(b, n, INNER)
            x = x + o @ wo
            h = shift_token(x)
            mu = h.mean(-1, keepdims=True)
            var = h.var(-1, keepdims=True)
            h = (h - mu) / jnp.sqrt(var + 1e-05) * lg + lb
            h = h @ w1 + b1
            a, g = jnp.split(h, 2, axis=-1)
            h = a * jax.nn.gelu(g, approximate=False)
            x = x + h @ w2 + b2
            return x
        key = jax.random.key(seed)
        ks = jax.random.split(key, 6)
        return {'x': jax.random.normal(ks[0], (B, N, DIM), jnp.float32), 'wqkv': jax.random.normal(ks[1], (DEPTH, DIM, 3 * INNER), jnp.float32) * 0.02, 'q_scale': jnp.ones((DEPTH, DIM_HEAD), jnp.float32), 'k_scale': jnp.ones((DEPTH, DIM_HEAD), jnp.float32), 'wo': jax.random.normal(ks[2], (DEPTH, INNER, DIM), jnp.float32) * 0.02, 'ln_g': jnp.ones((DEPTH, DIM), jnp.float32), 'ln_b': jnp.zeros((DEPTH, DIM), jnp.float32), 'w1': jax.random.normal(ks[3], (DEPTH, DIM, 2 * HID), jnp.float32) * 0.02, 'b1': jnp.zeros((DEPTH, 2 * HID), jnp.float32), 'w2': jax.random.normal(ks[4], (DEPTH, HID, DIM), jnp.float32) * 0.02, 'b2': jnp.zeros((DEPTH, DIM), jnp.float32)}
    _L0_ffn_in = _L0_ffn_setup()
    _d = {'L0_attn_x': _L0_attn_in['x'], 'L0_attn_w_qkv': _L0_attn_in['w_qkv'], 'L0_attn_w_o': _L0_attn_in['w_o'], 'L0_attn_ln1_g': _L0_attn_in['ln1_g'], 'L0_attn_ln1_b': _L0_attn_in['ln1_b'], 'L0_attn_ln2_g': _L0_attn_in['ln2_g'], 'L0_attn_ln2_b': _L0_attn_in['ln2_b'], 'L0_attn_mlp_w1': _L0_attn_in['mlp_w1'], 'L0_attn_mlp_b1': _L0_attn_in['mlp_b1'], 'L0_attn_mlp_w2': _L0_attn_in['mlp_w2'], 'L0_attn_mlp_b2': _L0_attn_in['mlp_b2'], 'L0_ffn_wqkv': _L0_ffn_in['wqkv'], 'L0_ffn_q_scale': _L0_ffn_in['q_scale'], 'L0_ffn_k_scale': _L0_ffn_in['k_scale'], 'L0_ffn_wo': _L0_ffn_in['wo'], 'L0_ffn_ln_g': _L0_ffn_in['ln_g'], 'L0_ffn_ln_b': _L0_ffn_in['ln_b'], 'L0_ffn_w1': _L0_ffn_in['w1'], 'L0_ffn_b1': _L0_ffn_in['b1'], 'L0_ffn_w2': _L0_ffn_in['w2'], 'L0_ffn_b2': _L0_ffn_in['b2']}
    _x0 = _d['L0_attn_x']
    _d['L0_attn_x'] = jax.random.normal(jax.random.fold_in(jax.random.key(seed), 1), (2, 2048, 256), dtype=_x0.dtype)
    del _x0
    return _d

def reference(L0_attn_x, L0_attn_w_qkv, L0_attn_w_o, L0_attn_ln1_g, L0_attn_ln1_b, L0_attn_ln2_g, L0_attn_ln2_b, L0_attn_mlp_w1, L0_attn_mlp_b1, L0_attn_mlp_w2, L0_attn_mlp_b2, L0_ffn_wqkv, L0_ffn_q_scale, L0_ffn_k_scale, L0_ffn_wo, L0_ffn_ln_g, L0_ffn_ln_b, L0_ffn_w1, L0_ffn_b1, L0_ffn_w2, L0_ffn_b2):

    def _L0_attn_ref(x, w_qkv, w_o, ln1_g, ln1_b, ln2_g, ln2_b, mlp_w1, mlp_b1, mlp_w2, mlp_b2):
        import jax, jax.numpy as jnp
        import numpy as np
        BATCH, SEQ, D_MODEL = (2, 1024, 256)
        N_HEADS = 16
        HEAD_DIM = D_MODEL // N_HEADS
        WINDOW = 128
        EPS = 1e-05

        def layer_norm(x, g, b):
            m = x.mean(-1, keepdims=True)
            v = ((x - m) ** 2).mean(-1, keepdims=True)
            return (x - m) * jax.lax.rsqrt(v + EPS) * g + b

        def sliding_window_attn(q, k, v, window, scale):
            B, H, S, D = q.shape
            W = window
            C = S // W
            qc = q.reshape(B, H, C, W, D)
            kc = k.reshape(B, H, C, W, D)
            vc = v.reshape(B, H, C, W, D)
            kprev = jnp.pad(kc, ((0, 0), (0, 0), (1, 0), (0, 0), (0, 0)))[:, :, :C]
            vprev = jnp.pad(vc, ((0, 0), (0, 0), (1, 0), (0, 0), (0, 0)))[:, :, :C]
            kcat = jnp.concatenate([kprev, kc], axis=3)
            vcat = jnp.concatenate([vprev, vc], axis=3)
            scores = jnp.einsum('bhcqd,bhckd->bhcqk', qc, kcat) * scale
            i = jnp.arange(W)[:, None]
            j = jnp.arange(2 * W)[None, :]
            band = (j >= i + 1) & (j <= i + W)
            cidx = jnp.arange(C)[:, None, None]
            valid = band[None] & ((cidx > 0) | (j[None] >= W))
            scores = jnp.where(valid[None, None], scores, -jnp.inf)
            attn = jax.nn.softmax(scores, axis=-1)
            out = jnp.einsum('bhcqk,bhckd->bhcqd', attn, vcat)
            return out.reshape(B, H, S, D)
        B, S, D = x.shape
        H, hd = (N_HEADS, HEAD_DIM)
        scale = 1.0 / np.sqrt(hd).astype(np.float32)
        h = layer_norm(x, ln1_g, ln1_b)
        qkv = (h @ w_qkv.T).reshape(B, S, 3, H, hd)
        q = jnp.transpose(qkv[:, :, 0], (0, 2, 1, 3))
        k = jnp.transpose(qkv[:, :, 1], (0, 2, 1, 3))
        v = jnp.transpose(qkv[:, :, 2], (0, 2, 1, 3))
        attn = sliding_window_attn(q, k, v, WINDOW, scale)
        attn = jnp.transpose(attn, (0, 2, 1, 3)).reshape(B, S, D)
        x = x + attn @ w_o.T
        h = layer_norm(x, ln2_g, ln2_b)
        h = jax.nn.gelu(h @ mlp_w1.T + mlp_b1, approximate=False)
        return x + h @ mlp_w2.T + mlp_b2

    def _L0_ffn_ref(x, wqkv, q_scale, k_scale, wo, ln_g, ln_b, w1, b1, w2, b2):
        import jax, jax.numpy as jnp
        import numpy as np
        DIM = 256
        DEPTH = 2
        HEADS = 8
        DIM_HEAD = 64
        WINDOW = 128
        INNER = HEADS * DIM_HEAD
        HID = int(DIM * 4 * 2 / 3)
        B, N = (2, 2048)
        QK_SCALE = 8.0

        def shift_token(t):
            t1, t2 = jnp.split(t, 2, axis=-1)
            t2 = jnp.pad(t2, ((0, 0), (1, 0), (0, 0)))[:, :-1]
            return jnp.concatenate([t1, t2], axis=-1)

        def l2norm(t):
            return t / jnp.clip(jnp.linalg.norm(t, axis=-1, keepdims=True), 1e-12)

        def rotate_half(x):
            x1, x2 = jnp.split(x, 2, axis=-1)
            return jnp.concatenate([-x2, x1], axis=-1)

        def rotary_xpos(q, k):
            n = q.shape[-2]
            half_idx = jnp.arange(0, DIM_HEAD, 2, dtype=jnp.float32)
            inv_freq = 1.0 / 10000.0 ** (half_idx / DIM_HEAD)
            t = jnp.arange(n, dtype=jnp.float32)
            freqs = t[:, None] * inv_freq[None, :]
            freqs = jnp.concatenate([freqs, freqs], axis=-1)
            base = (half_idx + 0.4 * DIM_HEAD) / (1.4 * DIM_HEAD)
            power = (t - n // 2) / float(WINDOW // 2)
            scale = base[None, :] ** power[:, None]
            scale = jnp.concatenate([scale, scale], axis=-1)
            cos, sin = (jnp.cos(freqs), jnp.sin(freqs))
            q = q * cos * scale + rotate_half(q) * sin * scale
            k = k * cos / scale + rotate_half(k) * sin / scale
            return (q, k)

        def local_attention(q, k, v):
            b, h, n, d = q.shape
            w = n // WINDOW
            bq = q.reshape(b, h, w, WINDOW, d) * QK_SCALE
            bk = k.reshape(b, h, w, WINDOW, d)
            bv = v.reshape(b, h, w, WINDOW, d)

            def look_around(t):
                p = jnp.pad(t, ((0, 0), (0, 0), (1, 0), (0, 0), (0, 0)))
                return jnp.concatenate([p[:, :, :w], p[:, :, 1:]], axis=3)
            bk, bv = (look_around(bk), look_around(bv))
            bt = jnp.arange(n).reshape(w, WINDOW)
            btp = jnp.pad(bt, ((1, 0), (0, 0)), constant_values=-1)
            btk = jnp.concatenate([btp[:w], btp[1:]], axis=1)
            sim = jnp.einsum('bhwid,bhwjd->bhwij', bq, bk)
            i = bt[:, :, None]
            j = btk[:, None, :]
            mask = (i < j) | (i > j + WINDOW) | (j == -1)
            sim = jnp.where(mask, -jnp.finfo(sim.dtype).max, sim)
            attn = jax.nn.softmax(sim, axis=-1)
            out = jnp.einsum('bhwij,bhwjd->bhwid', attn, bv)
            return out.reshape(b, h, n, d)

        def _layer(x, wqkv, qs, ksc, wo, lg, lb, w1, b1, w2, b2):
            b, n, _ = x.shape
            h = shift_token(x)
            qkv = h @ wqkv
            q, k, v = jnp.split(qkv, 3, axis=-1)
            to_heads = lambda t: t.reshape(b, n, HEADS, DIM_HEAD).transpose(0, 2, 1, 3)
            q, k, v = (to_heads(q), to_heads(k), to_heads(v))
            q = l2norm(q) * qs
            k = l2norm(k) * ksc
            q, k = rotary_xpos(q, k)
            o = local_attention(q, k, v)
            o = o.transpose(0, 2, 1, 3).reshape(b, n, INNER)
            x = x + o @ wo
            h = shift_token(x)
            mu = h.mean(-1, keepdims=True)
            var = h.var(-1, keepdims=True)
            h = (h - mu) / jnp.sqrt(var + 1e-05) * lg + lb
            h = h @ w1 + b1
            a, g = jnp.split(h, 2, axis=-1)
            h = a * jax.nn.gelu(g, approximate=False)
            x = x + h @ w2 + b2
            return x
        for l in range(DEPTH):
            x = _layer(x, wqkv[l], q_scale[l], k_scale[l], wo[l], ln_g[l], ln_b[l], w1[l], b1[l], w2[l], b2[l])
        return x
    x = L0_attn_x
    x = _layernorm(x + _L0_attn_ref(x, L0_attn_w_qkv, L0_attn_w_o, L0_attn_ln1_g, L0_attn_ln1_b, L0_attn_ln2_g, L0_attn_ln2_b, L0_attn_mlp_w1, L0_attn_mlp_b1, L0_attn_mlp_w2, L0_attn_mlp_b2), axis=-1)
    x = _layernorm(x + _L0_ffn_ref(x, L0_ffn_wqkv, L0_ffn_q_scale, L0_ffn_k_scale, L0_ffn_wo, L0_ffn_ln_g, L0_ffn_ln_b, L0_ffn_w1, L0_ffn_b1, L0_ffn_w2, L0_ffn_b2), axis=-1)
    return x

_drawn_inputs = setup_inputs


def setup_inputs(seed=0):
    import zlib

    import numpy as np

    out = dict(_drawn_inputs(seed))
    spreads = {'L0_attn_ln1_g': (1.0, 0.6),
     'L0_attn_ln1_b': (0.0, 0.8),
     'L0_attn_ln2_g': (1.0, 0.6),
     'L0_attn_ln2_b': (0.0, 2.0),
     'L0_attn_mlp_b1': (0.0, 1.427),
     'L0_attn_mlp_b2': (0.0, 0.561),
     'L0_ffn_q_scale': (1.0, 0.6),
     'L0_ffn_k_scale': (1.0, 0.6),
     'L0_ffn_ln_g': (1.0, 0.6),
     'L0_ffn_ln_b': (0.0, 0.8),
     'L0_ffn_b1': (0.0, 0.8),
     'L0_ffn_b2': (0.0, 0.1)}
    factors = {'L0_attn_w_qkv': 7.77,
     'L0_attn_w_o': 7.586,
     'L0_ffn_wqkv': 3.442,
     'L0_ffn_wo': 3.396,
     'L0_attn_mlp_w1': 2.894}
    for name, (base, spread) in spreads.items():
        noise = np.random.default_rng([zlib.crc32(name.encode()), seed]).standard_normal(out[name].shape)
        drawn = base * np.exp(spread * noise) if base else spread * noise
        out[name] = jnp.asarray(drawn.astype(out[name].dtype))
    for name, factor in factors.items():
        out[name] = (out[name] * factor).astype(out[name].dtype)
    return out
```

```python
from contextlib import ExitStack

import concourse.bass as bass
import numpy as np
from concourse import mybir

F32 = mybir.dt.float32
F32R = mybir.dt.float32r
ALU = mybir.AluOpType
ACT = mybir.ActivationFunctionType
AX = mybir.AxisListType

P = 128
B, SEQ, D = 2, 2048, 256
TOK = B * SEQ
NCH = TOK // P
U = 4
ITERS = NCH // U
KD = D // P
GT = 4 * P
NGRP = TOK // GT
LAYERS = 2
EPS = 1e-5
MASKED = -1.0e30
BIG = 3.0e38


class Attention:

    def __init__(self, name, heads, dim, row_step, layers, first_count):
        self.name = name
        self.NH, self.DH = heads, dim
        self.NP = heads // 2
        self.RS = row_step
        self.HPT = P // row_step
        self.NT = heads // self.HPT
        self.OC = heads * dim
        self.KO = self.OC // P
        self.QKV = 3 * self.OC
        self.WCOLS = KD * self.QKV + self.KO * D
        self.layers = layers

    def head(self, p, i):
        row, tiles = p % self.HPT, 2 * (p // self.HPT)
        return (tiles + i) * self.HPT + row


ATT_A = Attention("a", 16, 16, 32, 1, 0)
ATT_B = Attention("b", 8, 64, 64, LAYERS, 0)


class Mlp:

    def __init__(self, name, hidden, tile, gated):
        self.name = name
        self.H, self.FT, self.gated = hidden, tile, gated
        self.NF = -(-hidden // tile)
        self.rows = [min(tile, hidden - tile * f) for f in range(self.NF)]
        self.IN = hidden * (2 if gated else 1)
        self.WCOLS = KD * self.IN + self.NF * D


MLP_A = Mlp("a", 4 * D, P, False)
MLP_B = Mlp("b", int(D * 4 * 2 / 3), 114, True)
WA = max(ATT_A.WCOLS, ATT_B.WCOLS)
WM = max(MLP_A.WCOLS, MLP_B.WCOLS)


def build(nc, io):
    x_state = nc.dram_tensor("x_state", ((LAYERS + 1) * TOK, D), F32, kind="Internal").ap()
    x_state_sh = nc.dram_tensor("x_state_sh", ((LAYERS + 1) * (TOK + P), P), F32, kind="Internal").ap()
    x_mid = nc.dram_tensor("x_mid", (TOK, D), F32, kind="Internal").ap()
    x_mid_sh = nc.dram_tensor("x_mid_sh", (TOK + P, P), F32, kind="Internal").ap()

    ctx = ExitStack()
    with ctx:
        def sbuf(name, shape, dt=F32, at=ctx):
            return at.enter_context(nc.sbuf_tensor(name, shape, dt))

        def sem(name):
            return ctx.enter_context(nc.semaphore(name))

        bank = [ctx.enter_context(nc.psum_tensor(f"bank{i}", [P, 512], F32)) for i in range(8)]
        work = bank[0:3]
        scores = bank[3:5]
        probs_t = bank[5:7]
        heads_out = bank[7]

        wa_raw = sbuf("wa_raw", [P, WA])
        wm_raw = sbuf("wm_raw", [P, WM])
        wa_hi, wa_lo = sbuf("wa_hi", [P, WA], F32R), sbuf("wa_lo", [P, WA], F32R)
        wm_hi, wm_lo = sbuf("wm_hi", [P, WM], F32R), sbuf("wm_lo", [P, WM], F32R)
        ident = sbuf("ident", [P, P])
        zero_row = sbuf("zero_row", [P, 2, P])
        minus_half = sbuf("minus_half", [P, 16])
        vec_a = sbuf("vec_a", [P, 16])
        vec_b = sbuf("vec_b", [P, 16])
        row_b2 = sbuf("row_b2", [P, D])

        at_ctx = ExitStack()
        x_in = sbuf("x_in", [P, U, D], at=at_ctx)
        x_res = sbuf("x_res", [P, U, D], at=at_ctx)
        rope_in = sbuf("rope_in", [P, U, D], at=at_ctx)
        rope = sbuf("rope", [P, 4, 64], at=at_ctx)
        rope_scale = sbuf("rope_scale", [P, 4, 64], at=at_ctx)
        z = sbuf("z", [P, D], at=at_ctx)
        h32 = sbuf("h32", [P, D], at=at_ctx)
        h_hi, h_lo = sbuf("h_hi", [P, D], F32R, at_ctx), sbuf("h_lo", [P, D], F32R, at_ctx)
        qk = [sbuf("q_tok", [P, 512], at=at_ctx), sbuf("k_tok", [P, 512], at=at_ctx)]
        squares = [sbuf("q_sq", [P, 512], at=at_ctx), sbuf("k_sq", [P, 512], at=at_ctx)]
        cos_part = [sbuf("q_cos", [P, 512], at=at_ctx), sbuf("k_cos", [P, 512], at=at_ctx)]
        rot = [sbuf("q_rot", [P, 512], at=at_ctx), sbuf("k_rot", [P, 512], at=at_ctx)]
        norm2 = sbuf("norm2", [P, 16], at=at_ctx)
        norm2c = sbuf("norm2c", [P, 16], at=at_ctx)
        rnorm = sbuf("rnorm", [P, 16], at=at_ctx)
        stats = sbuf("stats", [P, 6], at=at_ctx)
        mean_var = sbuf("mean_var", [P, 2], at=at_ctx)
        var_eps = sbuf("var_eps", [P, 1], at=at_ctx)
        rstd = sbuf("rstd", [P, 1], at=at_ctx)
        q_t = sbuf("q_t", [P, 4, P], at=at_ctx)
        k_t = sbuf("k_t", [P, 4, (U + 1) * P], at=at_ctx)
        v_tok = [sbuf(f"v_tok{i}", [P, 512], at=at_ctx) for i in range(U)]
        masked = [sbuf(f"masked{i}", [P, 512], at=at_ctx) for i in range(2)]
        probs = [sbuf(f"probs{i}", [P, 512], at=at_ctx) for i in range(2)]
        pt = [sbuf(f"pt{i}", [P, 512], at=at_ctx) for i in range(2)]
        neg_max = sbuf("neg_max", [P, 16], at=at_ctx)
        row_sum = sbuf("row_sum", [P, 16], at=at_ctx)
        inv_sum = sbuf("inv_sum", [P, 16], at=at_ctx)
        o_tok = sbuf("o_tok", [P, 512], at=at_ctx)
        o_hi, o_lo = sbuf("o_hi", [P, 512], F32R, at_ctx), sbuf("o_lo", [P, 512], F32R, at_ctx)
        y_out = sbuf("y_out", [P, 2, D], at=at_ctx)
        mask = sbuf("mask", [P, 2 * P], at=at_ctx)
        mask0 = sbuf("mask0", [P, 2 * P], at=at_ctx)
        mask0_prev = sbuf("mask0_prev", [P, ITERS, P], at=at_ctx)
        at_ctx.close()

        m_ctx = ExitStack()
        g_in = [sbuf(f"g_in{i}", [P, 4, D], at=m_ctx) for i in range(2)]
        g_mid = [sbuf(f"g_mid{i}", [P, 4, D], at=m_ctx) for i in range(2)]
        g_old = [sbuf(f"g_old{i}", [P, 4, D], at=m_ctx) for i in range(2)]
        g_z = sbuf("g_z", [P, 4, D], at=m_ctx)
        g_stats = sbuf("g_stats", [P, 4, 6], at=m_ctx)
        g_mv = sbuf("g_mv", [P, 4, 2], at=m_ctx)
        g_ve = sbuf("g_ve", [P, 4], at=m_ctx)
        g_rstd = sbuf("g_rstd", [P, 4], at=m_ctx)
        f_stats = sbuf("f_stats", [P, 4, 6], at=m_ctx)
        f_mv = sbuf("f_mv", [P, 4, 2], at=m_ctx)
        f_ve = sbuf("f_ve", [P, 4], at=m_ctx)
        f_rstd = sbuf("f_rstd", [P, 4], at=m_ctx)
        g_h32 = sbuf("g_h32", [P, KD, GT], at=m_ctx)
        g_h_hi, g_h_lo = sbuf("g_h_hi", [P, KD, GT], F32R, m_ctx), sbuf("g_h_lo", [P, KD, GT], F32R, m_ctx)
        gate = [sbuf(f"gate{i}", [P, GT], at=m_ctx) for i in range(2)]
        hid = [sbuf(f"hid{i}", [P, GT], at=m_ctx) for i in range(2)]
        u_hi, u_lo = sbuf("u_hi", [P, 8, GT], F32R, m_ctx), sbuf("u_lo", [P, 8, GT], F32R, m_ctx)
        g_sum = sbuf("g_sum", [P, 4, D], at=m_ctx)
        g_new = sbuf("g_new", [P, 4, D], at=m_ctx)
        g_fin = sbuf("g_fin", [P, 4, D], at=m_ctx)
        m_ctx.close()

        consts_loaded = sem("consts_loaded")
        consts_set = sem("consts_set")
        zero_rows_stored = sem("zero_rows_stored")
        wa_loaded, wm_loaded = sem("wa_loaded"), sem("wm_loaded")
        wa_split, wm_split = sem("wa_split"), sem("wm_split")
        wa_hi_done, wm_hi_done = sem("wa_hi_done"), sem("wm_hi_done")

        def sems(prefix, names):
            return {n: sem(f"{prefix}_{n}") for n in names.split()}

        att_names = """load0 load1 load2 load3 store0 store1 params phase_set
            ln_stats ln_aggr ln_var ln_rstd z_ready xt_ready h32_ready h_hi h_lo
            q_proj k_proj v_proj q_copied k_copied v_copied q_squared k_squared norm2_part norm2_ready rnorm_ready
            rope_ready q_parts k_parts q_rot k_rot qt_ready kt_ready qt_copied kt_copied
            mask0_ready scores_ready masked_ready probs_ready pt_ready pt_dve pt_act pv_done
            inv_ready o_ready ot_ready o_hi o_lo wo_ready y_ready"""
        SA = sems("a", " ".join(n for n in att_names.split() if n not in
                                "k_proj q_squared k_squared norm2_part norm2_ready rnorm_ready rope_ready q_parts k_parts q_rot k_rot".split()))
        SB = sems("b", " ".join(n for n in att_names.split() if n not in
                                "ln_stats ln_aggr ln_var ln_rstd z_ready h32_ready".split()))
        mlp_names = """load0 load1 store params stats aggr var rstd z_ready xt_ready h32_ready h_hi h_lo
            in_ready gate_ready hid_ready u_hi u_lo_dve u_lo_pool y_ready y_added res_ready
            f_sum f_stats f_aggr f_var f_rstd fin_ready"""
        MA = sems("ma", " ".join(n for n in mlp_names.split() if n not in ("hid_ready", "u_lo_pool")))
        MB = sems("mb", mlp_names)

        def wait_apart(eng, *waits):
            values = [(s, v if isinstance(v, int) else eng.snap(v)) for s, v in waits]
            for _, v in values:
                if not isinstance(v, int):
                    eng.lower_val(v)
            eng.wait_ge(consts_set, 1)
            for s, v in values:
                eng.wait_ge(s, v)

        block = ctx.enter_context(nc.Block())

        def attention_loop(eng, c, layer, prologue, step):
            base = 0 if layer is None else eng.snap(layer * NCH)
            prologue(base)
            with eng.Fori(0, ITERS - 1) as j:
                g0 = eng.snap(j * U) if layer is None else eng.snap(layer * NCH + j * U)
                for e in range(U):
                    step(g0 + e, e, j, j * U + e, True, True)
            last = U * (ITERS - 1)
            for e in range(U):
                step(base + last + e, e, ITERS - 1, last + e, e < U - 1, e < U - 2)

        def load_attention_weights(sp, which):
            sp.dma_start(wa_raw[:, 0:which.shape[-1]], which).then_inc(wa_loaded, 16)

        def load_mlp_weights(sp, which):
            sp.dma_start(wm_raw[:, 0:which.shape[-1]], which).then_inc(wm_loaded, 16)

        def sp_attention(sp, c, S, layer):
            gated = c is ATT_B

            def load(n_local, slot):
                rows = bass.ds(n_local * P, P) if not isinstance(n_local, int) else slice(n_local * P, n_local * P + P)
                if c is ATT_A:
                    sp.dma_start(x_in[:, slot, :], io["x"][rows, :]).then_inc(S[f"load{slot}"], 16)
                    return
                srow = bass.ds(layer * TOK + n_local * P, P)
                hrow = bass.ds(layer * (TOK + P) + n_local * P, P)
                s = S[f"load{slot}"]
                sp.dma_start(x_in[:, slot, 0:P], x_state[srow, 0:P]).then_inc(s, 16)
                sp.dma_start(x_in[:, slot, P:D], x_state_sh[hrow, :]).then_inc(s, 16)
                sp.dma_start(x_res[:, slot, :], x_state[srow, :]).then_inc(s, 16)
                sp.dma_start(rope_in[:, slot, :], io["rope"][rows, :]).then_inc(s, 16)

            def prologue(base):
                load(0, 0)
                load(1, 1)
                if c is ATT_A:
                    sp.dma_start(mask[:], io["mask_a"]).then_inc(S["params"], 16)
                    sp.dma_start(mask0[:], io["mask_a"]).then_inc(S["params"], 16)
                    sp.dma_start(mask0_prev[:], io["mask_a0"]).then_inc(S["params"], 16)
                    sp.dma_start(vec_a[:], io["vec_a"]).then_inc(S["params"], 16)
                else:
                    sp.dma_start(mask[:], io["mask_b"]).then_inc(S["params"], 16)
                    sp.dma_start(mask0[:], io["mask_b"]).then_inc(S["params"], 16)
                    sp.dma_start(mask0_prev[:], io["mask_b0"]).then_inc(S["params"], 16)
                    sp.dma_start(rope_scale[:].rearrange("p a d -> p (a d)"),
                                 io["rope_scale"][bass.ds(layer * P, P), :]).then_inc(S["params"], 16)
                load(2, 2)
                load(3, 3)

            def step(g, e, j, g_local, more, more2):
                sp.wait_ge(S["y_ready"], g + 1)
                rows = bass.ds(g_local * P, P) if not isinstance(g_local, int) else slice(g_local * P, g_local * P + P)
                hrows = bass.ds(g_local * P + 1, P) if not isinstance(g_local, int) else \
                    slice(g_local * P + 1, g_local * P + 1 + P)
                sp.dma_start(x_mid[rows, :], y_out[:, e % 2, :]).then_inc(S[f"store{e % 2}"], 16)
                if gated:
                    sp.dma_start(x_mid_sh[hrows, :], y_out[:, e % 2, P:D]).then_inc(S[f"store{e % 2}"], 16)
                if not isinstance(j, int):
                    load(g_local + U, e)

            attention_loop(sp, c, layer, prologue, step)
            n = 32 if gated else 16
            for e in range(2):
                sp.wait_ge(S[f"store{e}"], n * (NCH // 2) + n if layer is None else
                           layer * (n * (NCH // 2)) + (n * (NCH // 2) + n))
            if gated:
                sp.dma_start(x_mid_sh[0:1, :], zero_row[0:1, 0, :]).then_inc(zero_rows_stored, 16)
                sp.dma_start(x_mid_sh[SEQ:SEQ + 1, :], zero_row[0:1, 1, :]).then_inc(zero_rows_stored, 16)
                sp.wait_ge(zero_rows_stored, layer * 64 + 32)

        def sp_mlp(sp, c, S, layer):
            def token_rows(ap, start, cols=slice(0, D)):
                r = bass.ds(start, GT) if not isinstance(start, int) else slice(start, start + GT)
                return ap[r, cols].rearrange("(c p) d -> p c d", p=P)

            def load(t_local, slot):
                s = S[f"load{slot}"]
                if c is MLP_A:
                    sp.dma_start(g_in[slot][:], token_rows(x_mid, t_local * GT)).then_inc(s, 16)
                    sp.dma_start(g_old[slot][:], token_rows(io["x"], t_local * GT)).then_inc(s, 16)
                    return
                sp.dma_start(g_in[slot][:, :, 0:P], token_rows(x_mid, t_local * GT, slice(0, P))).then_inc(s, 16)
                sp.dma_start(g_in[slot][:, :, P:D], token_rows(x_mid_sh, t_local * GT, slice(0, P))).then_inc(s, 16)
                sp.dma_start(g_mid[slot][:], token_rows(x_mid, t_local * GT)).then_inc(s, 16)
                sp.dma_start(g_old[slot][:], token_rows(x_state, t_local * GT)).then_inc(s, 16)

            load(0, 0)
            if c is MLP_A:
                sp.dma_start(row_b2[:], io["b2_a"]).then_inc(S["params"], 16)
            else:
                sp.dma_start(row_b2[:], io["b2_b"][bass.ds(layer * P, P), :]).then_inc(S["params"], 16)
                sp.dma_start(vec_b[:], io["vec_b"][bass.ds(layer * P, P), :]).then_inc(S["params"], 16)
            load(1, 1)
            load_attention_weights(sp, io["w_att_b"][0:P, :] if c is MLP_A else io["w_att_b"][P:2 * P, :])
            base = 0 if layer is None else layer * NGRP

            def store(t_local, t):
                s = S["store"]
                sp.wait_ge(S["fin_ready"], t + 1)
                if c is MLP_A:
                    sp.dma_start(token_rows(x_state, t_local * GT), g_fin[:]).then_inc(s, 16)
                    sp.dma_start(token_rows(x_state_sh, t_local * GT + 1, slice(0, P)), g_fin[:, :, P:D]).then_inc(s, 16)
                    return
                sp.dma_start(token_rows(x_state, (layer + 1) * TOK + t_local * GT), g_new[:]).then_inc(s, 16)
                sp.dma_start(token_rows(x_state_sh, (layer + 1) * (TOK + P) + t_local * GT + 1, slice(0, P)),
                             g_new[:, :, P:D]).then_inc(s, 16)
                sp.dma_start(token_rows(io["out"], t_local * GT), g_fin[:]).then_inc(s, 16)

            n = 32 if c is MLP_A else 48
            with sp.Fori(0, NGRP // 2 - 1) as i:
                t0 = sp.snap(i * 2) if layer is None else sp.snap(layer * NGRP + i * 2)
                for e in range(2):
                    store(i * 2 + e, t0 + e)
                    load(i * 2 + e + 2, e)
            for e in range(2):
                store(NGRP - 2 + e, base + NGRP - 2 + e)
            sp.wait_ge(S["store"], base * n + (n * NGRP + n))
            first = 0 if c is MLP_A else (layer + 1) * (TOK + P)
            for b in range(B):
                at = first + b * SEQ
                r = slice(at, at + 1) if isinstance(at, int) else bass.ds(at, 1)
                sp.dma_start(x_state_sh[r, :], zero_row[0:1, b, :]).then_inc(
                    S["params"] if c is MLP_A else zero_rows_stored, 16)
            if c is MLP_A:
                sp.wait_ge(S["params"], 16 + 32)
            else:
                wait_apart(sp, (zero_rows_stored, layer * 64 + 64))

        @block.sync
        def _(sp):
            for e in range(2):
                sp.sem_inc(SA[f"store{e}"], 16)
                sp.sem_inc(SB[f"store{e}"], 32)
            sp.sem_inc(MA["store"], 32)
            sp.sem_inc(MB["store"], 48)
            sp.dma_start(ident[:], io["ident"]).then_inc(consts_loaded, 16)
            sp.wait_ge(consts_set, 1)
            load_attention_weights(sp, io["w_att_a"])
            load_mlp_weights(sp, io["w_mlp_a"])
            sp_attention(sp, ATT_A, SA, None)
            sp_mlp(sp, MLP_A, MA, None)
            with sp.Fori(0, LAYERS) as layer:
                load_mlp_weights(sp, io["w_mlp_b"][bass.ds(layer * P, P), :])
                sp_attention(sp, ATT_B, SB, layer)
                sp_mlp(sp, MLP_B, MB, layer)

        def product3(out, a_hi, a_lo, b_hi, b_lo, first, last):
            nc.tensor.matmul(out, a_hi, b_hi, start=first, stop=False)
            nc.tensor.matmul(out, a_hi, b_lo, start=False, stop=False)
            return nc.tensor.matmul(out, a_lo, b_hi, start=False, stop=last)

        def pe_attention(pe, c, S, layer):
            wqkv_hi = wa_hi[:, 0:KD * c.QKV].rearrange("p (k n) -> p k n", k=KD)
            wqkv_lo = wa_lo[:, 0:KD * c.QKV].rearrange("p (k n) -> p k n", k=KD)
            wo_hi = wa_hi[:, KD * c.QKV:c.WCOLS].rearrange("p (k n) -> p k n", k=c.KO)
            wo_lo = wa_lo[:, KD * c.QKV:c.WCOLS].rearrange("p (k n) -> p k n", k=c.KO)

            def project(n, part):
                if part == 0:
                    pe.wait_ge(S["h_hi"], n + 1)
                    pe.wait_ge(S["h_lo"], n + 1)
                if c is ATT_A:
                    if part == 2:
                        return
                    out, c0, w = [(work[1], 0, 512), (work[2], 512, 256)][part]
                    done = S[["q_proj", "v_proj"][part]]
                else:
                    out, c0, w = [(work[1], 0, 512), (work[2], 512, 512), (work[0], 1024, 512)][part]
                    done = S[["q_proj", "k_proj", "v_proj"][part]]
                for k in range(KD):
                    mm = product3(out[:, 0:w], h_hi[:, k * P:k * P + P], h_lo[:, k * P:k * P + P],
                                  wqkv_hi[:, k, c0:c0 + w], wqkv_lo[:, k, c0:c0 + w], k == 0, k == KD - 1)
                mm.then_inc(done, 1)

            def transpose_x(m, slot):
                if c is ATT_A:
                    pe.wait_ge(S["z_ready"], m + 1)
                    src = z[:, :]
                else:
                    pe.wait_ge(S[f"load{slot}"], load_count(c, m, slot))
                    src = x_in[:, slot, :]
                for k in range(KD):
                    mm = nc.tensor.transpose(work[1][:, k * P:k * P + P], src[:, k * P:k * P + P], ident[:])
                mm.then_inc(S["xt_ready"], 1)

            def transpose_qk(n):
                src = qk if c is ATT_A else rot
                pe.wait_ge(S["q_copied"] if c is ATT_A else S["q_rot"], n + 1)
                pe.wait_ge(S["k_copied"] if c is ATT_A else S["k_rot"], n + 1)
                for i in range(c.NT):
                    mm = nc.tensor.transpose(work[1][:, i * P:i * P + P], src[0][:, i * P:i * P + P], ident[:])
                mm.then_inc(S["qt_ready"], 1)
                if c is ATT_A:
                    pe.wait_ge(S["v_copied"], n + 1)
                for i in range(c.NT):
                    mm = nc.tensor.transpose(work[2][:, i * P:i * P + P], src[1][:, i * P:i * P + P], ident[:])
                mm.then_inc(S["kt_ready"], 1)

            def score_pair(g, e, p):
                if p >= 2:
                    pe.wait_ge(S["masked_ready"], g * c.NP + (p - 1))
                for hh in range(2):
                    h = c.head(p, hh)
                    t, r = h // c.HPT, (h % c.HPT) * c.RS
                    mm = nc.tensor.matmul(scores[p % 2][:, hh * 256:hh * 256 + 256], q_t[r:r + c.DH, t, :],
                                          k_t[r:r + c.DH, t, e * P:e * P + 2 * P], start=True, stop=True)
                mm.then_inc(S["scores_ready"], 1)

            def transpose_probs(g, p):
                pe.wait_ge(S["probs_ready"], g * c.NP + (p + 1))
                for i in range(4):
                    mm = nc.tensor.transpose(probs_t[p % 2][:, i * P:i * P + P], probs[p % 2][:, i * P:i * P + P],
                                             ident[:])
                mm.then_inc(S["pt_ready"], 1)

            def value_pair(g, e, p):
                by, k, per = evacuator(c, p)
                pe.wait_ge(S[by], g * per + (k + 1))
                for hh in range(2):
                    h = c.head(p, hh)
                    cols = slice(h * c.DH, h * c.DH + c.DH)
                    for blk, slot in ((0, (e - 1) % U), (1, e)):
                        i = 2 * hh + blk
                        mm = nc.tensor.matmul(heads_out[:, cols], pt[p % 2][:, i * P:i * P + P], v_tok[slot][:, cols],
                                              start=(blk == 0), stop=(blk == 1))
                mm.then_inc(S["pv_done"], 1)

            def output(g, more):
                pe.wait_ge(S["o_ready"], g + 1)
                if more and c is ATT_B:
                    pe.wait_ge(S["v_copied"], g + 2)
                for k in range(c.KO):
                    mm = nc.tensor.transpose(work[0][:, k * P:k * P + P], o_tok[:, k * P:k * P + P], ident[:])
                mm.then_inc(S["ot_ready"], 1)

            def out_project(g):
                pe.wait_ge(S["o_hi"], g + 1)
                pe.wait_ge(S["o_lo"], g + 1)
                for k in range(c.KO):
                    mm = product3(work[0][:, 0:D], o_hi[:, k * P:k * P + P], o_lo[:, k * P:k * P + P],
                                  wo_hi[:, k, :], wo_lo[:, k, :], k == 0, k == c.KO - 1)
                mm.then_inc(S["wo_ready"], 1)

            def prologue(base):
                transpose_x(base, 0)
                pe.wait_ge(wa_split, 1 if layer is None else layer + 2)
                pe.wait_ge(wa_hi_done, 1 if layer is None else layer + 2)
                for part in range(3):
                    project(base, part)
                transpose_qk(base)
                pe.wait_ge(S["qt_copied"], base + 1)
                transpose_x(base + 1, 1)

            def step(g, e, j, g_local, more, more2):
                pe.wait_ge(S["qt_copied"], g + 1)
                pe.wait_ge(S["kt_copied"], g + 1)
                pe.wait_ge(S["phase_set"], 2 if layer is None else layer * 2 + 2)
                score_pair(g, e, 0)
                score_pair(g, e, 1)
                for p in range(c.NP):
                    if more and p < 3:
                        project(g + 1, p)
                    transpose_probs(g, p)
                    if p + 2 < c.NP:
                        score_pair(g, e, p + 2)
                    if p == 0:
                        pe.wait_ge(S["v_copied"], g + 1)
                    else:
                        value_pair(g, e, p - 1)
                value_pair(g, e, c.NP - 1)
                if more:
                    transpose_qk(g + 1)
                output(g, more)
                if more2:
                    pe.wait_ge(S["qt_copied"], g + 2)
                    transpose_x(g + 2, (e + 2) % U)
                out_project(g)

            attention_loop(pe, c, layer, prologue, step)

        def load_count(c, n, slot):
            per = 16 if c is ATT_A else 64
            return (n - slot) * (per // U) + per

        def evacuator(c, p):
            if c is ATT_A:
                return ("pt_dve", p // 2, 4) if p % 2 == 0 else ("pt_act", p // 2, 4)
            return ("pt_dve", 0, 1) if p == 0 else ("pt_act", p - 1, 3)

        def pe_mlp(pe, c, S, layer):
            w1_hi = wm_hi[:, 0:KD * c.IN].rearrange("p (k n) -> p k n", k=KD)
            w1_lo = wm_lo[:, 0:KD * c.IN].rearrange("p (k n) -> p k n", k=KD)
            w2_hi = wm_hi[:, KD * c.IN:c.WCOLS].rearrange("p (k n) -> p k n", k=c.NF)
            w2_lo = wm_lo[:, KD * c.IN:c.WCOLS].rearrange("p (k n) -> p k n", k=c.NF)
            h_banks, xt_banks, y_banks = bank[0:4], bank[4:6], bank[6:8]

            def transpose_z(t):
                pe.wait_ge(S["z_ready"], t + 1)
                for k in range(KD):
                    for i in range(4):
                        mm = nc.tensor.transpose(xt_banks[k][:, i * P:i * P + P], g_z[:, i, k * P:k * P + P], ident[:])
                mm.then_inc(S["xt_ready"], 1)

            def hidden(t, f):
                r = c.rows[f]
                if c.gated:
                    if f >= 2:
                        pe.wait_ge(S["hid_ready"], t * c.NF + (f - 1))
                    targets = [(h_banks[(2 * f) % 4], c.H + f * c.FT), (h_banks[(2 * f + 1) % 4], f * c.FT)]
                else:
                    if f >= 4:
                        pe.wait_ge(S["gate_ready"], t * c.NF + (f - 3))
                    targets = [(h_banks[f % 4], f * c.FT)]
                for out, c0 in targets:
                    for k in range(KD):
                        mm = product3(out[0:r, :], w1_hi[:, k, c0:c0 + r], w1_lo[:, k, c0:c0 + r],
                                      g_h_hi[:, k, :], g_h_lo[:, k, :], k == 0, k == KD - 1)
                    mm.then_inc(S["in_ready"], 1)

            def down(t, half):
                if half == 1:
                    pe.wait_ge(S["y_added"], t * 4 + 2)
                for f in range(c.NF):
                    r = c.rows[f]
                    if half == 0:
                        pe.wait_ge(S["u_hi"], t * c.NF + (f + 1))
                        if c.gated:
                            pe.wait_ge(S[["u_lo_dve", "u_lo_pool"][f % 2]], t * 3 + (f // 2 + 1))
                        else:
                            pe.wait_ge(S["u_lo_dve"], t * c.NF + (f + 1))
                    for i in range(2):
                        ch = 2 * half + i
                        mm = product3(y_banks[i][:, 0:D], u_hi[0:r, f, ch * P:ch * P + P], u_lo[0:r, f, ch * P:ch * P + P],
                                      w2_hi[0:r, f, :], w2_lo[0:r, f, :], f == 0, f == c.NF - 1)
                mm.then_inc(S["y_ready"], 1)

            def group(t, more):
                pe.wait_ge(S["h_hi"], t + 1)
                pe.wait_ge(S["h_lo"], t + 1)
                for f in range(c.NF):
                    hidden(t, f)
                if more:
                    transpose_z(t + 1)
                down(t, 0)
                down(t, 1)

            base = 0 if layer is None else pe.snap(layer * NGRP)
            transpose_z(base)
            pe.wait_ge(consts_loaded, 16)
            pe.wait_ge(wm_split, 1 if layer is None else layer + 2)
            pe.wait_ge(wm_hi_done, 1 if layer is None else layer + 2)
            with pe.Fori(0, NGRP - 1) as i:
                group(pe.snap(i + 0) if layer is None else pe.snap(layer * NGRP + i), True)
            group(base + (NGRP - 1), False)

        @block.tensor
        def _(pe):
            pe.wait_ge(consts_loaded, 16)
            pe_attention(pe, ATT_A, SA, None)
            pe_mlp(pe, MLP_A, MA, None)
            with pe.Fori(0, LAYERS) as layer:
                pe_attention(pe, ATT_B, SB, layer)
                pe_mlp(pe, MLP_B, MB, layer)

        def split_low(v, raw, hi, lo, cols, loaded, hi_done, done, layer):
            v.wait_ge(loaded, 16 if layer is None else layer * 16 + 32)
            v.wait_ge(hi_done, 1 if layer is None else layer + 2)
            nc.vector.tensor_tensor(lo[:, 0:cols], raw[:, 0:cols], hi[:, 0:cols].bitcast(F32),
                                    ALU.subtract).then_inc(done, 1)

        def dve_attention(v, c, S, layer):
            split_low(v, wa_raw, wa_hi, wa_lo, c.WCOLS, wa_loaded, wa_hi_done, wa_split, layer)

            def heads(ap, n=None):
                return ap.rearrange("p (h d) -> p h d", d=c.DH)

            def layer_norm_stats(m, slot):
                v.wait_ge(S[f"load{slot}"], load_count(c, m, slot))
                nc.vector.bn_stats(stats[:], x_in[:, slot, :]).then_inc(S["ln_stats"], 1)
                wait_apart(v, (S["ln_stats"], m + 1))
                nc.vector.bn_aggr(mean_var[:], stats[:]).then_inc(S["ln_aggr"], 1)
                v.wait_ge(S["ln_aggr"], m + 1)
                nc.vector.tensor_scalar_add(var_eps[:], mean_var[:, 1:2], EPS).then_inc(S["ln_var"], 1)

            def normalize(m, slot):
                v.wait_ge(S["ln_rstd"], m + 1)
                nc.vector.tensor_scalar(z[:], x_in[:, slot, :], mean_var[:, 0:1], rstd[:], ALU.subtract,
                                        ALU.mult).then_inc(S["z_ready"], 1)

            def h_transposed(m):
                v.wait_ge(S["xt_ready"], m + 1)
                if c is ATT_A:
                    for k in range(KD):
                        ins = nc.vector.tensor_scalar(h32[:, k * P:k * P + P], work[1][:, k * P:k * P + P],
                                                      vec_a[:, k:k + 1], vec_a[:, 2 + k:3 + k], ALU.mult, ALU.add)
                    ins.then_inc(S["h32_ready"], 1)
                else:
                    v.wait_ge(S["h_hi"], m + 1)
                    nc.vector.tensor_tensor(h_lo[:], work[1][:, 0:D], h_hi[:].bitcast(F32),
                                            ALU.subtract).then_inc(S["h_lo"], 1)

            def norms(n, i):
                v.wait_ge(S[["q_squared", "k_squared"][i]], n + 1)
                nc.vector.tensor_reduce(norm2[:, 8 * i:8 * i + 8], heads(squares[i][:]), AX.X,
                                        ALU.add).then_inc(S["norm2_part"], 1)
                if i == 1:
                    v.wait_ge(S["norm2_part"], 2 * n + 2)
                    nc.vector.tensor_scalar_max(norm2c[:], norm2[:], 1e-24).then_inc(S["norm2_ready"], 1)

            def rotate_q(n):
                v.wait_ge(S["rope_ready"], n + 1)
                v.wait_ge(S["q_copied"], n + 1)
                rotate(nc.vector, 0, S["q_parts"])
                v.wait_ge(S["q_parts"], 4 * n + 3)
                nc.vector.tensor_tensor(cos_part[0][:], cos_part[0][:], squares[0][:], ALU.add).then_inc(S["q_parts"], 1)

            def scale_rotated(n):
                for i, summed, done in ((0, "q_parts", "q_rot"), (1, "k_parts", "k_rot")):
                    v.wait_ge(S[summed], 4 * n + 4)
                    v.wait_ge(S["rnorm_ready"], n + 1)
                    r = rnorm[:, 8 * i:8 * i + 8].unsqueeze(2).to_broadcast([P, c.NH, c.DH])
                    nc.vector.tensor_tensor(heads(rot[i][:]), heads(cos_part[i][:]), r, ALU.mult).then_inc(S[done], 1)

            def copy_q_t(n):
                v.wait_ge(S["qt_ready"], n + 1)
                nc.vector.tensor_copy(q_t[:].rearrange("p t q -> p (t q)"), work[1][:]).then_inc(S["qt_copied"], 1)

            def mask_pair(g, e, p):
                waits = [(S["scores_ready"], g * c.NP + (p + 1))]
                if p >= 2:
                    waits.append((S["probs_ready"], g * c.NP + (p - 1)))
                if e == 0 and p == 0:
                    waits.append((S["mask0_ready"], g_iter[0]))
                wait_apart(v, *waits)
                for hh in range(2):
                    h = c.head(p, hh)
                    cols = slice(hh * 256, hh * 256 + 256)
                    ins = nc.vector.tensor_tensor_reduce(masked[p % 2][:, cols], scores[p % 2][:, cols],
                                                         (mask0 if e == 0 else mask)[:], -1.0, BIG, ALU.add, ALU.min,
                                                         neg_max[:, h:h + 1])
                ins.then_inc(S["masked_ready"], 1)

            def copy_probs(g, p):
                by, k, per = evacuator(c, p)
                if by != "pt_dve":
                    return
                v.wait_ge(S["pt_ready"], g * c.NP + (p + 1))
                if p >= 2:
                    v.wait_ge(S["pv_done"], g * c.NP + (p - 1))
                nc.vector.tensor_copy(pt[p % 2][:], probs_t[p % 2][:]).then_inc(S["pt_dve"], 1)

            def normalize_heads(g):
                v.wait_ge(S["pv_done"], g * c.NP + c.NP)
                nc.vector.reciprocal(inv_sum[:, 0:c.NH], row_sum[:, 0:c.NH]).then_inc(S["inv_ready"], 1)
                v.wait_ge(S["inv_ready"], g + 1)
                r = inv_sum[:, 0:c.NH].unsqueeze(2).to_broadcast([P, c.NH, c.DH])
                nc.vector.tensor_tensor(heads(o_tok[:, 0:c.OC]), heads(heads_out[:, 0:c.OC]), r,
                                        ALU.mult).then_inc(S["o_ready"], 1)

            def split_o(g):
                v.wait_ge(S["ot_ready"], g + 1)
                v.wait_ge(S["o_hi"], g + 1)
                nc.vector.tensor_tensor(o_lo[:, 0:c.OC], work[0][:, 0:c.OC], o_hi[:, 0:c.OC].bitcast(F32),
                                        ALU.subtract).then_inc(S["o_lo"], 1)

            def add_residual(g, e):
                v.wait_ge(S["wo_ready"], g + 1)
                per = 16 if c is ATT_A else 32
                v.wait_ge(S[f"store{e % 2}"], (g - e % 2) * (per // 2) + per)
                res = x_in if c is ATT_A else x_res
                nc.vector.tensor_tensor(y_out[:, e % 2, :], work[0][:, 0:D], res[:, e, :], ALU.add).then_inc(S["y_ready"], 1)

            def make_mask0(it, j):
                src = mask0_prev[:, j, :] if isinstance(j, int) else \
                    mask0_prev[:, bass.ds(j, 1), :].rearrange("p a k -> p (a k)")
                nc.vector.tensor_copy(mask0[:, 0:P], src).then_inc(S["mask0_ready"], 1)

            g_iter = [None]

            def prologue(base):
                v.wait_ge(S["params"], 64 if layer is None else layer * 64 + 64)
                if c is ATT_A:
                    layer_norm_stats(base, 0)
                    normalize(base, 0)
                    h_transposed(base)
                    layer_norm_stats(base + 1, 1)
                    normalize(base + 1, 1)
                else:
                    h_transposed(base)
                    norms(base, 0)
                    norms(base, 1)
                    rotate_q(base)
                    scale_rotated(base)
                copy_q_t(base)
                h_transposed(base + 1)

            def step(g, e, j, g_local, more, more2):
                if e == 0:
                    it = ITERS - 1 if isinstance(j, int) else j
                    g_iter[0] = it + 1 if layer is None else layer * ITERS + (it + 1)
                    make_mask0(None, j)
                n, m, ms = g + 1, g + 2, (e + 2) % U
                if c is ATT_A:
                    between = {1: lambda: layer_norm_stats(m, ms) if more2 else None,
                               5: lambda: normalize(m, ms) if more2 else None}
                else:
                    between = {1: lambda: norms(n, 0) if more else None,
                               2: lambda: (norms(n, 1), rotate_q(n)) if more else None}
                mask_pair(g, e, 0)
                for p in range(c.NP):
                    if p + 1 < c.NP:
                        mask_pair(g, e, p + 1)
                    copy_probs(g, p)
                    if p in between:
                        between[p]()
                if more and c is ATT_B:
                    scale_rotated(n)
                normalize_heads(g)
                if more:
                    copy_q_t(n)
                split_o(g)
                if more2:
                    h_transposed(m)
                add_residual(g, e)

            attention_loop(v, c, layer, prologue, step)

        def rotate(engine, i, done):
            x = qk[i][:].rearrange("p (h d) -> p h d", d=64)
            half = 32
            def table(a, lo, hi):
                return rope[:, a, lo:hi].unsqueeze(1).to_broadcast([P, 8, hi - lo])
            engine.tensor_tensor(cos_part[i][:].rearrange("p (h d) -> p h d", d=64), x, table(2 * i, 0, 64),
                                 ALU.mult).then_inc(done, 1)
            s = squares[i][:].rearrange("p (h d) -> p h d", d=64)
            engine.tensor_tensor(s[:, :, 0:half], x[:, :, half:64], table(2 * i + 1, 0, half), ALU.mult).then_inc(done, 1)
            engine.tensor_tensor(s[:, :, half:64], x[:, :, 0:half], table(2 * i + 1, half, 64), ALU.mult).then_inc(done, 1)

        def m_load_count(c, t, slot):
            per = 32 if c is MLP_A else 64
            return (t - slot) * (per // 2) + per

        def dve_mlp(v, c, S, layer):
            split_low(v, wm_raw, wm_hi, wm_lo, c.WCOLS, wm_loaded, wm_hi_done, wm_split, layer)
            vec = vec_a if c is MLP_A else vec_b
            g0c = 4 if c is MLP_A else 0

            def norm_stats(t, slot):
                v.wait_ge(S[f"load{slot}"], m_load_count(c, t, slot))
                for i in range(4):
                    ins = nc.vector.bn_stats(g_stats[:, i, :], g_in[slot][:, i, :])
                ins.then_inc(S["stats"], 1)
                wait_apart(v, (S["stats"], t + 1))
                for i in range(4):
                    ins = nc.vector.bn_aggr(g_mv[:, i, :], g_stats[:, i, :])
                ins.then_inc(S["aggr"], 1)
                v.wait_ge(S["aggr"], t + 1)
                nc.vector.tensor_scalar_add(g_ve[:], g_mv[:, :, 1], EPS).then_inc(S["var"], 1)

            def normalize(t, slot):
                v.wait_ge(S["rstd"], t + 1)
                for i in range(4):
                    ins = nc.vector.tensor_scalar(g_z[:, i, :], g_in[slot][:, i, :], g_mv[:, i, 0:1],
                                                  g_rstd[:, i:i + 1], ALU.subtract, ALU.mult)
                ins.then_inc(S["z_ready"], 1)

            def gain_bias(t):
                v.wait_ge(S["xt_ready"], t + 1)
                for k in range(KD):
                    nc.vector.tensor_scalar(g_h32[:, k, :], bank[4 + k][:], vec[:, g0c + k:g0c + k + 1],
                                            vec[:, g0c + 2 + k:g0c + 3 + k], ALU.mult, ALU.add).then_inc(S["h32_ready"], 1)

            def value(t, f):
                r = c.rows[f]
                v.wait_ge(S["in_ready"], t * (2 * c.NF) + (2 * f + 2))
                v.wait_ge(S["gate_ready"], t * c.NF + (f + 1))
                if f >= 2:
                    v.wait_ge(S["u_hi"], t * c.NF + (f - 1))
                    v.wait_ge(S[["u_lo_dve", "u_lo_pool"][f % 2]], t * 3 + (f // 2))
                nc.vector.scalar_tensor_tensor(hid[f % 2][0:r, :], bank[(2 * f + 1) % 4][0:r, :], vec[0:r, 4 + f:5 + f],
                                               gate[f % 2][0:r, :], ALU.add, ALU.mult).then_inc(S["hid_ready"], 1)

            def low(t, f):
                r = c.rows[f]
                src = hid if c.gated else gate
                v.wait_ge(S["u_hi"], t * c.NF + (f + 1))
                if c.gated:
                    v.wait_ge(S["hid_ready"], t * c.NF + (f + 1))
                nc.vector.tensor_tensor(u_lo[0:r, f, :], src[f % 2][0:r, :], u_hi[0:r, f, :].bitcast(F32),
                                        ALU.subtract).then_inc(S["u_lo_dve"], 1)

            def group(t, slot, more):
                if more:
                    norm_stats(t + 1, 1 - slot)
                if c.gated:
                    for f in range(c.NF):
                        value(t, f)
                        if f % 2 == 0:
                            low(t, f)
                        if f == 2 and more:
                            normalize(t + 1, 1 - slot)
                else:
                    for f in range(c.NF):
                        low(t, f)
                        if f == 4 and more:
                            normalize(t + 1, 1 - slot)
                if more:
                    gain_bias(t + 1)
                v.wait_ge(S["res_ready"], t + 1)
                n = 32 if c is MLP_A else 48
                v.wait_ge(S["store"], t * n + n)
                for i in range(4):
                    if i % 2 == 0:
                        v.wait_ge(S["y_ready"], t * 2 + (i // 2 + 1))
                    nc.vector.tensor_tensor(g_new[:, i, :], bank[6 + i % 2][:, 0:D], g_sum[:, i, :],
                                            ALU.add).then_inc(S["y_added"], 1)
                v.wait_ge(S["y_added"], t * 4 + 4)
                nc.vector.tensor_tensor(g_sum[:], g_new[:], g_old[slot][:], ALU.add).then_inc(S["f_sum"], 1)
                v.wait_ge(S["f_sum"], t + 1)
                for i in range(4):
                    ins = nc.vector.bn_stats(f_stats[:, i, :], g_sum[:, i, :])
                ins.then_inc(S["f_stats"], 1)
                wait_apart(v, (S["f_stats"], t + 1))
                for i in range(4):
                    ins = nc.vector.bn_aggr(f_mv[:, i, :], f_stats[:, i, :])
                ins.then_inc(S["f_aggr"], 1)
                v.wait_ge(S["f_aggr"], t + 1)
                nc.vector.tensor_scalar_add(f_ve[:], f_mv[:, :, 1], EPS).then_inc(S["f_var"], 1)

            base = 0 if layer is None else v.snap(layer * NGRP)
            v.wait_ge(S["params"], 16 if layer is None else layer * 32 + 32)
            norm_stats(base, 0)
            normalize(base, 0)
            gain_bias(base)
            with v.Fori(0, NGRP // 2 - 1) as i:
                t0 = v.snap(i * 2) if layer is None else v.snap(layer * NGRP + i * 2)
                for e in range(2):
                    group(t0 + e, e, True)
            group(base + (NGRP - 2), 0, True)
            group(base + (NGRP - 1), 1, False)

        @block.vector
        def _(v):
            nc.vector.memset(zero_row[:], 0.0)
            nc.vector.memset(minus_half[:], -0.5).then_inc(consts_set, 1)
            dve_attention(v, ATT_A, SA, None)
            dve_mlp(v, MLP_A, MA, None)
            with v.Fori(0, LAYERS) as layer:
                dve_attention(v, ATT_B, SB, layer)
                dve_mlp(v, MLP_B, MB, layer)

        def split_high(a, raw, hi, cols, loaded, done, layer):
            a.wait_ge(loaded, 16 if layer is None else layer * 16 + 32)
            nc.scalar.activation(hi[:, 0:cols], raw[:, 0:cols], ACT.Copy).then_inc(done, 1)

        def act_attention(a, c, S, layer):
            split_high(a, wa_raw, wa_hi, c.WCOLS, wa_loaded, wa_hi_done, layer)

            def h_high(m):
                if c is ATT_A:
                    a.wait_ge(S["h32_ready"], m + 1)
                    nc.scalar.activation(h_hi[:], h32[:], ACT.Copy).then_inc(S["h_hi"], 1)
                else:
                    a.wait_ge(S["xt_ready"], m + 1)
                    nc.scalar.activation(h_hi[:], work[1][:, 0:D], ACT.Copy).then_inc(S["h_hi"], 1)

            def copy_qkv(n, slot, part):
                if c is ATT_A:
                    if part == 0:
                        a.wait_ge(S["q_proj"], n + 1)
                        for i, scale, done in ((0, c.DH ** -0.5, "q_copied"), (1, 1.0, "k_copied")):
                            nc.scalar.activation(qk[i][:].rearrange("p (h d) -> p h d", d=32)[:, :, 0:c.DH],
                                                 work[1][:, i * 256:i * 256 + 256].rearrange("p (h d) -> p h d", d=c.DH),
                                                 ACT.Copy, scale=scale).then_inc(S[done], 1)
                    elif part == 1:
                        a.wait_ge(S["v_proj"], n + 1)
                        nc.scalar.activation(v_tok[slot][:, 0:c.OC], work[2][:, 0:c.OC], ACT.Copy).then_inc(S["v_copied"], 1)
                    return
                if part < 2:
                    proj, copied, squared = (("q_proj", "q_copied", "q_squared"), ("k_proj", "k_copied", "k_squared"))[part]
                    a.wait_ge(S[proj], n + 1)
                    nc.scalar.activation(qk[part][:], work[1 + part][:], ACT.Copy).then_inc(S[copied], 1)
                    nc.scalar.activation(squares[part][:], work[1 + part][:], ACT.Square).then_inc(S[squared], 1)
                else:
                    a.wait_ge(S["v_proj"], n + 1)
                    nc.scalar.activation(v_tok[slot][:], work[0][:], ACT.Copy).then_inc(S["v_copied"], 1)

            def copy_k_t(n, slot):
                a.wait_ge(S["kt_ready"], n + 1)
                src = work[2][:].rearrange("p (t q) -> p t q", q=P)
                if slot == U - 1:
                    nc.scalar.activation(k_t[:, :, 0:P], src, ACT.Copy)
                nc.scalar.activation(k_t[:, :, (slot + 1) * P:(slot + 2) * P], src, ACT.Copy).then_inc(S["kt_copied"], 1)

            def exponentials(g, p):
                a.wait_ge(S["masked_ready"], g * c.NP + (p + 1))
                if p >= 2:
                    a.wait_ge(S["pt_ready"], g * c.NP + (p - 1))
                for hh in range(2):
                    h = c.head(p, hh)
                    cols = slice(hh * 256, hh * 256 + 256)
                    ins = nc.scalar.activation(probs[p % 2][:, cols], masked[p % 2][:, cols], ACT.Exp,
                                               bias=neg_max[:, h:h + 1], scale=-1.0, accum_out=row_sum[:, h:h + 1])
                ins.then_inc(S["probs_ready"], 1)

            def copy_probs(g, p):
                by, k, per = evacuator(c, p)
                if by != "pt_act":
                    return
                a.wait_ge(S["pt_ready"], g * c.NP + (p + 1))
                if p >= 2:
                    a.wait_ge(S["pv_done"], g * c.NP + (p - 1))
                nc.scalar.activation(pt[p % 2][:], probs_t[p % 2][:], ACT.Copy).then_inc(S["pt_act"], 1)

            def o_high(g):
                a.wait_ge(S["ot_ready"], g + 1)
                nc.scalar.activation(o_hi[:, 0:c.OC], work[0][:, 0:c.OC], ACT.Copy).then_inc(S["o_hi"], 1)

            def prologue(base):
                h_high(base)
                a.wait_ge(S["phase_set"], 2 if layer is None else layer * 2 + 2)
                for part in range(3):
                    copy_qkv(base, 0, part)
                copy_k_t(base, 0)
                h_high(base + 1)

            def step(g, e, j, g_local, more, more2):
                n, ns = g + 1, (e + 1) % U
                exponentials(g, 0)
                for p in range(c.NP):
                    if p + 1 < c.NP:
                        exponentials(g, p + 1)
                    if more and p < 3 and c is ATT_A:
                        copy_qkv(n, ns, p)
                    if more and p < 3 and c is ATT_B and p > 0:
                        copy_qkv(n, ns, p)
                    copy_probs(g, p)
                    if more and p == 0 and c is ATT_B:
                        copy_qkv(n, ns, p)
                if more:
                    copy_k_t(n, ns)
                o_high(g)
                if more2:
                    h_high(g + 2)

            attention_loop(a, c, layer, prologue, step)

        def act_mlp(a, c, S, layer):
            split_high(a, wm_raw, wm_hi, c.WCOLS, wm_loaded, wm_hi_done, layer)
            vec, b0 = (vec_a, 8) if c is MLP_A else (vec_b, 10)

            def h_high(t):
                a.wait_ge(S["h32_ready"], t * KD + KD)
                nc.scalar.activation(g_h_hi[:], g_h32[:], ACT.Copy).then_inc(S["h_hi"], 1)

            def gates(t, f):
                r = c.rows[f]
                if c.gated:
                    a.wait_ge(S["in_ready"], t * (2 * c.NF) + (2 * f + 1))
                    if f >= 2:
                        a.wait_ge(S["hid_ready"], t * c.NF + (f - 1))
                    src = bank[(2 * f) % 4]
                else:
                    a.wait_ge(S["in_ready"], t * c.NF + (f + 1))
                    if f >= 2:
                        a.wait_ge(S["u_lo_dve"], t * c.NF + (f - 1))
                    src = bank[f % 4]
                nc.scalar.activation(gate[f % 2][0:r, :], src[0:r, :], ACT.Gelu,
                                     bias=vec[0:r, b0 + f:b0 + f + 1]).then_inc(S["gate_ready"], 1)

            def high(t, f):
                r = c.rows[f]
                src = hid if c.gated else gate
                a.wait_ge(S["hid_ready"] if c.gated else S["gate_ready"], t * c.NF + (f + 1))
                if f == 0:
                    pass
                nc.scalar.activation(u_hi[0:r, f, :], src[f % 2][0:r, :], ACT.Copy).then_inc(S["u_hi"], 1)

            def group(t, more):
                gates(t, 0)
                for f in range(c.NF):
                    if f + 1 < c.NF:
                        gates(t, f + 1)
                    high(t, f)
                if more:
                    h_high(t + 1)

            base = 0 if layer is None else a.snap(layer * NGRP)
            h_high(base)
            with a.Fori(0, NGRP - 1) as i:
                group(a.snap(i + 0) if layer is None else a.snap(layer * NGRP + i), True)
            group(base + (NGRP - 1), False)

        @block.scalar
        def _(a):
            act_attention(a, ATT_A, SA, None)
            act_mlp(a, MLP_A, MA, None)
            with a.Fori(0, LAYERS) as layer:
                act_attention(a, ATT_B, SB, layer)
                act_mlp(a, MLP_B, MB, layer)

        def pool_attention(pool, c, S, layer):
            def set_start(base):
                wait_apart(pool, (S["load0"], 16 if layer is None else layer * (64 * ITERS) + 64))
                nc.gpsimd.memset(k_t[:, :, 0:P], 0.0)
                nc.gpsimd.memset(v_tok[U - 1][:], 0.0).then_inc(S["phase_set"], 1)
                nc.gpsimd.memset(qk[0][:], 0.0)
                nc.gpsimd.memset(qk[1][:], 0.0).then_inc(S["phase_set"], 1)

            def inverse_std(m):
                pool.wait_ge(S["ln_var"], m + 1)
                nc.gpsimd.tensor_tensor(rstd[:], var_eps[:], minus_half[:, 0:1], ALU.pow).then_inc(S["ln_rstd"], 1)

            def h_low(m):
                pool.wait_ge(S["h_hi"], m + 1)
                nc.gpsimd.tensor_tensor(h_lo[:], h32[:], h_hi[:].bitcast(F32), ALU.subtract).then_inc(S["h_lo"], 1)

            def tables(n, slot, steady):
                pool.wait_ge(S[f"load{slot}"], load_count(c, n, slot))
                if steady:
                    pool.wait_ge(S["q_rot"], n)
                    pool.wait_ge(S["k_rot"], n)
                nc.gpsimd.tensor_tensor(rope[:].rearrange("p a d -> p (a d)"), rope_in[:, slot, :],
                                        rope_scale[:].rearrange("p a d -> p (a d)"), ALU.mult).then_inc(S["rope_ready"], 1)

            def rotate_k(n):
                pool.wait_ge(S["rope_ready"], n + 1)
                pool.wait_ge(S["k_squared"], n + 1)
                pool.wait_ge(S["norm2_part"], 2 * n + 2)
                rotate(nc.gpsimd, 1, S["k_parts"])
                pool.wait_ge(S["norm2_ready"], n + 1)
                nc.gpsimd.tensor_tensor(rnorm[:], norm2c[:], minus_half[:], ALU.pow).then_inc(S["rnorm_ready"], 1)
                pool.wait_ge(S["k_parts"], 4 * n + 3)
                nc.gpsimd.tensor_tensor(cos_part[1][:], cos_part[1][:], squares[1][:], ALU.add).then_inc(S["k_parts"], 1)

            def prologue(base):
                set_start(base)
                if c is ATT_A:
                    inverse_std(base)
                    inverse_std(base + 1)
                    h_low(base)
                    h_low(base + 1)
                else:
                    pool.wait_ge(S["params"], layer * 64 + 64)
                    tables(base, 0, False)
                    rotate_k(base)

            def step(g, e, j, g_local, more, more2):
                if c is ATT_A:
                    if more2:
                        inverse_std(g + 2)
                        h_low(g + 2)
                elif more:
                    tables(g + 1, (e + 1) % U, True)
                    rotate_k(g + 1)

            attention_loop(pool, c, layer, prologue, step)

        def pool_mlp(pool, c, S, layer):
            def inverse_std(t):
                pool.wait_ge(S["var"], t + 1)
                nc.gpsimd.tensor_tensor(g_rstd[:], g_ve[:], minus_half[:, 0:4], ALU.pow).then_inc(S["rstd"], 1)

            def h_low(t):
                pool.wait_ge(S["h_hi"], t + 1)
                nc.gpsimd.tensor_tensor(g_h_lo[:], g_h32[:], g_h_hi[:].bitcast(F32), ALU.subtract).then_inc(S["h_lo"], 1)

            def residual(t, slot, steady):
                pool.wait_ge(S[f"load{slot}"], m_load_count(c, t, slot))
                if steady:
                    pool.wait_ge(S["fin_ready"], t)
                src = g_in if c is MLP_A else g_mid
                b = row_b2[:].unsqueeze(1).to_broadcast([P, 4, D])
                nc.gpsimd.tensor_tensor(g_sum[:], src[slot][:], b, ALU.add).then_inc(S["res_ready"], 1)

            def low(t, f):
                r = c.rows[f]
                pool.wait_ge(S["u_hi"], t * c.NF + (f + 1))
                nc.gpsimd.tensor_tensor(u_lo[0:r, f, :], hid[f % 2][0:r, :], u_hi[0:r, f, :].bitcast(F32),
                                        ALU.subtract).then_inc(S["u_lo_pool"], 1)

            def finish(t):
                pool.wait_ge(S["f_var"], t + 1)
                nc.gpsimd.tensor_tensor(f_rstd[:], f_ve[:], minus_half[:, 0:4], ALU.pow).then_inc(S["f_rstd"], 1)
                wait_apart(pool, (S["f_rstd"], t + 1))
                for i in range(4):
                    ins = nc.gpsimd.tensor_scalar(g_fin[:, i, :], g_sum[:, i, :], f_mv[:, i, 0:1], f_rstd[:, i:i + 1],
                                                  ALU.subtract, ALU.mult)
                ins.then_inc(S["fin_ready"], 1)

            def group(t, slot, more, steady=True):
                residual(t, slot, steady)
                if more:
                    inverse_std(t + 1)
                if c.gated:
                    for f in range(1, c.NF, 2):
                        low(t, f)
                if more:
                    h_low(t + 1)
                finish(t)

            base = 0 if layer is None else pool.snap(layer * NGRP)
            pool.wait_ge(S["params"], 16 if layer is None else layer * 32 + 32)
            inverse_std(base)
            h_low(base)
            group(base, 0, True, False)
            with pool.Fori(0, NGRP // 2 - 1) as i:
                t0 = pool.snap(i * 2 + 1) if layer is None else pool.snap(layer * NGRP + i * 2 + 1)
                for e in range(2):
                    group(t0 + e, 1 - e, True)
            group(base + (NGRP - 1), 1, False)

        @block.gpsimd
        def _(pool):
            pool_attention(pool, ATT_A, SA, None)
            pool_mlp(pool, MLP_A, MA, None)
            with pool.Fori(0, LAYERS) as layer:
                pool_attention(pool, ATT_B, SB, layer)
                pool_mlp(pool, MLP_B, MB, layer)


def contraction_tiles(w, tile=P):
    k, n = w.shape
    tiles = -(-k // tile)
    out = np.zeros((P, tiles, n), np.float32)
    for i in range(tiles):
        part = w[i * tile:(i + 1) * tile]
        out[:part.shape[0], i] = part
    return out.reshape(P, tiles * n)


def columns(*vectors_and_tiles):
    cols = []
    for vec, tile in vectors_and_tiles:
        for i in range(0, len(vec), tile):
            col = np.zeros(P, np.float32)
            col[:len(vec[i:i + tile])] = vec[i:i + tile]
            cols.append(col)
    out = np.zeros((P, 16), np.float32)
    out[:, :len(cols)] = np.stack(cols, 1)
    return out


def window_masks(first_key):
    q, k = np.arange(P)[:, None], np.arange(2 * P)[None, :]
    full = np.where((k >= q + first_key) & (k <= q + P), 0.0, MASKED).astype(np.float32)
    first = np.repeat(full[:, None, :P], ITERS, 1)
    first[:, ::ITERS // B] = MASKED
    return full, np.ascontiguousarray(first)


def rope_tables():
    dim, window, qk_scale = ATT_B.DH, P, 8.0
    half = np.arange(0, dim, 2, dtype=np.float32)
    inv_freq = (np.float32(1.0) / np.float32(10000.0) ** (half / np.float32(dim))).astype(np.float32)
    t = np.arange(SEQ, dtype=np.float32)
    freqs = t[:, None] * inv_freq[None, :]
    cos, sin = np.cos(freqs), np.sin(freqs)
    base = ((half + np.float32(0.4 * dim)) / np.float32(1.4 * dim)).astype(np.float32)
    power = ((t - SEQ // 2) / np.float32(window // 2)).astype(np.float32)
    scale = np.power(base[None, :], power[:, None]).astype(np.float32)
    parts = []
    for s in (scale * np.float32(qk_scale), np.float32(1.0) / scale):
        parts += [np.concatenate([cos * s, cos * s], 1), np.concatenate([-sin * s, sin * s], 1)]
    return np.tile(np.concatenate(parts, 1).astype(np.float32), (B, 1))


def kernel(L0_attn_x, L0_attn_w_qkv, L0_attn_w_o, L0_attn_ln1_g, L0_attn_ln1_b, L0_attn_ln2_g, L0_attn_ln2_b,
           L0_attn_mlp_w1, L0_attn_mlp_b1, L0_attn_mlp_w2, L0_attn_mlp_b2, L0_ffn_wqkv, L0_ffn_q_scale,
           L0_ffn_k_scale, L0_ffn_wo, L0_ffn_ln_g, L0_ffn_ln_b, L0_ffn_w1, L0_ffn_b1, L0_ffn_w2, L0_ffn_b2):
    import concourse.bacc as bacc
    from concourse.bass_utils import run_bass_kernel_spmd

    a = [np.asarray(t) for t in (L0_attn_x, L0_attn_w_qkv, L0_attn_w_o, L0_attn_mlp_w1, L0_attn_mlp_w2)]
    x, w_qkv, w_o, w1, w2 = a
    wqkv_b, wo_b, w1_b, w2_b = (np.asarray(t) for t in (L0_ffn_wqkv, L0_ffn_wo, L0_ffn_w1, L0_ffn_w2))
    qs, ks = np.asarray(L0_ffn_q_scale), np.asarray(L0_ffn_k_scale)
    lg, lb, b1, b2 = (np.asarray(t) for t in (L0_ffn_ln_g, L0_ffn_ln_b, L0_ffn_b1, L0_ffn_b2))
    mask_a, mask_a0 = window_masks(1)
    mask_b, mask_b0 = window_masks(0)

    def swap(s):
        return np.concatenate([s[ATT_B.DH // 2:], s[:ATT_B.DH // 2]])

    H = MLP_B.H
    data = {
        "x": x.reshape(TOK, D),
        "w_att_a": np.concatenate([contraction_tiles(w_qkv.T), contraction_tiles(w_o.T)], 1),
        "w_mlp_a": np.concatenate([contraction_tiles(w1.T), contraction_tiles(w2.T)], 1),
        "w_att_b": np.concatenate([np.concatenate([contraction_tiles(wqkv_b[l]), contraction_tiles(wo_b[l])], 1)
                                   for l in range(LAYERS)], 0),
        "w_mlp_b": np.concatenate([np.concatenate([contraction_tiles(w1_b[l]), contraction_tiles(w2_b[l], MLP_B.FT)], 1)
                                   for l in range(LAYERS)], 0),
        "vec_a": columns((np.asarray(L0_attn_ln1_g), P), (np.asarray(L0_attn_ln1_b), P), (np.asarray(L0_attn_ln2_g), P),
                         (np.asarray(L0_attn_ln2_b), P), (np.asarray(L0_attn_mlp_b1), P)),
        "vec_b": np.concatenate([columns((lg[l], P), (lb[l], P), (b1[l][:H], MLP_B.FT), (b1[l][H:], MLP_B.FT))
                                 for l in range(LAYERS)], 0),
        "b2_a": np.broadcast_to(np.asarray(L0_attn_mlp_b2), (P, D)),
        "b2_b": np.concatenate([np.broadcast_to(b2[l], (P, D)) for l in range(LAYERS)], 0),
        "rope": rope_tables(),
        "rope_scale": np.concatenate([np.broadcast_to(np.concatenate([qs[l], swap(qs[l]), ks[l], swap(ks[l])]), (P, D))
                                      for l in range(LAYERS)], 0),
        "mask_a": mask_a, "mask_a0": mask_a0, "mask_b": mask_b, "mask_b0": mask_b0,
        "ident": np.eye(P, dtype=np.float32),
    }
    nc = bacc.Bacc("TRN2", target_bir_lowering=False, num_devices=1)
    arrays, io = {}, {}
    for name, arr in data.items():
        arrays[f"in_{name}"] = np.ascontiguousarray(arr)
        io[name] = nc.dram_tensor(f"in_{name}", arrays[f"in_{name}"].shape, F32, kind="ExternalInput").ap()
    io["out"] = nc.dram_tensor("out_x", (TOK, D), F32, kind="ExternalOutput").ap()
    build(nc, io)
    r = run_bass_kernel_spmd(nc, [arrays], core_ids=[0])
    return r.results[0]["out_x"].reshape(B, SEQ, D)
```

```python
from contextlib import ExitStack

import concourse.bass as bass
import numpy as np
from concourse import mybir

F32 = mybir.dt.float32
F32R = mybir.dt.float32r
ALU = mybir.AluOpType
ACT = mybir.ActivationFunctionType
AX = mybir.AxisListType

P = 128
B, SEQ, D = 2, 2048, 256
TOK = B * SEQ
NCH = TOK // P
U = 4
ITERS = NCH // U
KD = D // P
GT = 4 * P
NGRP = TOK // GT
LAYERS = 2
EPS = 1e-5
MASKED = -1.0e30
BIG = 3.0e38


class Attention:

    def __init__(self, heads, dim, rows, row_step, ahead):
        self.NH, self.DH = heads, dim
        self.NP = heads // 2
        self.R = rows
        self.RS = row_step
        self.HPT = P // row_step
        self.NT = heads // self.HPT
        self.OC = heads * dim
        self.KO = self.OC // P
        self.QKV = 3 * self.OC
        self.WCOLS = KD * self.QKV + self.KO * D
        self.TB = self.NT // 4
        self.AHEAD = ahead

    def head(self, p, i):
        row, tiles = p % self.HPT, 2 * (p // self.HPT)
        return (tiles + i) * self.HPT + row


ATT_A = Attention(heads=16, dim=16, rows=48, row_step=64, ahead=1)
ATT_B = Attention(heads=8, dim=64, rows=64, row_step=64, ahead=2)


class Mlp:

    def __init__(self, hidden, tile, gated):
        self.H, self.FT, self.gated = hidden, tile, gated
        self.NF = -(-hidden // tile)
        self.rows = [min(tile, hidden - tile * f) for f in range(self.NF)]
        self.IN = hidden * (2 if gated else 1)
        self.WCOLS = KD * self.IN + self.NF * D


MLP_A = Mlp(4 * D, P, False)
MLP_B = Mlp(int(D * 4 * 2 / 3), 114, True)
WA = max(ATT_A.WCOLS, ATT_B.WCOLS)
WM = max(MLP_A.WCOLS, MLP_B.WCOLS)


def build(nc, io):
    x_state = nc.dram_tensor("x_state", ((LAYERS + 1) * TOK, D), F32, kind="Internal").ap()
    x_state_sh = nc.dram_tensor("x_state_sh", ((LAYERS + 1) * (TOK + P), P), F32, kind="Internal").ap()
    x_mid = nc.dram_tensor("x_mid", (TOK, D), F32, kind="Internal").ap()
    x_mid_sh = nc.dram_tensor("x_mid_sh", (TOK + P, P), F32, kind="Internal").ap()

    ctx = ExitStack()
    with ctx:
        def sbuf(name, shape, dt=F32, at=ctx):
            return at.enter_context(nc.sbuf_tensor(name, shape, dt))

        def sem(name):
            return ctx.enter_context(nc.semaphore(name))

        bank = [ctx.enter_context(nc.psum_tensor(f"bank{i}", [P, 512], F32)) for i in range(8)]
        work = bank[0:3]
        scores = bank[3:5]
        probs_t = bank[5:7]
        heads_out = bank[7]

        wa_raw = sbuf("wa_raw", [P, WA])
        wm_raw = sbuf("wm_raw", [P, WM])
        wa_hi, wa_lo = sbuf("wa_hi", [P, WA], F32R), sbuf("wa_lo", [P, WA], F32R)
        wm_hi, wm_lo = sbuf("wm_hi", [P, WM], F32R), sbuf("wm_lo", [P, WM], F32R)
        ident = sbuf("ident", [P, P])
        zero_row = sbuf("zero_row", [P, 2, P])
        minus_half = sbuf("minus_half", [P, 16])
        vec_a = sbuf("vec_a", [P, 16])
        vec_b = sbuf("vec_b", [P, 16])
        row_b2 = sbuf("row_b2", [P, D])

        at_ctx = ExitStack()
        x_in = sbuf("x_in", [P, U, D], at=at_ctx)
        h_hi, h_lo = sbuf("h_hi", [P, D], F32R, at_ctx), sbuf("h_lo", [P, D], F32R, at_ctx)
        v_tok = [sbuf(f"v_tok{i}", [P, 512], at=at_ctx) for i in range(U)]
        masked = [sbuf(f"masked{i}", [P, 512], at=at_ctx) for i in range(2)]
        probs = [sbuf(f"probs{i}", [P, 512], at=at_ctx) for i in range(2)]
        pt = [sbuf(f"pt{i}", [P, 512], at=at_ctx) for i in range(2)]
        neg_max = sbuf("neg_max", [P, 16], at=at_ctx)
        row_sum = sbuf("row_sum", [P, 2, 16], at=at_ctx)
        inv_sum = sbuf("inv_sum", [P, 16], at=at_ctx)
        o_tok = sbuf("o_tok", [P, 512], at=at_ctx)
        o_hi, o_lo = sbuf("o_hi", [P, 512], F32R, at_ctx), sbuf("o_lo", [P, 512], F32R, at_ctx)
        y_out = sbuf("y_out", [P, 2, D], at=at_ctx)
        mask = sbuf("mask", [P, 2 * P], at=at_ctx)
        mask0 = sbuf("mask0", [P, 2 * P], at=at_ctx)
        mask0_prev = sbuf("mask0_prev", [P, ITERS, P], at=at_ctx)
        b_ctx = ExitStack()
        x_res = sbuf("x_res", [P, U, D], at=b_ctx)
        rope_in = sbuf("rope_in", [P, U, D], at=b_ctx)
        rope = sbuf("rope", [P, 4, 64], at=b_ctx)
        rope_scale = sbuf("rope_scale", [P, 4, 64], at=b_ctx)
        qk = [sbuf("q_tok", [P, 512], at=b_ctx), sbuf("k_tok", [P, 512], at=b_ctx)]
        squares = [sbuf("q_sq", [P, 512], at=b_ctx), sbuf("k_sq", [P, 512], at=b_ctx)]
        cos_part = [sbuf("q_cos", [P, 512], at=b_ctx), sbuf("k_cos", [P, 512], at=b_ctx)]
        rot = [sbuf("q_rot", [P, 512], at=b_ctx), sbuf("k_rot", [P, 512], at=b_ctx)]
        norm2 = sbuf("norm2", [P, 16], at=b_ctx)
        norm2c = sbuf("norm2c", [P, 16], at=b_ctx)
        rnorm = sbuf("rnorm", [P, 16], at=b_ctx)
        q_t_b = sbuf("q_t_b", [P, ATT_B.NT, P], at=b_ctx)
        k_t_b = sbuf("k_t_b", [P, ATT_B.NT, (U + 1) * P], at=b_ctx)
        b_ctx.close()
        a_ctx = ExitStack()
        z = sbuf("z", [P, D], at=a_ctx)
        h32 = sbuf("h32", [P, D], at=a_ctx)
        stats = sbuf("stats", [P, 6], at=a_ctx)
        mean_var = sbuf("mean_var", [P, 2], at=a_ctx)
        var_eps = sbuf("var_eps", [P, 1], at=a_ctx)
        rstd = sbuf("rstd", [P, 1], at=a_ctx)
        q_stack = sbuf("q_stack", [P, 16, 4, 16], F32R, a_ctx)
        k_stack = sbuf("k_stack", [P, 16, 4, 16], F32R, a_ctx)
        q_t_a = sbuf("q_t_a", [P, ATT_A.NT, P], F32R, a_ctx)
        k_t_a = sbuf("k_t_a", [P, ATT_A.NT, (U + 1) * P], F32R, a_ctx)
        a_ctx.close()
        at_ctx.close()

        m_ctx = ExitStack()
        g_in = [sbuf(f"g_in{i}", [P, 4, D], at=m_ctx) for i in range(2)]
        g_mid = [sbuf(f"g_mid{i}", [P, 4, D], at=m_ctx) for i in range(2)]
        g_old = [sbuf(f"g_old{i}", [P, 4, D], at=m_ctx) for i in range(2)]
        g_z = sbuf("g_z", [P, 4, D], at=m_ctx)
        g_stats = sbuf("g_stats", [P, 4, 6], at=m_ctx)
        g_mv = sbuf("g_mv", [P, 4, 2], at=m_ctx)
        g_ve = sbuf("g_ve", [P, 4], at=m_ctx)
        g_rstd = sbuf("g_rstd", [P, 4], at=m_ctx)
        f_stats = sbuf("f_stats", [P, 4, 6], at=m_ctx)
        f_mv = sbuf("f_mv", [P, 4, 2], at=m_ctx)
        f_ve = sbuf("f_ve", [P, 4], at=m_ctx)
        f_rstd = sbuf("f_rstd", [P, 4], at=m_ctx)
        g_h32 = sbuf("g_h32", [P, KD, GT], at=m_ctx)
        g_h_hi, g_h_lo = sbuf("g_h_hi", [P, KD, GT], F32R, m_ctx), sbuf("g_h_lo", [P, KD, GT], F32R, m_ctx)
        gate = [sbuf(f"gate{i}", [P, GT], at=m_ctx) for i in range(2)]
        hid = [sbuf(f"hid{i}", [P, GT], at=m_ctx) for i in range(2)]
        u_hi, u_lo = sbuf("u_hi", [P, 8, GT], F32R, m_ctx), sbuf("u_lo", [P, 8, GT], F32R, m_ctx)
        g_sum = sbuf("g_sum", [P, 4, D], at=m_ctx)
        g_new = sbuf("g_new", [P, 4, D], at=m_ctx)
        g_fin = sbuf("g_fin", [P, 4, D], at=m_ctx)
        m_ctx.close()

        consts_loaded = sem("consts_loaded")
        consts_set = sem("consts_set")
        zero_rows_stored = sem("zero_rows_stored")
        wa_loaded, wm_loaded = sem("wa_loaded"), sem("wm_loaded")
        wa_split, wm_split = sem("wa_split"), sem("wm_split")
        wa_hi_done, wm_hi_done = sem("wa_hi_done"), sem("wm_hi_done")

        def sems(prefix, names):
            return {n: sem(f"{prefix}_{n}") for n in names.split()}

        att_names = """load0 load1 load2 load3 store0 store1 params phase_set
            ln_stats ln_aggr ln_var ln_rstd z_ready xt_ready h32_ready h_hi h_lo
            q_proj k_proj v_proj q_hi k_hi q_lo k_lo q_copied k_copied v_copied q_squared k_squared norm2_part norm2_ready rnorm_ready
            rope_ready q_parts k_parts q_rot k_rot qt_ready kt_ready qt_copied kt_copied
            mask0_ready scores_ready masked_ready probs_ready pt_ready pt_dve pt_act pv_done
            inv_ready o_ready ot_ready o_hi o_lo wo_ready y_ready"""
        SA = sems("a", " ".join(n for n in att_names.split() if n not in
                                "k_proj q_copied k_copied q_squared k_squared norm2_part norm2_ready rnorm_ready rope_ready q_parts k_parts q_rot k_rot".split()))
        SB = sems("b", " ".join(n for n in att_names.split() if n not in
                                "ln_stats ln_aggr ln_var ln_rstd z_ready h32_ready q_hi k_hi q_lo k_lo".split()))
        mlp_names = """load0 load1 store params stats aggr var rstd z_ready xt_ready h32_ready h_hi h_lo
            in_ready gate_ready hid_ready u_hi u_lo_dve u_lo_pool y_ready y_added res_ready
            f_sum f_stats f_aggr f_var f_rstd fin_ready"""
        MA = sems("ma", " ".join(n for n in mlp_names.split() if n not in ("hid_ready", "u_lo_pool")))
        MB = sems("mb", mlp_names)

        def wait_apart(eng, *waits):
            values = [(s, v if isinstance(v, int) else eng.snap(v)) for s, v in waits]
            for _, v in values:
                if not isinstance(v, int):
                    eng.lower_val(v)
            eng.wait_ge(consts_set, 1)
            for s, v in values:
                eng.wait_ge(s, v)

        block = ctx.enter_context(nc.Block())

        def attention_loop(eng, c, layer, prologue, step):
            base = 0 if layer is None else eng.snap(layer * NCH)
            prologue(base)
            start = 1 if c is ATT_A else 0
            for e in range(U * start):
                step(base + e, e, 0, e, {d: e + d >= 0 for d in range(-1, 4)})
            with eng.Fori(start, ITERS - 1) as j:
                g0 = eng.snap(j * U) if layer is None else eng.snap(layer * NCH + j * U)
                for e in range(U):
                    step(g0 + e, e, j, j * U + e, {d: True for d in range(-1, 4)})
            last = U * (ITERS - 1)
            for e in range(U):
                step(base + last + e, e, ITERS - 1, last + e, {d: e + d < U for d in range(-1, 4)})

        def load_attention_weights(sp, which):
            sp.dma_start(wa_raw[:, 0:which.shape[-1]], which).then_inc(wa_loaded, 16)

        def load_mlp_weights(sp, which):
            sp.dma_start(wm_raw[:, 0:which.shape[-1]], which).then_inc(wm_loaded, 16)

        def sp_attention(sp, c, S, layer):
            gated = c is ATT_B

            def load(n_local, slot):
                rows = bass.ds(n_local * P, P) if not isinstance(n_local, int) else slice(n_local * P, n_local * P + P)
                if c is ATT_A:
                    sp.dma_start(x_in[:, slot, :], io["x"][rows, :]).then_inc(S[f"load{slot}"], 16)
                    return
                srow = bass.ds(layer * TOK + n_local * P, P)
                hrow = bass.ds(layer * (TOK + P) + n_local * P, P)
                s = S[f"load{slot}"]
                sp.dma_start(x_in[:, slot, 0:P], x_state[srow, 0:P]).then_inc(s, 16)
                sp.dma_start(x_in[:, slot, P:D], x_state_sh[hrow, :]).then_inc(s, 16)
                sp.dma_start(x_res[:, slot, :], x_state[srow, :]).then_inc(s, 16)
                sp.dma_start(rope_in[:, slot, :], io["rope"][rows, :]).then_inc(s, 16)

            def prologue(base):
                load(0, 0)
                load(1, 1)
                if c is ATT_A:
                    sp.dma_start(mask[:], io["mask_a"]).then_inc(S["params"], 16)
                    sp.dma_start(mask0[:], io["mask_a"]).then_inc(S["params"], 16)
                    sp.dma_start(mask0_prev[:], io["mask_a0"]).then_inc(S["params"], 16)
                    sp.dma_start(vec_a[:], io["vec_a"]).then_inc(S["params"], 16)
                else:
                    sp.dma_start(mask[:], io["mask_b"]).then_inc(S["params"], 16)
                    sp.dma_start(mask0[:], io["mask_b"]).then_inc(S["params"], 16)
                    sp.dma_start(mask0_prev[:], io["mask_b0"]).then_inc(S["params"], 16)
                    sp.dma_start(rope_scale[:].rearrange("p a d -> p (a d)"),
                                 io["rope_scale"][bass.ds(layer * P, P), :]).then_inc(S["params"], 16)
                load(2, 2)
                load(3, 3)

            def step(g, e, j, g_local, more):
                sp.wait_ge(S["y_ready"], g + 1)
                rows = bass.ds(g_local * P, P) if not isinstance(g_local, int) else slice(g_local * P, g_local * P + P)
                hrows = bass.ds(g_local * P + 1, P) if not isinstance(g_local, int) else \
                    slice(g_local * P + 1, g_local * P + 1 + P)
                sp.dma_start(x_mid[rows, :], y_out[:, e % 2, :]).then_inc(S[f"store{e % 2}"], 16)
                if gated:
                    sp.dma_start(x_mid_sh[hrows, :], y_out[:, e % 2, P:D]).then_inc(S[f"store{e % 2}"], 16)
                if not isinstance(j, int) or j < ITERS - 1:
                    load(g_local + U, e)

            attention_loop(sp, c, layer, prologue, step)
            n = 32 if gated else 16
            for e in range(2):
                sp.wait_ge(S[f"store{e}"], n * (NCH // 2) + n if layer is None else
                           layer * (n * (NCH // 2)) + (n * (NCH // 2) + n))
            if gated:
                sp.dma_start(x_mid_sh[0:1, :], zero_row[0:1, 0, :]).then_inc(zero_rows_stored, 16)
                sp.dma_start(x_mid_sh[SEQ:SEQ + 1, :], zero_row[0:1, 1, :]).then_inc(zero_rows_stored, 16)
                sp.wait_ge(zero_rows_stored, layer * 64 + 32)

        def sp_mlp(sp, c, S, layer):
            def token_rows(ap, start, cols=slice(0, D)):
                r = bass.ds(start, GT) if not isinstance(start, int) else slice(start, start + GT)
                return ap[r, cols].rearrange("(c p) d -> p c d", p=P)

            def load(t_local, slot):
                s = S[f"load{slot}"]
                if c is MLP_A:
                    sp.dma_start(g_in[slot][:], token_rows(x_mid, t_local * GT)).then_inc(s, 16)
                    sp.dma_start(g_old[slot][:], token_rows(io["x"], t_local * GT)).then_inc(s, 16)
                    return
                sp.dma_start(g_in[slot][:, :, 0:P], token_rows(x_mid, t_local * GT, slice(0, P))).then_inc(s, 16)
                sp.dma_start(g_in[slot][:, :, P:D], token_rows(x_mid_sh, t_local * GT, slice(0, P))).then_inc(s, 16)
                sp.dma_start(g_mid[slot][:], token_rows(x_mid, t_local * GT)).then_inc(s, 16)
                sp.dma_start(g_old[slot][:], token_rows(x_state, t_local * GT)).then_inc(s, 16)

            load(0, 0)
            if c is MLP_A:
                sp.dma_start(row_b2[:], io["b2_a"]).then_inc(S["params"], 16)
            else:
                sp.dma_start(row_b2[:], io["b2_b"][bass.ds(layer * P, P), :]).then_inc(S["params"], 16)
                sp.dma_start(vec_b[:], io["vec_b"][bass.ds(layer * P, P), :]).then_inc(S["params"], 16)
            load(1, 1)
            load_attention_weights(sp, io["w_att_b"][0:P, :] if c is MLP_A else io["w_att_b"][P:2 * P, :])
            base = 0 if layer is None else layer * NGRP

            def store(t_local, t):
                s = S["store"]
                sp.wait_ge(S["fin_ready"], t + 1)
                if c is MLP_A:
                    sp.dma_start(token_rows(x_state, t_local * GT), g_fin[:]).then_inc(s, 16)
                    sp.dma_start(token_rows(x_state_sh, t_local * GT + 1, slice(0, P)), g_fin[:, :, P:D]).then_inc(s, 16)
                    return
                sp.dma_start(token_rows(x_state, (layer + 1) * TOK + t_local * GT), g_new[:]).then_inc(s, 16)
                sp.dma_start(token_rows(x_state_sh, (layer + 1) * (TOK + P) + t_local * GT + 1, slice(0, P)),
                             g_new[:, :, P:D]).then_inc(s, 16)
                sp.dma_start(token_rows(io["out"], t_local * GT), g_fin[:]).then_inc(s, 16)

            n = 32 if c is MLP_A else 48
            with sp.Fori(0, NGRP // 2 - 1) as i:
                t0 = sp.snap(i * 2) if layer is None else sp.snap(layer * NGRP + i * 2)
                for e in range(2):
                    store(i * 2 + e, t0 + e)
                    load(i * 2 + e + 2, e)
            for e in range(2):
                store(NGRP - 2 + e, base + NGRP - 2 + e)
            sp.wait_ge(S["store"], base * n + (n * NGRP + n))
            first = 0 if c is MLP_A else (layer + 1) * (TOK + P)
            for b in range(B):
                at = first + b * SEQ
                r = slice(at, at + 1) if isinstance(at, int) else bass.ds(at, 1)
                sp.dma_start(x_state_sh[r, :], zero_row[0:1, b, :]).then_inc(
                    S["params"] if c is MLP_A else zero_rows_stored, 16)
            if c is MLP_A:
                sp.wait_ge(S["params"], 16 + 32)
            else:
                wait_apart(sp, (zero_rows_stored, layer * 64 + 64))

        @block.sync
        def _(sp):
            for e in range(2):
                sp.sem_inc(SA[f"store{e}"], 16)
                sp.sem_inc(SB[f"store{e}"], 32)
            sp.sem_inc(MA["store"], 32)
            sp.sem_inc(MB["store"], 48)
            sp.dma_start(ident[:], io["ident"]).then_inc(consts_loaded, 16)
            sp.wait_ge(consts_set, 1)
            load_attention_weights(sp, io["w_att_a"])
            load_mlp_weights(sp, io["w_mlp_a"])
            sp_attention(sp, ATT_A, SA, None)
            sp_mlp(sp, MLP_A, MA, None)
            with sp.Fori(0, LAYERS) as layer:
                load_mlp_weights(sp, io["w_mlp_b"][bass.ds(layer * P, P), :])
                sp_attention(sp, ATT_B, SB, layer)
                sp_mlp(sp, MLP_B, MB, layer)

        def product3(out, a_hi, a_lo, b_hi, b_lo, first, last):
            nc.tensor.matmul(out, a_hi, b_hi, start=first, stop=False)
            nc.tensor.matmul(out, a_hi, b_lo, start=False, stop=False)
            return nc.tensor.matmul(out, a_lo, b_hi, start=False, stop=last)

        def pe_attention(pe, c, S, layer):
            wqkv_hi = wa_hi[:, 0:KD * c.QKV].rearrange("p (k n) -> p k n", k=KD)
            wqkv_lo = wa_lo[:, 0:KD * c.QKV].rearrange("p (k n) -> p k n", k=KD)
            wo_hi = wa_hi[:, KD * c.QKV:c.WCOLS].rearrange("p (k n) -> p k n", k=c.KO)
            wo_lo = wa_lo[:, KD * c.QKV:c.WCOLS].rearrange("p (k n) -> p k n", k=c.KO)
            q_t, k_t = (q_t_a, k_t_a) if c is ATT_A else (q_t_b, k_t_b)

            def project(n, part, n_before=None):
                if part == 0:
                    pe.wait_ge(S["h_hi"], n + 1)
                    pe.wait_ge(S["h_lo"], n + 1)
                if c is ATT_A:
                    if part == 2:
                        return
                    out, c0, w = [(work[1], 0, 512), (work[2], 512, 256)][part]
                    done = S[["q_proj", "v_proj"][part]]
                else:
                    if n_before is not None and part > 0:
                        pe.wait_ge(S[["", "k_squared", "v_copied"][part]], n_before + 1)
                    out, c0, w = [(work[1], 0, 512), (work[2], 512, 512), (work[0], 1024, 512)][part]
                    done = S[["q_proj", "k_proj", "v_proj"][part]]
                for k in range(KD):
                    mm = product3(out[:, 0:w], h_hi[:, k * P:k * P + P], h_lo[:, k * P:k * P + P],
                                  wqkv_hi[:, k, c0:c0 + w], wqkv_lo[:, k, c0:c0 + w], k == 0, k == KD - 1)
                mm.then_inc(done, 1)

            def transpose_x(m, slot):
                if c is ATT_A:
                    pe.wait_ge(S["z_ready"], m + 1)
                    src = z[:, :]
                else:
                    pe.wait_ge(S[f"load{slot}"], load_count(c, m, slot))
                    src = x_in[:, slot, :]
                for k in range(KD):
                    mm = nc.tensor.transpose(work[1][:, k * P:k * P + P], src[:, k * P:k * P + P], ident[:])
                mm.then_inc(S["xt_ready"], 1)

            def transpose_tiles(bank_, source, tile0, done):
                for i in range(4):
                    mm = nc.tensor.transpose(bank_[:, i * P:i * P + P], source[:, (tile0 + i) * P:(tile0 + i + 1) * P],
                                             ident[:])
                mm.then_inc(done, 1)

            def transpose_stack(n, part):
                if part == 0:
                    pe.wait_ge(S["q_lo"], n + 1)
                    pe.wait_ge(S["k_lo"], n + 1)
                elif part == 1:
                    pe.wait_ge(S["v_copied"], n + 1)
                else:
                    pe.wait_ge(S["kt_copied"], n * 2 + (part - 1))
                src = (k_stack if part < 2 else q_stack)[:].rearrange("p h s d -> p (h s d)").bitcast(F32)
                transpose_tiles(work[1 + part % 2], src, 4 * (part % 2), S["kt_ready" if part < 2 else "qt_ready"])

            def transpose_qk(n, projected):
                for i, (rotated, squared, done) in enumerate((("q_rot", "q_squared", "qt_ready"),
                                                              ("k_rot", "k_squared", "kt_ready"))):
                    if projected is not None:
                        pe.wait_ge(S[squared], projected + 1)
                    pe.wait_ge(S[rotated], n + 1)
                    transpose_tiles(work[1 + i], rot[i], 0, S[done])

            def score_pair(g, e, p, first=False):
                if p == 0:
                    pe.wait_ge(S["qt_copied"], g * c.TB + 1)
                    pe.wait_ge(S["kt_copied"], g * c.TB + c.TB)
                if p == 4:
                    pe.wait_ge(S["qt_copied"], g * c.TB + c.TB)
                if p >= 2 or not first:
                    pe.wait_ge(S["masked_ready"], g * c.NP + (p - 1))
                for hh in range(2):
                    h = c.head(p, hh)
                    t, r = h // c.HPT, (h % c.HPT) * c.RS
                    mm = nc.tensor.matmul(scores[p % 2][:, hh * 256:hh * 256 + 256], q_t[r:r + c.R, t, :],
                                          k_t[r:r + c.R, t, e * P:e * P + 2 * P], start=True, stop=True)
                mm.then_inc(S["scores_ready"], 1)

            def transpose_probs(g, p):
                pe.wait_ge(S["probs_ready"], g * c.NP + (p + 1))
                for i in range(4):
                    mm = nc.tensor.transpose(probs_t[p % 2][:, i * P:i * P + P], probs[p % 2][:, i * P:i * P + P],
                                             ident[:])
                mm.then_inc(S["pt_ready"], 1)

            def value_pair(g, e, p):
                by, k, per = evacuator(c, p)
                pe.wait_ge(S[by], g * per + (k + 1))
                for hh in range(2):
                    h = c.head(p, hh)
                    cols = slice(h * c.DH, h * c.DH + c.DH)
                    for blk, slot in ((0, (e - 1) % U), (1, e)):
                        i = 2 * hh + blk
                        mm = nc.tensor.matmul(heads_out[:, cols], pt[p % 2][:, i * P:i * P + P], v_tok[slot][:, cols],
                                              start=(blk == 0), stop=(blk == 1))
                mm.then_inc(S["pv_done"], 1)

            def output(g, more):
                pe.wait_ge(S["o_ready"], g + 1)
                if more[2] and c is ATT_B:
                    pe.wait_ge(S["v_copied"], g + 3)
                for k in range(c.KO):
                    mm = nc.tensor.transpose(work[0][:, k * P:k * P + P], o_tok[:, k * P:k * P + P], ident[:])
                mm.then_inc(S["ot_ready"], 1)

            def out_project(g):
                pe.wait_ge(S["o_hi"], g + 1)
                pe.wait_ge(S["o_lo"], g + 1)
                for k in range(c.KO):
                    mm = product3(work[0][:, 0:D], o_hi[:, k * P:k * P + P], o_lo[:, k * P:k * P + P],
                                  wo_hi[:, k, :], wo_lo[:, k, :], k == 0, k == c.KO - 1)
                mm.then_inc(S["wo_ready"], 1)

            def prologue(base):
                transpose_x(base, 0)
                pe.wait_ge(wa_split, 1 if layer is None else layer + 2)
                pe.wait_ge(wa_hi_done, 1 if layer is None else layer + 2)
                for part in range(3):
                    project(base, part)
                if c is ATT_A:
                    for part in range(4):
                        transpose_stack(base, part)
                else:
                    pe.wait_ge(S["q_squared"], base + 1)
                    transpose_x(base + 1, 1)
                    for part in range(3):
                        project(base + 1, part, base)
                    transpose_qk(base, base + 1)
                pe.wait_ge(S["phase_set"], 2 if layer is None else layer * 2 + 2)
                score_pair(base, 0, 0, True)
                score_pair(base, 0, 1, True)
                transpose_x(base + c.AHEAD, c.AHEAD)

            def step_a(g, e, j, g_local, more):
                for p in range(c.NP):
                    transpose_probs(g, p)
                    if p + 2 < c.NP:
                        score_pair(g, e, p + 2)
                    elif more[1]:
                        score_pair(g + 1, (e + 1) % U, p + 2 - c.NP)
                    if more[1]:
                        if p < 2:
                            project(g + 1, p)
                        elif p < 6:
                            transpose_stack(g + 1, p - 2)
                    if p == 0:
                        pe.wait_ge(S["v_copied"], g + 1)
                        if more[-1]:
                            value_pair(g - 1, (e - 1) % U, c.NP - 1)
                    else:
                        if p == 1 and more[-1]:
                            pe.wait_ge(S["o_ready"], g)
                        value_pair(g, e, p - 1)
                    if p == 2 and more[-1]:
                        output(g - 1, more)
                    if p == 4 and more[-1]:
                        out_project(g - 1)
                    if p == 6 and more[2]:
                        transpose_x(g + 2, (e + 2) % U)
                if not more[1]:
                    value_pair(g, e, c.NP - 1)
                    output(g, more)
                    out_project(g)

            def step(g, e, j, g_local, more):
                n = g + c.AHEAD
                for p in range(c.NP):
                    transpose_probs(g, p)
                    if p + 2 < c.NP:
                        score_pair(g, e, p + 2)
                    if more[2] and p < 3:
                        project(n, p)
                    if p == 0:
                        pe.wait_ge(S["v_copied"], g + 1)
                    else:
                        value_pair(g, e, p - 1)
                if more[1]:
                    transpose_qk(g + 1, n if more[2] else None)
                value_pair(g, e, c.NP - 1)
                if more[1]:
                    score_pair(g + 1, (e + 1) % U, 0)
                output(g, more)
                if more[1]:
                    score_pair(g + 1, (e + 1) % U, 1)
                if more[c.AHEAD + 1]:
                    transpose_x(n + 1, (e + c.AHEAD + 1) % U)
                out_project(g)

            attention_loop(pe, c, layer, prologue, step_a if c is ATT_A else step)

        def load_count(c, n, slot):
            per = 16 if c is ATT_A else 64
            return (n - slot) * (per // U) + per

        def evacuator(c, p):
            if c is ATT_A:
                return ("pt_dve", p // 2, 4) if p % 2 == 0 else ("pt_act", p // 2, 4)
            return ("pt_dve", 0, 1) if p == 0 else ("pt_act", p - 1, 3)

        def pe_mlp(pe, c, S, layer):
            w1_hi = wm_hi[:, 0:KD * c.IN].rearrange("p (k n) -> p k n", k=KD)
            w1_lo = wm_lo[:, 0:KD * c.IN].rearrange("p (k n) -> p k n", k=KD)
            w2_hi = wm_hi[:, KD * c.IN:c.WCOLS].rearrange("p (k n) -> p k n", k=c.NF)
            w2_lo = wm_lo[:, KD * c.IN:c.WCOLS].rearrange("p (k n) -> p k n", k=c.NF)
            h_banks, xt_banks, y_banks = bank[0:4], bank[4:6], bank[6:8]

            def transpose_z(t):
                pe.wait_ge(S["z_ready"], t + 1)
                for k in range(KD):
                    for i in range(4):
                        mm = nc.tensor.transpose(xt_banks[k][:, i * P:i * P + P], g_z[:, i, k * P:k * P + P], ident[:])
                mm.then_inc(S["xt_ready"], 1)

            def hidden(t, f):
                r = c.rows[f]
                if c.gated:
                    if f >= 2:
                        pe.wait_ge(S["hid_ready"], t * c.NF + (f - 1))
                    targets = [(h_banks[(2 * f) % 4], c.H + f * c.FT), (h_banks[(2 * f + 1) % 4], f * c.FT)]
                else:
                    if f >= 4:
                        pe.wait_ge(S["gate_ready"], t * c.NF + (f - 3))
                    targets = [(h_banks[f % 4], f * c.FT)]
                for out, c0 in targets:
                    for k in range(KD):
                        mm = product3(out[0:r, :], w1_hi[:, k, c0:c0 + r], w1_lo[:, k, c0:c0 + r],
                                      g_h_hi[:, k, :], g_h_lo[:, k, :], k == 0, k == KD - 1)
                    mm.then_inc(S["in_ready"], 1)

            def down(t, half):
                if half == 1:
                    pe.wait_ge(S["y_added"], t * 4 + 2)
                for f in range(c.NF):
                    r = c.rows[f]
                    if half == 0:
                        pe.wait_ge(S["u_hi"], t * c.NF + (f + 1))
                        if c.gated:
                            pe.wait_ge(S[["u_lo_dve", "u_lo_pool"][f % 2]], t * 3 + (f // 2 + 1))
                        else:
                            pe.wait_ge(S["u_lo_dve"], t * c.NF + (f + 1))
                    for i in range(2):
                        ch = 2 * half + i
                        mm = product3(y_banks[i][:, 0:D], u_hi[0:r, f, ch * P:ch * P + P], u_lo[0:r, f, ch * P:ch * P + P],
                                      w2_hi[0:r, f, :], w2_lo[0:r, f, :], f == 0, f == c.NF - 1)
                mm.then_inc(S["y_ready"], 1)

            def group(t, more):
                pe.wait_ge(S["h_hi"], t + 1)
                pe.wait_ge(S["h_lo"], t + 1)
                for f in range(c.NF):
                    hidden(t, f)
                if more:
                    transpose_z(t + 1)
                down(t, 0)
                down(t, 1)

            base = 0 if layer is None else pe.snap(layer * NGRP)
            transpose_z(base)
            pe.wait_ge(consts_loaded, 16)
            pe.wait_ge(wm_split, 1 if layer is None else layer + 2)
            pe.wait_ge(wm_hi_done, 1 if layer is None else layer + 2)
            with pe.Fori(0, NGRP - 1) as i:
                group(pe.snap(i + 0) if layer is None else pe.snap(layer * NGRP + i), True)
            group(base + (NGRP - 1), False)

        @block.tensor
        def _(pe):
            pe.wait_ge(consts_loaded, 16)
            pe_attention(pe, ATT_A, SA, None)
            pe_mlp(pe, MLP_A, MA, None)
            with pe.Fori(0, LAYERS) as layer:
                pe_attention(pe, ATT_B, SB, layer)
                pe_mlp(pe, MLP_B, MB, layer)

        def split_low(v, raw, hi, lo, cols, loaded, hi_done, done, layer):
            v.wait_ge(loaded, 16 if layer is None else layer * 16 + 32)
            v.wait_ge(hi_done, 1 if layer is None else layer + 2)
            nc.vector.tensor_tensor(lo[:, 0:cols], raw[:, 0:cols], hi[:, 0:cols].bitcast(F32),
                                    ALU.subtract).then_inc(done, 1)

        def dve_attention(v, c, S, layer):
            split_low(v, wa_raw, wa_hi, wa_lo, c.WCOLS, wa_loaded, wa_hi_done, wa_split, layer)

            def heads(ap, n=None):
                return ap.rearrange("p (h d) -> p h d", d=c.DH)

            def layer_norm_stats(m, slot):
                v.wait_ge(S[f"load{slot}"], load_count(c, m, slot))
                nc.vector.bn_stats(stats[:], x_in[:, slot, :]).then_inc(S["ln_stats"], 1)
                wait_apart(v, (S["ln_stats"], m + 1))
                nc.vector.bn_aggr(mean_var[:], stats[:]).then_inc(S["ln_aggr"], 1)
                v.wait_ge(S["ln_aggr"], m + 1)
                nc.vector.tensor_scalar_add(var_eps[:], mean_var[:, 1:2], EPS).then_inc(S["ln_var"], 1)

            def normalize(m, slot):
                v.wait_ge(S["ln_rstd"], m + 1)
                nc.vector.tensor_scalar(z[:], x_in[:, slot, :], mean_var[:, 0:1], rstd[:], ALU.subtract,
                                        ALU.mult).then_inc(S["z_ready"], 1)

            def h_transposed(m):
                v.wait_ge(S["xt_ready"], m + 1)
                if c is ATT_A:
                    for k in range(KD):
                        ins = nc.vector.tensor_scalar(h32[:, k * P:k * P + P], work[1][:, k * P:k * P + P],
                                                      vec_a[:, k:k + 1], vec_a[:, 2 + k:3 + k], ALU.mult, ALU.add)
                    ins.then_inc(S["h32_ready"], 1)
                else:
                    v.wait_ge(S["h_hi"], m + 1)
                    nc.vector.tensor_tensor(h_lo[:], work[1][:, 0:D], h_hi[:].bitcast(F32),
                                            ALU.subtract).then_inc(S["h_lo"], 1)

            def split_qk_low(n):
                v.wait_ge(S["k_hi"], n + 1)
                v.wait_ge(S["q_hi"], n + 1)
                q_src = work[1][:, 0:256].rearrange("p (h d) -> p h d", d=c.DH)
                k_src = work[1][:, 256:512].rearrange("p (h d) -> p h d", d=c.DH)
                nc.vector.scalar_tensor_tensor(q_stack[:, :, 2, :], q_src, c.DH ** -0.5, q_stack[:, :, 0, :].bitcast(F32),
                                               ALU.mult, ALU.subtract).then_inc(S["q_lo"], 1)
                nc.vector.tensor_tensor(k_stack[:, :, 1, :], k_src, k_stack[:, :, 0, :].bitcast(F32),
                                        ALU.subtract).then_inc(S["k_lo"], 1)

            def norms(n, i):
                v.wait_ge(S[["q_squared", "k_squared"][i]], n + 1)
                nc.vector.tensor_reduce(norm2[:, 8 * i:8 * i + 8], heads(squares[i][:]), AX.X,
                                        ALU.add).then_inc(S["norm2_part"], 1)
                if i == 1:
                    v.wait_ge(S["norm2_part"], 2 * n + 2)
                    nc.vector.tensor_scalar_max(norm2c[:], norm2[:], 1e-24).then_inc(S["norm2_ready"], 1)

            def rotate_q(n):
                v.wait_ge(S["rope_ready"], n + 1)
                v.wait_ge(S["q_copied"], n + 1)
                rotate(nc.vector, 0, S["q_parts"])
                v.wait_ge(S["q_parts"], 4 * n + 3)
                nc.vector.tensor_tensor(cos_part[0][:], cos_part[0][:], squares[0][:], ALU.add).then_inc(S["q_parts"], 1)

            def scale_rotated(n):
                for i, summed, done in ((0, "q_parts", "q_rot"), (1, "k_parts", "k_rot")):
                    v.wait_ge(S[summed], 4 * n + 4)
                    v.wait_ge(S["rnorm_ready"], n + 1)
                    r = rnorm[:, 8 * i:8 * i + 8].unsqueeze(2).to_broadcast([P, c.NH, c.DH])
                    nc.vector.tensor_tensor(heads(rot[i][:]), heads(cos_part[i][:]), r, ALU.mult).then_inc(S[done], 1)

            def copy_q_t(n, half=0):
                v.wait_ge(S["qt_ready"], n * c.TB + (half + 1))
                q_t = q_t_a if c is ATT_A else q_t_b
                nc.vector.tensor_copy(q_t[:, 4 * half:4 * half + 4, :].rearrange("p t q -> p (t q)"),
                                      work[1 + half][:]).then_inc(S["qt_copied"], 1)

            def mask_pair(g, e, p, it=None, first=False):
                waits = [(S["scores_ready"], g * c.NP + (p + 1))]
                if p >= 2 or not first:
                    waits.append((S["probs_ready"], g * c.NP + (p - 1)))
                if e == 0 and p == 0:
                    waits.append((S["mask0_ready"], it))
                wait_apart(v, *waits)
                for hh in range(2):
                    h = c.head(p, hh)
                    cols = slice(hh * 256, hh * 256 + 256)
                    ins = nc.vector.tensor_tensor_reduce(masked[p % 2][:, cols], scores[p % 2][:, cols],
                                                         (mask0 if e == 0 else mask)[:], -1.0, BIG, ALU.add, ALU.min,
                                                         neg_max[:, h:h + 1])
                ins.then_inc(S["masked_ready"], 1)

            def copy_probs(g, p):
                by, k, per = evacuator(c, p)
                if by != "pt_dve":
                    return
                v.wait_ge(S["pt_ready"], g * c.NP + (p + 1))
                if p >= 2:
                    v.wait_ge(S["pv_done"], g * c.NP + (p - 1))
                nc.vector.tensor_copy(pt[p % 2][:], probs_t[p % 2][:]).then_inc(S["pt_dve"], 1)

            def normalize_heads(g, e):
                v.wait_ge(S["pv_done"], g * c.NP + c.NP)
                nc.vector.reciprocal(inv_sum[:, 0:c.NH], row_sum[:, e % 2, 0:c.NH]).then_inc(S["inv_ready"], 1)
                v.wait_ge(S["inv_ready"], g + 1)
                r = inv_sum[:, 0:c.NH].unsqueeze(2).to_broadcast([P, c.NH, c.DH])
                nc.vector.tensor_tensor(heads(o_tok[:, 0:c.OC]), heads(heads_out[:, 0:c.OC]), r,
                                        ALU.mult).then_inc(S["o_ready"], 1)

            def split_o(g):
                v.wait_ge(S["ot_ready"], g + 1)
                v.wait_ge(S["o_hi"], g + 1)
                nc.vector.tensor_tensor(o_lo[:, 0:c.OC], work[0][:, 0:c.OC], o_hi[:, 0:c.OC].bitcast(F32),
                                        ALU.subtract).then_inc(S["o_lo"], 1)

            def add_residual(g, e):
                v.wait_ge(S["wo_ready"], g + 1)
                per = 16 if c is ATT_A else 32
                v.wait_ge(S[f"store{e % 2}"], (g - e % 2) * (per // 2) + per)
                res = x_in if c is ATT_A else x_res
                nc.vector.tensor_tensor(y_out[:, e % 2, :], work[0][:, 0:D], res[:, e, :], ALU.add).then_inc(S["y_ready"], 1)

            def make_mask0(j):
                src = mask0_prev[:, j, :] if isinstance(j, int) else \
                    mask0_prev[:, bass.ds(j, 1), :].rearrange("p a k -> p (a k)")
                nc.vector.tensor_copy(mask0[:, 0:P], src).then_inc(S["mask0_ready"], 1)

            def prologue(base):
                v.wait_ge(S["params"], 64 if layer is None else layer * 64 + 64)
                make_mask0(0)
                if c is ATT_A:
                    layer_norm_stats(base, 0)
                    normalize(base, 0)
                    h_transposed(base)
                    layer_norm_stats(base + 1, 1)
                    normalize(base + 1, 1)
                    split_qk_low(base)
                    copy_q_t(base, 0)
                    copy_q_t(base, 1)
                else:
                    h_transposed(base)
                    h_transposed(base + 1)
                    norms(base, 0)
                    norms(base, 1)
                    rotate_q(base)
                    scale_rotated(base)
                    norms(base + 1, 0)
                    norms(base + 1, 1)
                    rotate_q(base + 1)
                    copy_q_t(base)
                it = 1 if layer is None else layer * ITERS + 1
                mask_pair(base, 0, 0, it, True)
                mask_pair(base, 0, 1, None, True)
                h_transposed(base + c.AHEAD)

            def step_a(g, e, j, g_local, more):
                before, ms = (e - 1) % U, (e + 2) % U
                for p in range(c.NP):
                    copy_probs(g, p)
                    if p + 2 < c.NP:
                        mask_pair(g, e, p + 2)
                    elif more[1]:
                        it = None
                        if p == 6 and e == U - 1:
                            make_mask0(j + 1)
                            it = j + 2
                        mask_pair(g + 1, (e + 1) % U, p + 2 - c.NP, it)
                    if p == 0 and more[-1]:
                        normalize_heads(g - 1, before)
                    if p == 1 and more[1]:
                        split_qk_low(g + 1)
                    if p == 2 and more[2]:
                        layer_norm_stats(g + 2, ms)
                    if p == 3 and more[-1]:
                        split_o(g - 1)
                    if p == 4 and more[2]:
                        normalize(g + 2, ms)
                    if p == 5:
                        if more[1]:
                            copy_q_t(g + 1, 0)
                        if more[-1]:
                            add_residual(g - 1, before)
                    if p == 6:
                        if more[1]:
                            copy_q_t(g + 1, 1)
                        if more[2]:
                            h_transposed(g + 2)
                if not more[1]:
                    normalize_heads(g, e)
                    split_o(g)
                    add_residual(g, e)

            def step(g, e, j, g_local, more):
                n, m, ms = g + c.AHEAD, g + c.AHEAD + 1, (e + c.AHEAD + 1) % U
                for p in range(c.NP):
                    copy_probs(g, p)
                    if p + 2 < c.NP:
                        mask_pair(g, e, p + 2)
                    if p == 0 and more[1]:
                        scale_rotated(g + 1)
                    if p == 1 and more[2]:
                        norms(n, 0)
                    if p == 2 and more[2]:
                        norms(n, 1)
                        rotate_q(n)
                    if p == 3 and more[1]:
                        copy_q_t(g + 1)
                it = None
                if e == U - 1 and more[1]:
                    make_mask0(j + 1)
                    it = layer * ITERS + (j + 2)
                normalize_heads(g, e)
                if more[1]:
                    mask_pair(g + 1, (e + 1) % U, 0, it)
                split_o(g)
                if more[1]:
                    mask_pair(g + 1, (e + 1) % U, 1)
                if more[c.AHEAD + 1]:
                    h_transposed(m)
                add_residual(g, e)

            attention_loop(v, c, layer, prologue, step_a if c is ATT_A else step)

        def rotate(engine, i, done):
            x = qk[i][:].rearrange("p (h d) -> p h d", d=64)
            half = 32
            def table(a, lo, hi):
                return rope[:, a, lo:hi].unsqueeze(1).to_broadcast([P, 8, hi - lo])
            engine.tensor_tensor(cos_part[i][:].rearrange("p (h d) -> p h d", d=64), x, table(2 * i, 0, 64),
                                 ALU.mult).then_inc(done, 1)
            s = squares[i][:].rearrange("p (h d) -> p h d", d=64)
            engine.tensor_tensor(s[:, :, 0:half], x[:, :, half:64], table(2 * i + 1, 0, half), ALU.mult).then_inc(done, 1)
            engine.tensor_tensor(s[:, :, half:64], x[:, :, 0:half], table(2 * i + 1, half, 64), ALU.mult).then_inc(done, 1)

        def m_load_count(c, t, slot):
            per = 32 if c is MLP_A else 64
            return (t - slot) * (per // 2) + per

        def dve_mlp(v, c, S, layer):
            split_low(v, wm_raw, wm_hi, wm_lo, c.WCOLS, wm_loaded, wm_hi_done, wm_split, layer)
            vec = vec_a if c is MLP_A else vec_b
            g0c = 4 if c is MLP_A else 0

            def norm_stats(t, slot):
                v.wait_ge(S[f"load{slot}"], m_load_count(c, t, slot))
                for i in range(4):
                    ins = nc.vector.bn_stats(g_stats[:, i, :], g_in[slot][:, i, :])
                ins.then_inc(S["stats"], 1)
                wait_apart(v, (S["stats"], t + 1))
                for i in range(4):
                    ins = nc.vector.bn_aggr(g_mv[:, i, :], g_stats[:, i, :])
                ins.then_inc(S["aggr"], 1)
                v.wait_ge(S["aggr"], t + 1)
                nc.vector.tensor_scalar_add(g_ve[:], g_mv[:, :, 1], EPS).then_inc(S["var"], 1)

            def normalize(t, slot):
                v.wait_ge(S["rstd"], t + 1)
                for i in range(4):
                    ins = nc.vector.tensor_scalar(g_z[:, i, :], g_in[slot][:, i, :], g_mv[:, i, 0:1],
                                                  g_rstd[:, i:i + 1], ALU.subtract, ALU.mult)
                ins.then_inc(S["z_ready"], 1)

            def gain_bias(t):
                v.wait_ge(S["xt_ready"], t + 1)
                for k in range(KD):
                    nc.vector.tensor_scalar(g_h32[:, k, :], bank[4 + k][:], vec[:, g0c + k:g0c + k + 1],
                                            vec[:, g0c + 2 + k:g0c + 3 + k], ALU.mult, ALU.add).then_inc(S["h32_ready"], 1)

            def value(t, f):
                r = c.rows[f]
                v.wait_ge(S["in_ready"], t * (2 * c.NF) + (2 * f + 2))
                v.wait_ge(S["gate_ready"], t * c.NF + (f + 1))
                if f >= 2:
                    v.wait_ge(S["u_hi"], t * c.NF + (f - 1))
                    v.wait_ge(S[["u_lo_dve", "u_lo_pool"][f % 2]], t * 3 + (f // 2))
                nc.vector.scalar_tensor_tensor(hid[f % 2][0:r, :], bank[(2 * f + 1) % 4][0:r, :], vec[0:r, 4 + f:5 + f],
                                               gate[f % 2][0:r, :], ALU.add, ALU.mult).then_inc(S["hid_ready"], 1)

            def low(t, f):
                r = c.rows[f]
                src = hid if c.gated else gate
                v.wait_ge(S["u_hi"], t * c.NF + (f + 1))
                if c.gated:
                    v.wait_ge(S["hid_ready"], t * c.NF + (f + 1))
                nc.vector.tensor_tensor(u_lo[0:r, f, :], src[f % 2][0:r, :], u_hi[0:r, f, :].bitcast(F32),
                                        ALU.subtract).then_inc(S["u_lo_dve"], 1)

            def group(t, slot, more):
                if more:
                    norm_stats(t + 1, 1 - slot)
                if c.gated:
                    for f in range(c.NF):
                        value(t, f)
                        if f % 2 == 0:
                            low(t, f)
                        if f == 2 and more:
                            normalize(t + 1, 1 - slot)
                else:
                    for f in range(c.NF):
                        low(t, f)
                        if f == 4 and more:
                            normalize(t + 1, 1 - slot)
                if more:
                    gain_bias(t + 1)
                v.wait_ge(S["res_ready"], t + 1)
                n = 32 if c is MLP_A else 48
                v.wait_ge(S["store"], t * n + n)
                for i in range(4):
                    if i % 2 == 0:
                        v.wait_ge(S["y_ready"], t * 2 + (i // 2 + 1))
                    nc.vector.tensor_tensor(g_new[:, i, :], bank[6 + i % 2][:, 0:D], g_sum[:, i, :],
                                            ALU.add).then_inc(S["y_added"], 1)
                v.wait_ge(S["y_added"], t * 4 + 4)
                nc.vector.tensor_tensor(g_sum[:], g_new[:], g_old[slot][:], ALU.add).then_inc(S["f_sum"], 1)
                v.wait_ge(S["f_sum"], t + 1)
                for i in range(4):
                    ins = nc.vector.bn_stats(f_stats[:, i, :], g_sum[:, i, :])
                ins.then_inc(S["f_stats"], 1)
                wait_apart(v, (S["f_stats"], t + 1))
                for i in range(4):
                    ins = nc.vector.bn_aggr(f_mv[:, i, :], f_stats[:, i, :])
                ins.then_inc(S["f_aggr"], 1)
                v.wait_ge(S["f_aggr"], t + 1)
                nc.vector.tensor_scalar_add(f_ve[:], f_mv[:, :, 1], EPS).then_inc(S["f_var"], 1)

            base = 0 if layer is None else v.snap(layer * NGRP)
            v.wait_ge(S["params"], 16 if layer is None else layer * 32 + 32)
            norm_stats(base, 0)
            normalize(base, 0)
            gain_bias(base)
            with v.Fori(0, NGRP // 2 - 1) as i:
                t0 = v.snap(i * 2) if layer is None else v.snap(layer * NGRP + i * 2)
                for e in range(2):
                    group(t0 + e, e, True)
            group(base + (NGRP - 2), 0, True)
            group(base + (NGRP - 1), 1, False)

        @block.vector
        def _(v):
            nc.vector.memset(zero_row[:], 0.0)
            nc.vector.memset(minus_half[:], -0.5).then_inc(consts_set, 1)
            dve_attention(v, ATT_A, SA, None)
            dve_mlp(v, MLP_A, MA, None)
            with v.Fori(0, LAYERS) as layer:
                dve_attention(v, ATT_B, SB, layer)
                dve_mlp(v, MLP_B, MB, layer)

        def split_high(a, raw, hi, cols, loaded, done, layer):
            a.wait_ge(loaded, 16 if layer is None else layer * 16 + 32)
            nc.scalar.activation(hi[:, 0:cols], raw[:, 0:cols], ACT.Copy).then_inc(done, 1)

        def act_attention(a, c, S, layer):
            k_t = k_t_a if c is ATT_A else k_t_b
            split_high(a, wa_raw, wa_hi, c.WCOLS, wa_loaded, wa_hi_done, layer)

            def h_high(m):
                if c is ATT_A:
                    a.wait_ge(S["h32_ready"], m + 1)
                    nc.scalar.activation(h_hi[:], h32[:], ACT.Copy).then_inc(S["h_hi"], 1)
                else:
                    a.wait_ge(S["xt_ready"], m + 1)
                    nc.scalar.activation(h_hi[:], work[1][:, 0:D], ACT.Copy).then_inc(S["h_hi"], 1)

            def copy_qkv(n, slot, part, steady=True):
                if c is ATT_A:
                    if part == 0:
                        a.wait_ge(S["q_proj"], n + 1)
                        for i, scale, out, done in ((0, c.DH ** -0.5, q_stack[:, :, 0:2, :], "q_hi"),
                                                    (1, 1.0, k_stack[:, :, 0:3:2, :], "k_hi")):
                            src = work[1][:, i * 256:i * 256 + 256].rearrange("p (h d) -> p h d", d=c.DH)
                            nc.scalar.activation(out, src.unsqueeze(2).to_broadcast([P, c.NH, 2, c.DH]), ACT.Copy,
                                                 scale=scale).then_inc(S[done], 1)
                    elif part == 1:
                        a.wait_ge(S["v_proj"], n + 1)
                        nc.scalar.activation(v_tok[slot][:, 0:c.OC], work[2][:, 0:c.OC], ACT.Copy).then_inc(S["v_copied"], 1)
                    return
                if part < 2:
                    if steady:
                        a.wait_ge(S[["q_parts", "k_parts"][part]], 4 * n)
                    proj, copied, squared = (("q_proj", "q_copied", "q_squared"), ("k_proj", "k_copied", "k_squared"))[part]
                    a.wait_ge(S[proj], n + 1)
                    nc.scalar.activation(qk[part][:], work[1 + part][:], ACT.Copy).then_inc(S[copied], 1)
                    nc.scalar.activation(squares[part][:], work[1 + part][:], ACT.Square).then_inc(S[squared], 1)
                else:
                    a.wait_ge(S["v_proj"], n + 1)
                    nc.scalar.activation(v_tok[slot][:], work[0][:], ACT.Copy).then_inc(S["v_copied"], 1)

            def copy_k_t(n, slot, half=0):
                a.wait_ge(S["kt_ready"], n * c.TB + (half + 1))
                src = work[(1 + half) if c is ATT_A else 2][:].rearrange("p (t q) -> p t q", q=P)
                rows = slice(4 * half, 4 * half + 4)
                if slot == U - 1:
                    nc.scalar.activation(k_t[:, rows, 0:P], src, ACT.Copy)
                nc.scalar.activation(k_t[:, rows, (slot + 1) * P:(slot + 2) * P], src, ACT.Copy).then_inc(S["kt_copied"], 1)

            def exponentials(g, e, p, first=False):
                a.wait_ge(S["masked_ready"], g * c.NP + (p + 1))
                if p >= 2 or not first:
                    a.wait_ge(S["pt_ready"], g * c.NP + (p - 1))
                for hh in range(2):
                    h = c.head(p, hh)
                    cols = slice(hh * 256, hh * 256 + 256)
                    ins = nc.scalar.activation(probs[p % 2][:, cols], masked[p % 2][:, cols], ACT.Exp,
                                               bias=neg_max[:, h:h + 1], scale=-1.0, accum_out=row_sum[:, e % 2, h:h + 1])
                ins.then_inc(S["probs_ready"], 1)

            def copy_probs(g, p):
                by, k, per = evacuator(c, p)
                if by != "pt_act":
                    return
                a.wait_ge(S["pt_ready"], g * c.NP + (p + 1))
                if p >= 2:
                    a.wait_ge(S["pv_done"], g * c.NP + (p - 1))
                nc.scalar.activation(pt[p % 2][:], probs_t[p % 2][:], ACT.Copy).then_inc(S["pt_act"], 1)

            def o_high(g):
                a.wait_ge(S["ot_ready"], g + 1)
                nc.scalar.activation(o_hi[:, 0:c.OC], work[0][:, 0:c.OC], ACT.Copy).then_inc(S["o_hi"], 1)

            def prologue(base):
                h_high(base)
                a.wait_ge(S["phase_set"], 2 if layer is None else layer * 2 + 2)
                if c is ATT_A:
                    nc.scalar.activation(k_t[:, :, 0:P], zero_row[:, 0:1, :].to_broadcast([P, c.NT, P]), ACT.Copy)
                for part in range(3):
                    copy_qkv(base, 0, part, False)
                if c is ATT_B:
                    h_high(base + 1)
                    for part in range(3):
                        copy_qkv(base + 1, 1, part)
                for half in range(c.TB):
                    copy_k_t(base, 0, half)
                exponentials(base, 0, 0, True)
                if c is ATT_B:
                    h_high(base + 2)
                exponentials(base, 0, 1, True)
                if c is ATT_A:
                    h_high(base + 1)

            def step_a(g, e, j, g_local, more):
                ns = (e + 1) % U
                for p in range(c.NP):
                    copy_probs(g, p)
                    if p + 2 < c.NP:
                        exponentials(g, e, p + 2)
                    elif more[1]:
                        exponentials(g + 1, ns, p + 2 - c.NP)
                    if more[1]:
                        if p < 2:
                            copy_qkv(g + 1, ns, p)
                        elif p < 4:
                            copy_k_t(g + 1, ns, p - 2)
                    if p == 2 and more[-1]:
                        o_high(g - 1)
                    if p == 6 and more[2]:
                        h_high(g + 2)
                if not more[1]:
                    o_high(g)

            def step(g, e, j, g_local, more):
                n, ns = g + 2, (e + 2) % U
                for p in range(c.NP):
                    copy_probs(g, p)
                    if p + 2 < c.NP:
                        exponentials(g, e, p + 2)
                    if more[2] and p < 3:
                        copy_qkv(n, ns, p)
                if more[1]:
                    copy_k_t(g + 1, (e + 1) % U)
                o_high(g)
                if more[1]:
                    exponentials(g + 1, e + 1, 0)
                if more[3]:
                    h_high(g + 3)
                if more[1]:
                    exponentials(g + 1, e + 1, 1)

            attention_loop(a, c, layer, prologue, step_a if c is ATT_A else step)

        def act_mlp(a, c, S, layer):
            split_high(a, wm_raw, wm_hi, c.WCOLS, wm_loaded, wm_hi_done, layer)
            vec, b0 = (vec_a, 8) if c is MLP_A else (vec_b, 10)

            def h_high(t):
                a.wait_ge(S["h32_ready"], t * KD + KD)
                nc.scalar.activation(g_h_hi[:], g_h32[:], ACT.Copy).then_inc(S["h_hi"], 1)

            def gates(t, f):
                r = c.rows[f]
                if c.gated:
                    a.wait_ge(S["in_ready"], t * (2 * c.NF) + (2 * f + 1))
                    if f >= 2:
                        a.wait_ge(S["hid_ready"], t * c.NF + (f - 1))
                    src = bank[(2 * f) % 4]
                else:
                    a.wait_ge(S["in_ready"], t * c.NF + (f + 1))
                    if f >= 2:
                        a.wait_ge(S["u_lo_dve"], t * c.NF + (f - 1))
                    src = bank[f % 4]
                nc.scalar.activation(gate[f % 2][0:r, :], src[0:r, :], ACT.Gelu,
                                     bias=vec[0:r, b0 + f:b0 + f + 1]).then_inc(S["gate_ready"], 1)

            def high(t, f):
                r = c.rows[f]
                src = hid if c.gated else gate
                a.wait_ge(S["hid_ready"] if c.gated else S["gate_ready"], t * c.NF + (f + 1))
                if f == 0:
                    pass
                nc.scalar.activation(u_hi[0:r, f, :], src[f % 2][0:r, :], ACT.Copy).then_inc(S["u_hi"], 1)

            def group(t, more):
                gates(t, 0)
                for f in range(c.NF):
                    if f + 1 < c.NF:
                        gates(t, f + 1)
                    high(t, f)
                if more:
                    h_high(t + 1)

            base = 0 if layer is None else a.snap(layer * NGRP)
            h_high(base)
            with a.Fori(0, NGRP - 1) as i:
                group(a.snap(i + 0) if layer is None else a.snap(layer * NGRP + i), True)
            group(base + (NGRP - 1), False)

        @block.scalar
        def _(a):
            act_attention(a, ATT_A, SA, None)
            act_mlp(a, MLP_A, MA, None)
            with a.Fori(0, LAYERS) as layer:
                act_attention(a, ATT_B, SB, layer)
                act_mlp(a, MLP_B, MB, layer)

        def pool_attention(pool, c, S, layer):
            def set_start(base):
                wait_apart(pool, (S["load0"], 16 if layer is None else layer * (64 * ITERS) + 64))
                if c is ATT_B:
                    nc.gpsimd.memset(k_t_b[:, :, 0:P], 0.0).then_inc(S["phase_set"], 1)
                else:
                    nc.gpsimd.memset(q_stack[:].rearrange("p h s d -> p (h s d)").bitcast(F32), 0.0)
                    nc.gpsimd.memset(k_stack[:].rearrange("p h s d -> p (h s d)").bitcast(F32), 0.0).then_inc(
                        S["phase_set"], 1)
                nc.gpsimd.memset(v_tok[U - 1][:], 0.0).then_inc(S["phase_set"], 1)

            def inverse_std(m):
                pool.wait_ge(S["ln_var"], m + 1)
                nc.gpsimd.tensor_tensor(rstd[:], var_eps[:], minus_half[:, 0:1], ALU.pow).then_inc(S["ln_rstd"], 1)

            def h_low(m):
                pool.wait_ge(S["h_hi"], m + 1)
                nc.gpsimd.tensor_tensor(h_lo[:], h32[:], h_hi[:].bitcast(F32), ALU.subtract).then_inc(S["h_lo"], 1)

            def tables(n, slot, steady):
                pool.wait_ge(S[f"load{slot}"], load_count(c, n, slot))
                if steady:
                    pool.wait_ge(S["q_parts"], 4 * n)
                    pool.wait_ge(S["k_parts"], 4 * n)
                nc.gpsimd.tensor_tensor(rope[:].rearrange("p a d -> p (a d)"), rope_in[:, slot, :],
                                        rope_scale[:].rearrange("p a d -> p (a d)"), ALU.mult).then_inc(S["rope_ready"], 1)

            def rotate_k(n, steady):
                if steady:
                    pool.wait_ge(S["k_rot"], n)
                pool.wait_ge(S["rope_ready"], n + 1)
                pool.wait_ge(S["k_squared"], n + 1)
                pool.wait_ge(S["norm2_part"], 2 * n + 2)
                rotate(nc.gpsimd, 1, S["k_parts"])
                pool.wait_ge(S["norm2_ready"], n + 1)
                nc.gpsimd.tensor_tensor(rnorm[:], norm2c[:], minus_half[:], ALU.pow).then_inc(S["rnorm_ready"], 1)
                pool.wait_ge(S["k_parts"], 4 * n + 3)
                nc.gpsimd.tensor_tensor(cos_part[1][:], cos_part[1][:], squares[1][:], ALU.add).then_inc(S["k_parts"], 1)

            def prologue(base):
                set_start(base)
                if c is ATT_A:
                    inverse_std(base)
                    inverse_std(base + 1)
                    h_low(base)
                    h_low(base + 1)
                else:
                    pool.wait_ge(S["params"], layer * 64 + 64)
                    tables(base, 0, False)
                    rotate_k(base, False)
                    tables(base + 1, 1, True)
                    rotate_k(base + 1, True)

            def step(g, e, j, g_local, more):
                if c is ATT_A:
                    if more[2]:
                        inverse_std(g + 2)
                        h_low(g + 2)
                elif more[2]:
                    tables(g + 2, (e + 2) % U, True)
                    rotate_k(g + 2, True)

            attention_loop(pool, c, layer, prologue, step)

        def pool_mlp(pool, c, S, layer):
            def inverse_std(t):
                pool.wait_ge(S["var"], t + 1)
                nc.gpsimd.tensor_tensor(g_rstd[:], g_ve[:], minus_half[:, 0:4], ALU.pow).then_inc(S["rstd"], 1)

            def h_low(t):
                pool.wait_ge(S["h_hi"], t + 1)
                nc.gpsimd.tensor_tensor(g_h_lo[:], g_h32[:], g_h_hi[:].bitcast(F32), ALU.subtract).then_inc(S["h_lo"], 1)

            def residual(t, slot, steady):
                pool.wait_ge(S[f"load{slot}"], m_load_count(c, t, slot))
                if steady:
                    pool.wait_ge(S["fin_ready"], t)
                src = g_in if c is MLP_A else g_mid
                b = row_b2[:].unsqueeze(1).to_broadcast([P, 4, D])
                nc.gpsimd.tensor_tensor(g_sum[:], src[slot][:], b, ALU.add).then_inc(S["res_ready"], 1)

            def low(t, f):
                r = c.rows[f]
                pool.wait_ge(S["u_hi"], t * c.NF + (f + 1))
                nc.gpsimd.tensor_tensor(u_lo[0:r, f, :], hid[f % 2][0:r, :], u_hi[0:r, f, :].bitcast(F32),
                                        ALU.subtract).then_inc(S["u_lo_pool"], 1)

            def finish(t):
                pool.wait_ge(S["f_var"], t + 1)
                nc.gpsimd.tensor_tensor(f_rstd[:], f_ve[:], minus_half[:, 0:4], ALU.pow).then_inc(S["f_rstd"], 1)
                wait_apart(pool, (S["f_rstd"], t + 1))
                for i in range(4):
                    ins = nc.gpsimd.tensor_scalar(g_fin[:, i, :], g_sum[:, i, :], f_mv[:, i, 0:1], f_rstd[:, i:i + 1],
                                                  ALU.subtract, ALU.mult)
                ins.then_inc(S["fin_ready"], 1)

            def group(t, slot, more, steady=True):
                residual(t, slot, steady)
                if more:
                    inverse_std(t + 1)
                if c.gated:
                    for f in range(1, c.NF, 2):
                        low(t, f)
                if more:
                    h_low(t + 1)
                finish(t)

            base = 0 if layer is None else pool.snap(layer * NGRP)
            pool.wait_ge(S["params"], 16 if layer is None else layer * 32 + 32)
            inverse_std(base)
            h_low(base)
            group(base, 0, True, False)
            with pool.Fori(0, NGRP // 2 - 1) as i:
                t0 = pool.snap(i * 2 + 1) if layer is None else pool.snap(layer * NGRP + i * 2 + 1)
                for e in range(2):
                    group(t0 + e, 1 - e, True)
            group(base + (NGRP - 1), 1, False)

        @block.gpsimd
        def _(pool):
            pool_attention(pool, ATT_A, SA, None)
            pool_mlp(pool, MLP_A, MA, None)
            with pool.Fori(0, LAYERS) as layer:
                pool_attention(pool, ATT_B, SB, layer)
                pool_mlp(pool, MLP_B, MB, layer)


def contraction_tiles(w, tile=P):
    k, n = w.shape
    tiles = -(-k // tile)
    out = np.zeros((P, tiles, n), np.float32)
    for i in range(tiles):
        part = w[i * tile:(i + 1) * tile]
        out[:part.shape[0], i] = part
    return out.reshape(P, tiles * n)


def columns(*vectors_and_tiles):
    cols = []
    for vec, tile in vectors_and_tiles:
        for i in range(0, len(vec), tile):
            col = np.zeros(P, np.float32)
            col[:len(vec[i:i + tile])] = vec[i:i + tile]
            cols.append(col)
    out = np.zeros((P, 16), np.float32)
    out[:, :len(cols)] = np.stack(cols, 1)
    return out


def window_masks(first_key):
    q, k = np.arange(P)[:, None], np.arange(2 * P)[None, :]
    full = np.where((k >= q + first_key) & (k <= q + P), 0.0, MASKED).astype(np.float32)
    first = np.repeat(full[:, None, :P], ITERS, 1)
    first[:, ::ITERS // B] = MASKED
    return full, np.ascontiguousarray(first)


def rope_tables():
    dim, window, qk_scale = ATT_B.DH, P, 8.0
    half = np.arange(0, dim, 2, dtype=np.float32)
    inv_freq = (np.float32(1.0) / np.float32(10000.0) ** (half / np.float32(dim))).astype(np.float32)
    t = np.arange(SEQ, dtype=np.float32)
    freqs = t[:, None] * inv_freq[None, :]
    cos, sin = np.cos(freqs), np.sin(freqs)
    base = ((half + np.float32(0.4 * dim)) / np.float32(1.4 * dim)).astype(np.float32)
    power = ((t - SEQ // 2) / np.float32(window // 2)).astype(np.float32)
    scale = np.power(base[None, :], power[:, None]).astype(np.float32)
    parts = []
    for s in (scale * np.float32(qk_scale), np.float32(1.0) / scale):
        parts += [np.concatenate([cos * s, cos * s], 1), np.concatenate([-sin * s, sin * s], 1)]
    return np.tile(np.concatenate(parts, 1).astype(np.float32), (B, 1))


def kernel(L0_attn_x, L0_attn_w_qkv, L0_attn_w_o, L0_attn_ln1_g, L0_attn_ln1_b, L0_attn_ln2_g, L0_attn_ln2_b,
           L0_attn_mlp_w1, L0_attn_mlp_b1, L0_attn_mlp_w2, L0_attn_mlp_b2, L0_ffn_wqkv, L0_ffn_q_scale,
           L0_ffn_k_scale, L0_ffn_wo, L0_ffn_ln_g, L0_ffn_ln_b, L0_ffn_w1, L0_ffn_b1, L0_ffn_w2, L0_ffn_b2):
    import concourse.bacc as bacc
    from concourse.bass_utils import run_bass_kernel_spmd

    a = [np.asarray(t) for t in (L0_attn_x, L0_attn_w_qkv, L0_attn_w_o, L0_attn_mlp_w1, L0_attn_mlp_w2)]
    x, w_qkv, w_o, w1, w2 = a
    wqkv_b, wo_b, w1_b, w2_b = (np.asarray(t) for t in (L0_ffn_wqkv, L0_ffn_wo, L0_ffn_w1, L0_ffn_w2))
    qs, ks = np.asarray(L0_ffn_q_scale), np.asarray(L0_ffn_k_scale)
    lg, lb, b1, b2 = (np.asarray(t) for t in (L0_ffn_ln_g, L0_ffn_ln_b, L0_ffn_b1, L0_ffn_b2))
    mask_a, mask_a0 = window_masks(1)
    mask_b, mask_b0 = window_masks(0)

    def swap(s):
        return np.concatenate([s[ATT_B.DH // 2:], s[:ATT_B.DH // 2]])

    H = MLP_B.H
    data = {
        "x": x.reshape(TOK, D),
        "w_att_a": np.concatenate([contraction_tiles(w_qkv.T), contraction_tiles(w_o.T)], 1),
        "w_mlp_a": np.concatenate([contraction_tiles(w1.T), contraction_tiles(w2.T)], 1),
        "w_att_b": np.concatenate([np.concatenate([contraction_tiles(wqkv_b[l]), contraction_tiles(wo_b[l])], 1)
                                   for l in range(LAYERS)], 0),
        "w_mlp_b": np.concatenate([np.concatenate([contraction_tiles(w1_b[l]), contraction_tiles(w2_b[l], MLP_B.FT)], 1)
                                   for l in range(LAYERS)], 0),
        "vec_a": columns((np.asarray(L0_attn_ln1_g), P), (np.asarray(L0_attn_ln1_b), P), (np.asarray(L0_attn_ln2_g), P),
                         (np.asarray(L0_attn_ln2_b), P), (np.asarray(L0_attn_mlp_b1), P)),
        "vec_b": np.concatenate([columns((lg[l], P), (lb[l], P), (b1[l][:H], MLP_B.FT), (b1[l][H:], MLP_B.FT))
                                 for l in range(LAYERS)], 0),
        "b2_a": np.broadcast_to(np.asarray(L0_attn_mlp_b2), (P, D)),
        "b2_b": np.concatenate([np.broadcast_to(b2[l], (P, D)) for l in range(LAYERS)], 0),
        "rope": rope_tables(),
        "rope_scale": np.concatenate([np.broadcast_to(np.concatenate([qs[l], swap(qs[l]), ks[l], swap(ks[l])]), (P, D))
                                      for l in range(LAYERS)], 0),
        "mask_a": mask_a, "mask_a0": mask_a0, "mask_b": mask_b, "mask_b0": mask_b0,
        "ident": np.eye(P, dtype=np.float32),
    }
    nc = bacc.Bacc("TRN2", target_bir_lowering=False, num_devices=1)
    arrays, io = {}, {}
    for name, arr in data.items():
        arrays[f"in_{name}"] = np.ascontiguousarray(arr)
        io[name] = nc.dram_tensor(f"in_{name}", arrays[f"in_{name}"].shape, F32, kind="ExternalInput").ap()
    io["out"] = nc.dram_tensor("out_x", (TOK, D), F32, kind="ExternalOutput").ap()
    build(nc, io)
    r = run_bass_kernel_spmd(nc, [arrays], core_ids=[0])
    return r.results[0]["out_x"].reshape(B, SEQ, D)
```

```python
from contextlib import ExitStack

import concourse.bass as bass
import numpy as np
from concourse import mybir

F32 = mybir.dt.float32
F32R = mybir.dt.float32r
ALU = mybir.AluOpType
ACT = mybir.ActivationFunctionType
AX = mybir.AxisListType

P = 128
B, SEQ, D = 2, 2048, 256
TOK = B * SEQ
NCH = TOK // P
U = 4
ITERS = NCH // U
KD = D // P
GT = 4 * P
NGRP = TOK // GT
LAYERS = 2
EPS = 1e-5
RING = 4
SPLIT = 8
MASKED = -1.0e30
BIG = 3.0e38


class Attention:

    def __init__(self, heads, dim, rows, row_step, ahead):
        self.NH, self.DH = heads, dim
        self.NP = heads // 2
        self.R = rows
        self.RS = row_step
        self.HPT = P // row_step
        self.NT = heads // self.HPT
        self.OC = heads * dim
        self.KO = self.OC // P
        self.QKV = 3 * self.OC
        self.WCOLS = KD * self.QKV + self.KO * D
        self.TB = self.NT // 4
        self.AHEAD = ahead

    def head(self, p, i):
        row, tiles = p % self.HPT, 2 * (p // self.HPT)
        return (tiles + i) * self.HPT + row


ATT_A = Attention(heads=16, dim=16, rows=48, row_step=64, ahead=1)
ATT_B = Attention(heads=8, dim=64, rows=64, row_step=64, ahead=2)


class Mlp:

    def __init__(self, hidden, tile, gated):
        self.H, self.FT, self.gated = hidden, tile, gated
        self.NF = -(-hidden // tile)
        self.rows = [min(tile, hidden - tile * f) for f in range(self.NF)]
        self.IN = hidden * (2 if gated else 1)
        self.WCOLS = KD * self.IN + self.NF * D


MLP_A = Mlp(4 * D, P, False)
MLP_B = Mlp(int(D * 4 * 2 / 3), 114, True)
WA = max(ATT_A.WCOLS, ATT_B.WCOLS)
WM = max(MLP_A.WCOLS, MLP_B.WCOLS)


def build(nc, io):
    x_state = nc.dram_tensor("x_state", ((LAYERS + 1) * TOK, D), F32, kind="Internal").ap()
    x_state_sh = nc.dram_tensor("x_state_sh", ((LAYERS + 1) * (TOK + P), P), F32, kind="Internal").ap()
    x_mid = nc.dram_tensor("x_mid", (TOK, D), F32, kind="Internal").ap()
    x_mid_sh = nc.dram_tensor("x_mid_sh", (TOK + P, P), F32, kind="Internal").ap()

    ctx = ExitStack()
    with ctx:
        def sbuf(name, shape, dt=F32, at=ctx):
            return at.enter_context(nc.sbuf_tensor(name, shape, dt))

        def sem(name):
            return ctx.enter_context(nc.semaphore(name))

        bank = [ctx.enter_context(nc.psum_tensor(f"bank{i}", [P, 512], F32)) for i in range(8)]
        work = bank[0:3]
        scores = bank[3:5]
        probs_t = bank[5:7]
        heads_out = bank[7]

        w_raw = sbuf("w_raw", [P, max(WA, WM)])
        wa_hi, wa_lo = sbuf("wa_hi", [P, WA], F32R), sbuf("wa_lo", [P, WA], F32R)
        wm_hi, wm_lo = sbuf("wm_hi", [P, WM], F32R), sbuf("wm_lo", [P, WM], F32R)
        ident = sbuf("ident", [P, P])
        zero_row = sbuf("zero_row", [P, 2, P])
        minus_half = sbuf("minus_half", [P, 16])
        vec_a = sbuf("vec_a", [P, 16])
        vec_b = sbuf("vec_b", [P, 16])
        row_b2 = sbuf("row_b2", [P, D])

        g_in = [sbuf(f"g_in{i}", [P, 4, 3, P]) for i in range(2)]
        g_z = sbuf("g_z", [P, 4, D])
        g_stats = sbuf("g_stats", [P, 4, 6])
        g_mv = sbuf("g_mv", [P, 4, 2])
        g_ve = sbuf("g_ve", [P, 4])
        g_rstd = sbuf("g_rstd", [P, 4])
        g_h32 = sbuf("g_h32", [P, KD, GT])
        g_h_hi, g_h_lo = sbuf("g_h_hi", [P, KD, GT], F32R), sbuf("g_h_lo", [P, KD, GT], F32R)

        y_out = sbuf("y_out", [P, 2, D])

        x_in = sbuf("x_in", [P, U, 3, P])
        h_hi, h_lo = sbuf("h_hi", [P, D], F32R), sbuf("h_lo", [P, D], F32R)
        mask = sbuf("mask", [P, 2 * P])
        mask0 = sbuf("mask0", [P, 2 * P])
        mask0_prev = sbuf("mask0_prev", [P, ITERS, P])
        rope_in = sbuf("rope_in", [P, U, D])
        rope_scale = sbuf("rope_scale", [P, 4, 64])

        at_ctx = ExitStack()
        v_tok = [sbuf(f"v_tok{i}", [P, 512], at=at_ctx) for i in range(U)]
        masked = [sbuf(f"masked{i}", [P, 512], at=at_ctx) for i in range(2)]
        probs = [sbuf(f"probs{i}", [P, 512], at=at_ctx) for i in range(2)]
        pt = [sbuf(f"pt{i}", [P, 512], at=at_ctx) for i in range(2)]
        neg_max = sbuf("neg_max", [P, 16], at=at_ctx)
        row_sum = sbuf("row_sum", [P, 2, 16], at=at_ctx)
        inv_sum = sbuf("inv_sum", [P, 16], at=at_ctx)
        o_tok = sbuf("o_tok", [P, 512], at=at_ctx)
        o_hi, o_lo = sbuf("o_hi", [P, 512], F32R, at_ctx), sbuf("o_lo", [P, 512], F32R, at_ctx)
        b_ctx = ExitStack()
        rope = sbuf("rope", [P, 4, 64], at=b_ctx)
        qk = [sbuf("q_tok", [P, 512], at=b_ctx), sbuf("k_tok", [P, 512], at=b_ctx)]
        squares = [sbuf("q_sq", [P, 512], at=b_ctx), sbuf("k_sq", [P, 512], at=b_ctx)]
        cos_part = [sbuf("q_cos", [P, 512], at=b_ctx), sbuf("k_cos", [P, 512], at=b_ctx)]
        rot = [sbuf("q_rot", [P, 512], at=b_ctx), sbuf("k_rot", [P, 512], at=b_ctx)]
        norm2 = sbuf("norm2", [P, 16], at=b_ctx)
        norm2c = sbuf("norm2c", [P, 16], at=b_ctx)
        rnorm = sbuf("rnorm", [P, 16], at=b_ctx)
        q_t_hi, q_t_lo = [sbuf(f"q_t_{h}", [P, ATT_B.NT, P], F32R, b_ctx) for h in ("hi", "lo")]
        k_t_hi, k_t_lo = [sbuf(f"k_t_{h}", [P, ATT_B.NT, (U + 1) * P], F32R, b_ctx) for h in ("hi", "lo")]
        b_ctx.close()
        a_ctx = ExitStack()
        z = sbuf("z", [P, D], at=a_ctx)
        h32 = sbuf("h32", [P, D], at=a_ctx)
        stats = sbuf("stats", [P, 6], at=a_ctx)
        mean_var = sbuf("mean_var", [P, 2], at=a_ctx)
        var_eps = sbuf("var_eps", [P, 1], at=a_ctx)
        rstd = sbuf("rstd", [P, 1], at=a_ctx)
        q_stack = sbuf("q_stack", [P, 16, 4, 16], F32R, a_ctx)
        k_stack = sbuf("k_stack", [P, 16, 4, 16], F32R, a_ctx)
        q_t_a = sbuf("q_t_a", [P, ATT_A.NT, P], F32R, a_ctx)
        k_t_a = sbuf("k_t_a", [P, ATT_A.NT, (U + 1) * P], F32R, a_ctx)
        a_ctx.close()
        at_ctx.close()

        m_ctx = ExitStack()
        gate = [sbuf(f"gate{i}", [P, GT], at=m_ctx) for i in range(RING)]
        hid = [sbuf(f"hid{i}", [P, GT], at=m_ctx) for i in range(RING)]
        u_hi, u_lo = sbuf("u_hi", [P, 8, GT], F32R, m_ctx), sbuf("u_lo", [P, 8, GT], F32R, m_ctx)
        g_old = [sbuf(f"g_old{i}", [P, 4, D], at=m_ctx) for i in range(2)]
        f_stats = sbuf("f_stats", [P, 4, 6], at=m_ctx)
        f_mv = sbuf("f_mv", [P, 4, 2], at=m_ctx)
        f_ve = sbuf("f_ve", [P, 4], at=m_ctx)
        f_rstd = sbuf("f_rstd", [P, 4], at=m_ctx)
        g_sum = [sbuf(f"g_sum{i}", [P, 4, D], at=m_ctx) for i in range(2)]
        g_new = sbuf("g_new", [P, 4, D], at=m_ctx)
        g_fin = sbuf("g_fin", [P, 4, D], at=m_ctx)
        m_ctx.close()

        consts_loaded = sem("consts_loaded")
        consts_set = sem("consts_set")
        first_zero_stored = sem("first_zero_stored")
        zero_rows_stored = sem("zero_rows_stored")
        wa_loaded, wm_loaded = sem("wa_loaded"), sem("wm_loaded")
        wa_split, wm_split = sem("wa_split"), sem("wm_split")
        wa_hi_done, wm_hi_done = sem("wa_hi_done"), sem("wm_hi_done")

        def sems(prefix, names):
            return {n: sem(f"{prefix}_{n}") for n in names.split()}

        att_names = """load0 load1 load2 load3 store0 store1 params phase_set
            ln_stats ln_aggr ln_var ln_rstd z_ready xt_ready h32_ready h_hi h_lo
            q_proj k_proj v_proj qk_hi qk_lo v_copied q_squared k_squared norm2_part norm2_ready rnorm_ready
            rope_ready q_parts k_parts q_rot k_rot qt_hi kt_hi qt_ready kt_ready qt_copied kt_copied
            mask0_ready scores_ready masked_ready probs_ready pt_ready pt_dve pt_act pv_done
            inv_ready o_ready ot_ready o_hi o_lo wo_ready y_ready"""
        SA = sems("a", " ".join(n for n in att_names.split() if n not in
                                "k_proj q_squared k_squared norm2_part norm2_ready rnorm_ready rope_ready q_parts k_parts q_rot k_rot qt_hi kt_hi".split()))
        SB = sems("b", " ".join(n for n in att_names.split() if n not in
                                "ln_stats ln_aggr ln_var ln_rstd z_ready h32_ready qk_hi qk_lo".split()))
        mlp_names = """load0 load1 old0 old1 store out_store params stats aggr var rstd z_ready xt_ready h32_ready h_hi h_lo h_lo_pool
            in_ready gate_ready hid_ready u_hi u_lo_dve u_lo_pool y_ready y_added res_ready
            f_sum f_stats f_var f_rstd fin_ready"""
        MA = sems("ma", " ".join(n for n in mlp_names.split() if n not in ("hid_ready", "u_lo_pool", "out_store")))
        MB = sems("mb", mlp_names)

        def rows_of(start, n):
            return slice(start, start + n) if isinstance(start, int) else bass.ds(start, n)

        def next_layer(layer):
            return 0 if layer is None else layer + 1

        def next_mlp(c):
            return MLP_A if c is ATT_A else MLP_B

        def wait_apart(eng, *waits):
            values = [(s, v if isinstance(v, int) else eng.snap(v)) for s, v in waits]
            for _, v in values:
                if not isinstance(v, int):
                    eng.lower_val(v)
            eng.wait_ge(consts_set, 1)
            for s, v in values:
                eng.wait_ge(s, v)

        block = ctx.enter_context(nc.Block())

        def attention_loop(eng, c, layer, prologue, step):
            base = 0 if layer is None else eng.snap(layer * NCH)
            prologue(base)
            for e in range(U):
                step(base + e, e, 0, e, {d: e + d >= 0 for d in range(-1, 4)})
            with eng.Fori(1, ITERS - 1) as j:
                g0 = eng.snap(j * U) if layer is None else eng.snap(layer * NCH + j * U)
                for e in range(U):
                    step(g0 + e, e, j, j * U + e, {d: True for d in range(-1, 4)})
            last = U * (ITERS - 1)
            for e in range(U):
                step(base + last + e, e, ITERS - 1, last + e, {d: e + d < U for d in range(-1, 4)})

        def load_attention_weights(sp, which, splits):
            if splits is not None:
                sp.wait_ge(wm_split, splits * SPLIT)
            sp.dma_start(w_raw[:, 0:which.shape[-1]], which).then_inc(wa_loaded, 16)

        def load_mlp_weights(sp, which, splits):
            sp.wait_ge(wa_split, splits * SPLIT)
            sp.dma_start(w_raw[:, 0:which.shape[-1]], which).then_inc(wm_loaded, 16)

        def sp_attention(sp, c, S, layer, opening=False):
            gated = c is ATT_B

            def load(n_local, slot):
                rows = bass.ds(n_local * P, P) if not isinstance(n_local, int) else slice(n_local * P, n_local * P + P)
                if c is ATT_A:
                    sp.dma_start(x_in[:, slot, 0:2, :].rearrange("p a d -> p (a d)"),
                                 io["x"][rows, :]).then_inc(S[f"load{slot}"], 16)
                    return
                srow = rows_of(layer * TOK + n_local * P, P)
                hrow = rows_of(layer * (TOK + P) + n_local * P, P)
                s = S[f"load{slot}"]
                sp.dma_start(x_in[:, slot, 0:3:2, :], x_state[srow, :].rearrange("p (a d) -> p a d", a=2)).then_inc(s, 16)
                sp.dma_start(x_in[:, slot, 1, :], x_state_sh[hrow, :]).then_inc(s, 16)
                sp.dma_start(rope_in[:, slot, :], io["rope"][rows, :]).then_inc(s, 16)

            def first_loads():
                load(0, 0)
                if c is ATT_A:
                    sp.dma_start(ident[:], io["ident"]).then_inc(consts_loaded, 16)
                    sp.dma_start(vec_a[:], io["vec_a"]).then_inc(consts_loaded, 16)
                    load_attention_weights(sp, io["w_att_a"], None)
                load(1, 1)
                masks = (io["mask_a"], io["mask_a0"]) if c is ATT_A else (io["mask_b"], io["mask_b0"])
                sp.dma_start(mask[:], masks[0]).then_inc(S["params"], 16)
                sp.dma_start(mask0[:], masks[0]).then_inc(S["params"], 16)
                sp.dma_start(mask0_prev[:], masks[1]).then_inc(S["params"], 16)
                if c is ATT_B:
                    sp.dma_start(rope_scale[:].rearrange("p a d -> p (a d)"),
                                 io["rope_scale"][rows_of(layer * P, P), :]).then_inc(S["params"], 16)
                load(2, 2)
                load(3, 3)

            def prologue(base):
                if c is ATT_A:
                    first_loads()
                    load_mlp_weights(sp, io["w_mlp_a"], 1)
                    sp.wait_ge(consts_set, 1)
                    sp.dma_start(x_mid_sh[0:1, :], zero_row[0:1, 0, :]).then_inc(first_zero_stored, 16)
                    for l in range(LAYERS + 1):
                        at = l * (TOK + P)
                        sp.dma_start(x_state_sh[at:at + 1, :], zero_row[0:1, 0, :]).then_inc(first_zero_stored, 16)
                else:
                    sp.wait_ge(zero_rows_stored, layer * 32 + 16)
                    load_mlp_weights(sp, io["w_mlp_b"][bass.ds(layer * P, P), :], layer + 2)

            if opening:
                first_loads()
                return

            def step(g, e, j, g_local, more):
                sp.wait_ge(S["y_ready"], g + 1)
                rows = bass.ds(g_local * P, P) if not isinstance(g_local, int) else slice(g_local * P, g_local * P + P)
                hrows = bass.ds(g_local * P + 1, P) if not isinstance(g_local, int) else \
                    slice(g_local * P + 1, g_local * P + 1 + P)
                sp.dma_start(x_mid[rows, :], y_out[:, e % 2, :]).then_inc(S[f"store{e % 2}"], 16)
                if gated:
                    sp.dma_start(x_mid_sh[hrows, :], y_out[:, e % 2, P:D]).then_inc(S[f"store{e % 2}"], 16)
                if not isinstance(j, int) or j < ITERS - 1:
                    load(g_local + U, e)
                elif e == 0:
                    n, used = (32 if gated else 16), 2 * GT // P // 2
                    for i in range(2):
                        sp.wait_ge(S[f"store{i}"], n * used + n if layer is None else
                                   layer * (n * (NCH // 2)) + (n * used + n))
                    sp_mlp(sp, next_mlp(c), MA if c is ATT_A else MB, layer, opening=True)

            attention_loop(sp, c, layer, prologue, step)
            n = 32 if gated else 16
            for e in range(2):
                sp.wait_ge(S[f"store{e}"], n * (NCH // 2) + n if layer is None else
                           layer * (n * (NCH // 2)) + (n * (NCH // 2) + n))
            if gated:
                sp.dma_start(x_mid_sh[SEQ:SEQ + 1, :], zero_row[0:1, 1, :]).then_inc(zero_rows_stored, 16)

        def sp_mlp(sp, c, S, layer, opening=False):
            def token_rows(ap, start, cols=slice(0, D)):
                r = bass.ds(start, GT) if not isinstance(start, int) else slice(start, start + GT)
                return ap[r, cols].rearrange("(c p) d -> p c d", p=P)

            def load_old(t_local, slot):
                sp.dma_start(g_old[slot][:], token_rows(io["x"] if c is MLP_A else x_state, t_local * GT)).then_inc(
                    S[f"old{slot}"], 16)

            def load(t_local, slot):
                s = S[f"load{slot}"]
                if c is MLP_A:
                    sp.dma_start(g_in[slot][:, :, 0:2, :].rearrange("p c a d -> p c (a d)"),
                                 token_rows(x_mid, t_local * GT)).then_inc(s, 16)
                    return
                sp.dma_start(g_in[slot][:, :, 0, :], token_rows(x_mid, t_local * GT, slice(0, P))).then_inc(s, 16)
                sp.dma_start(g_in[slot][:, :, 1, :], token_rows(x_mid_sh, t_local * GT, slice(0, P))).then_inc(s, 16)
                sp.dma_start(g_in[slot][:, :, 2, :], token_rows(x_mid, t_local * GT, slice(P, D))).then_inc(s, 16)

            if opening:
                load(0, 0)
                if c is MLP_A:
                    sp.dma_start(row_b2[:], io["b2_a"]).then_inc(S["params"], 16)
                else:
                    sp.dma_start(vec_b[:], io["vec_b"][bass.ds(layer * P, P), :]).then_inc(S["params"], 16)
                    sp.dma_start(row_b2[:], io["b2_b"][bass.ds(layer * P, P), :]).then_inc(S["params"], 16)
                load(1, 1)
                return
            load_old(0, 0)
            load_old(1, 1)
            if c is MLP_B:
                sp.wait_ge(zero_rows_stored, layer * 32 + 32)
            load_attention_weights(sp, io["w_att_b"][0:P, :] if c is MLP_A else io["w_att_b"][P:2 * P, :],
                                   1 if layer is None else layer + 2)
            base = 0 if layer is None else layer * NGRP

            def store(t_local, t):
                s = S["store"]
                if c is MLP_A:
                    sp.wait_ge(S["fin_ready"], t + 1)
                    sp.dma_start(token_rows(x_state, t_local * GT), g_fin[:]).then_inc(s, 16)
                    sp.dma_start(token_rows(x_state_sh, t_local * GT + 1, slice(0, P)), g_fin[:, :, P:D]).then_inc(s, 16)
                    return
                sp.dma_start(token_rows(x_state, (layer + 1) * TOK + t_local * GT), g_new[:]).then_inc(s, 16)
                sp.dma_start(token_rows(x_state_sh, (layer + 1) * (TOK + P) + t_local * GT + 1, slice(0, P)),
                             g_new[:, :, P:D]).then_inc(s, 16)
                sp.wait_ge(S["fin_ready"], t + 1)
                sp.dma_start(token_rows(io["out"], t_local * GT), g_fin[:]).then_inc(S["out_store"], 16)

            n = 32
            with sp.Fori(0, NGRP // 2 - 1) as i:
                t0 = sp.snap(i * 2) if layer is None else sp.snap(layer * NGRP + i * 2)
                for e in range(2):
                    sp.wait_ge(S["f_sum"], t0 + (e + 1))
                    load(i * 2 + e + 2, e)
                    load_old(i * 2 + e + 2, e)
                    store(i * 2 + e, t0 + e)
            sp.wait_ge(S["store"], base * n + 2 * n)
            sp_attention(sp, ATT_B, SB, next_layer(layer), opening=True)
            for e in range(2):
                sp.wait_ge(S["f_sum"], base + (NGRP - 1 + e))
                store(NGRP - 2 + e, base + NGRP - 2 + e)
            sp.wait_ge(S["store"], base * n + (n * NGRP + n))
            if c is MLP_B:
                sp.wait_ge(S["out_store"], base * 16 + (16 * NGRP + 16))
            at = SEQ if c is MLP_A else (layer + 1) * (TOK + P) + SEQ
            r = slice(at, at + 1) if isinstance(at, int) else bass.ds(at, 1)
            sp.dma_start(x_state_sh[r, :], zero_row[0:1, 1, :]).then_inc(zero_rows_stored, 16)

        @block.sync
        def _(sp):
            for e in range(2):
                sp.sem_inc(SA[f"store{e}"], 16)
                sp.sem_inc(SB[f"store{e}"], 32)
            sp.sem_inc(MA["store"], 32)
            sp.sem_inc(MB["store"], 32)
            sp.sem_inc(MB["out_store"], 16)
            sp_attention(sp, ATT_A, SA, None)
            sp.wait_ge(first_zero_stored, 16 * (LAYERS + 2))
            sp_mlp(sp, MLP_A, MA, None)
            with sp.Fori(0, LAYERS) as layer:
                sp_attention(sp, ATT_B, SB, layer)
                sp_mlp(sp, MLP_B, MB, layer)
            for slot in range(U):
                sp.wait_ge(SB[f"load{slot}"], LAYERS * (NCH // U) * 48 + 48)
            sp.wait_ge(SB["params"], (LAYERS + 1) * 64)
            sp.wait_ge(zero_rows_stored, 16 + 32 * LAYERS)

        def product3(out, a_hi, a_lo, b_hi, b_lo, first, last):
            nc.tensor.matmul(out, a_hi, b_hi, start=first, stop=False)
            nc.tensor.matmul(out, a_hi, b_lo, start=False, stop=False)
            return nc.tensor.matmul(out, a_lo, b_hi, start=False, stop=last)

        def pe_attention(pe, c, S, layer, opening=False):
            wqkv_hi = wa_hi[:, 0:KD * c.QKV].rearrange("p (k n) -> p k n", k=KD)
            wqkv_lo = wa_lo[:, 0:KD * c.QKV].rearrange("p (k n) -> p k n", k=KD)
            wo_hi = wa_hi[:, KD * c.QKV:c.WCOLS].rearrange("p (k n) -> p k n", k=c.KO)
            wo_lo = wa_lo[:, KD * c.QKV:c.WCOLS].rearrange("p (k n) -> p k n", k=c.KO)

            def project(n, part, n_before=None):
                if part == 0:
                    pe.wait_ge(S["h_hi"], n + 1)
                    pe.wait_ge(S["h_lo"], n + 1)
                if c is ATT_A:
                    if part == 2:
                        return
                    out, c0, w = [(work[1], 0, 512), (work[2], 512, 256)][part]
                    done = S[["q_proj", "v_proj"][part]]
                else:
                    if n_before is not None and part > 0:
                        pe.wait_ge(S[["", "k_squared", "v_copied"][part]], n_before + 1)
                    out, c0, w = [(work[1], 0, 512), (work[2], 512, 512), (work[0], 1024, 512)][part]
                    done = S[["q_proj", "k_proj", "v_proj"][part]]
                for k in range(KD):
                    mm = product3(out[:, 0:w], h_hi[:, k * P:k * P + P], h_lo[:, k * P:k * P + P],
                                  wqkv_hi[:, k, c0:c0 + w], wqkv_lo[:, k, c0:c0 + w], k == 0, k == KD - 1)
                mm.then_inc(done, 1)

            def transpose_x(m, slot):
                if c is ATT_A:
                    pe.wait_ge(S["z_ready"], m + 1)
                    src = z[:, :]
                else:
                    pe.wait_ge(S[f"load{slot}"], load_count(c, m, slot))
                    src = x_in[:, slot, 0:2, :].rearrange("p a d -> p (a d)")
                for k in range(KD):
                    mm = nc.tensor.transpose(work[1][:, k * P:k * P + P], src[:, k * P:k * P + P], ident[:])
                mm.then_inc(S["xt_ready"], 1)

            def transpose_tiles(bank_, source, tile0, done):
                for i in range(4):
                    mm = nc.tensor.transpose(bank_[:, i * P:i * P + P], source[:, (tile0 + i) * P:(tile0 + i + 1) * P],
                                             ident[:])
                mm.then_inc(done, 1)

            def transpose_stack(n, part):
                if part == 0:
                    pe.wait_ge(S["qk_lo"], 2 * n + 2)
                elif part == 1:
                    pe.wait_ge(S["v_copied"], n + 1)
                else:
                    pe.wait_ge(S["kt_copied"], n * 2 + (part - 1))
                src = (k_stack if part < 2 else q_stack)[:].rearrange("p h s d -> p (h s d)").bitcast(F32)
                transpose_tiles(work[1 + part % 2], src, 4 * (part % 2), S["kt_ready" if part < 2 else "qt_ready"])

            def transpose_qk(n, projected):
                for i, rotated, squared, done in ((1, "k_rot", "k_squared", "kt_ready"),
                                                  (0, "q_rot", "q_squared", "qt_ready")):
                    if projected is not None:
                        pe.wait_ge(S[squared], projected + 1)
                    pe.wait_ge(S[rotated], n + 1)
                    transpose_tiles(work[1 + i], rot[i], 0, S[done])

            def score_pair(g, e, p, first=False):
                if p == 0:
                    pe.wait_ge(S["qt_copied"], g * c.TB + 1)
                    pe.wait_ge(S["kt_copied"], g * c.TB + c.TB)
                if p == 4:
                    pe.wait_ge(S["qt_copied"], g * c.TB + c.TB)
                if p >= 2 or not first:
                    pe.wait_ge(S["masked_ready"], g * c.NP + (p - 1))
                for hh in range(2):
                    h = c.head(p, hh)
                    t, r = h // c.HPT, (h % c.HPT) * c.RS
                    out = scores[p % 2][:, hh * 256:hh * 256 + 256]
                    rows, window = slice(r, r + c.R), slice(e * P, e * P + 2 * P)
                    if c is ATT_A:
                        mm = nc.tensor.matmul(out, q_t_a[rows, t, :], k_t_a[rows, t, window], start=True, stop=True)
                    else:
                        mm = product3(out, q_t_hi[rows, t, :], q_t_lo[rows, t, :],
                                      k_t_hi[rows, t, window], k_t_lo[rows, t, window], True, True)
                mm.then_inc(S["scores_ready"], 1)

            def transpose_probs(g, p):
                pe.wait_ge(S["probs_ready"], g * c.NP + (p + 1))
                for i in range(4):
                    mm = nc.tensor.transpose(probs_t[p % 2][:, i * P:i * P + P], probs[p % 2][:, i * P:i * P + P],
                                             ident[:])
                mm.then_inc(S["pt_ready"], 1)

            def value_pair(g, e, p):
                by, k, per = evacuator(c, p)
                pe.wait_ge(S[by], g * per + (k + 1))
                for hh in range(2):
                    h = c.head(p, hh)
                    cols = slice(h * c.DH, h * c.DH + c.DH)
                    for blk, slot in ((0, (e - 1) % U), (1, e)):
                        i = 2 * hh + blk
                        mm = nc.tensor.matmul(heads_out[:, cols], pt[p % 2][:, i * P:i * P + P], v_tok[slot][:, cols],
                                              start=(blk == 0), stop=(blk == 1))
                mm.then_inc(S["pv_done"], 1)

            def output(g, more):
                pe.wait_ge(S["o_ready"], g + 1)
                if more[2] and c is ATT_B:
                    pe.wait_ge(S["v_copied"], g + 3)
                for k in range(c.KO):
                    mm = nc.tensor.transpose(work[0][:, k * P:k * P + P], o_tok[:, k * P:k * P + P], ident[:])
                mm.then_inc(S["ot_ready"], 1)

            def out_project(g):
                pe.wait_ge(S["o_hi"], g + 1)
                pe.wait_ge(S["o_lo"], g + 1)
                for k in range(c.KO):
                    mm = product3(work[0][:, 0:D], o_hi[:, k * P:k * P + P], o_lo[:, k * P:k * P + P],
                                  wo_hi[:, k, :], wo_lo[:, k, :], k == 0, k == c.KO - 1)
                mm.then_inc(S["wo_ready"], 1)

            if opening:
                transpose_x(first_chunk(pe, layer), 0)
                return

            def prologue(base):
                if c is ATT_A:
                    transpose_x(base, 0)
                pe.wait_ge(wa_split, SPLIT if layer is None else layer * SPLIT + 2 * SPLIT)
                for part in range(3):
                    project(base, part)
                if c is ATT_A:
                    for part in range(4):
                        transpose_stack(base, part)
                else:
                    pe.wait_ge(S["q_squared"], base + 1)
                    transpose_x(base + 1, 1)
                    for part in range(3):
                        project(base + 1, part, base)
                    transpose_qk(base, base + 1)
                pe.wait_ge(S["phase_set"], 2 if layer is None else layer * 2 + 2)
                score_pair(base, 0, 0, True)
                score_pair(base, 0, 1, True)
                transpose_x(base + c.AHEAD, c.AHEAD)

            def step_a(g, e, j, g_local, more):
                for p in range(c.NP):
                    transpose_probs(g, p)
                    if p + 2 < c.NP:
                        score_pair(g, e, p + 2)
                    elif more[1]:
                        score_pair(g + 1, (e + 1) % U, p + 2 - c.NP)
                    if more[1]:
                        if p < 2:
                            project(g + 1, p)
                        elif p < 6:
                            transpose_stack(g + 1, p - 2)
                    if p == 0:
                        pe.wait_ge(S["v_copied"], g + 1)
                        if more[-1]:
                            value_pair(g - 1, (e - 1) % U, c.NP - 1)
                    else:
                        if p == 1 and more[-1]:
                            pe.wait_ge(S["o_ready"], g)
                        value_pair(g, e, p - 1)
                    if p == 2 and more[-1]:
                        output(g - 1, more)
                    if p == 4 and more[-1]:
                        out_project(g - 1)
                    if p == 6 and more[2]:
                        transpose_x(g + 2, (e + 2) % U)
                if not more[1]:
                    value_pair(g, e, c.NP - 1)
                    output(g, more)
                    pe_mlp(pe, next_mlp(c), MA, layer, opening=True)
                    out_project(g)

            def step(g, e, j, g_local, more):
                n = g + 2
                for p in range(c.NP):
                    transpose_probs(g, p)
                    if p + 2 < c.NP:
                        score_pair(g, e, p + 2)
                    if p < 2 and more[2]:
                        project(n, p)
                    if p == 0 and more[-1]:
                        out_project(g - 1)
                    if p == 0:
                        pe.wait_ge(S["v_copied"], g + 1)
                    else:
                        value_pair(g, e, p - 1)
                    if p == 2 and more[1]:
                        transpose_qk(g + 1, n if more[2] else None)
                    if p == 2 and more[2]:
                        project(n, p)
                if more[1]:
                    score_pair(g + 1, (e + 1) % U, 0)
                value_pair(g, e, c.NP - 1)
                if more[3]:
                    transpose_x(g + 3, (e + 3) % U)
                if more[1]:
                    score_pair(g + 1, (e + 1) % U, 1)
                output(g, more)
                if not more[1]:
                    pe_mlp(pe, next_mlp(c), MB, layer, opening=True)
                    out_project(g)

            attention_loop(pe, c, layer, prologue, step_a if c is ATT_A else step)
            pe.wait_ge(S["y_ready"], NCH if layer is None else layer * NCH + NCH)

        def first_chunk(eng, layer):
            return layer * NCH if isinstance(layer, int) else eng.snap(layer * NCH)

        def load_count(c, n, slot):
            per = 16 if c is ATT_A else 48
            return (n - slot) * (per // U) + per

        def evacuator(c, p):
            if c is ATT_A:
                return ("pt_dve", p // 2, 4) if p % 2 == 0 else ("pt_act", p // 2, 4)
            return ("pt_dve", 0, 1) if p == 0 else ("pt_act", p - 1, 3)

        HIDDEN_BANKS = (0, 1, 6, 7, 2, 3)

        def hidden_bank(c, f, part=0):
            return bank[HIDDEN_BANKS[(2 * f + part if c.gated else f) % 6]]

        def pe_mlp(pe, c, S, layer, opening=False):
            w1_hi = wm_hi[:, 0:KD * c.IN].rearrange("p (k n) -> p k n", k=KD)
            w1_lo = wm_lo[:, 0:KD * c.IN].rearrange("p (k n) -> p k n", k=KD)
            w2_hi = wm_hi[:, KD * c.IN:c.WCOLS].rearrange("p (k n) -> p k n", k=c.NF)
            w2_lo = wm_lo[:, KD * c.IN:c.WCOLS].rearrange("p (k n) -> p k n", k=c.NF)
            xt_banks = bank[4:6]
            y_banks = [bank[6:8], bank[2:4]]

            def transpose_z(t):
                pe.wait_ge(S["z_ready"], t + 1)
                for k in range(KD):
                    for i in range(4):
                        mm = nc.tensor.transpose(xt_banks[k][:, i * P:i * P + P], g_z[:, i, k * P:k * P + P], ident[:])
                mm.then_inc(S["xt_ready"], 1)

            def hidden(t, f, steady):
                r = c.rows[f]
                per = 2 if c.gated else 1
                if per * f >= 6:
                    pe.wait_ge(S["hid_ready" if c.gated else "gate_ready"], t * c.NF + (f - 6 // per + 1))
                elif per * f in (2, 4) and steady:
                    pe.wait_ge(S["y_added"], t * 4 - (4 - per * f))
                if c.gated:
                    targets = [(hidden_bank(c, f, 0), c.H + f * c.FT), (hidden_bank(c, f, 1), f * c.FT)]
                else:
                    targets = [(hidden_bank(c, f), f * c.FT)]
                for out, c0 in targets:
                    for k in range(KD):
                        mm = product3(out[0:r, :], w1_hi[:, k, c0:c0 + r], w1_lo[:, k, c0:c0 + r],
                                      g_h_hi[:, k, :], g_h_lo[:, k, :], k == 0, k == KD - 1)
                    mm.then_inc(S["in_ready"], 1)

            def down(t, half):
                if half == 0:
                    if c.gated:
                        pe.wait_ge(S["hid_ready"], t * c.NF + 5)
                    else:
                        pe.wait_ge(S["gate_ready"], t * c.NF + 4)
                for f in range(c.NF):
                    r = c.rows[f]
                    if half == 0:
                        pe.wait_ge(S["u_hi"], t * c.NF + (f + 1))
                        if c.gated:
                            pe.wait_ge(S[["u_lo_dve", "u_lo_pool"][f % 2]], t * 3 + (f // 2 + 1))
                        else:
                            pe.wait_ge(S["u_lo_dve"], t * c.NF + (f + 1))
                    for i in range(2):
                        ch = 2 * half + i
                        mm = product3(y_banks[half][i][:, 0:D], u_hi[0:r, f, ch * P:ch * P + P], u_lo[0:r, f, ch * P:ch * P + P],
                                      w2_hi[0:r, f, :], w2_lo[0:r, f, :], f == 0, f == c.NF - 1)
                mm.then_inc(S["y_ready"], 1)

            def group(t, more, steady=True):
                pe.wait_ge(S["h_hi"], t + 1)
                pe.wait_ge(S["h_lo"], t + 1)
                pe.wait_ge(S["h_lo_pool"], t + 1)
                for f in range(c.NF):
                    hidden(t, f, steady)
                if more:
                    transpose_z(t + 1)
                down(t, 0)
                if not more:
                    pe_attention(pe, ATT_B, SB, next_layer(layer), opening=True)
                down(t, 1)

            base = 0 if layer is None else pe.snap(layer * NGRP)
            if opening:
                transpose_z(base)
                return
            pe.wait_ge(wm_split, SPLIT if layer is None else layer * SPLIT + 2 * SPLIT)
            group(base, True, False)
            with pe.Fori(1, NGRP - 1) as i:
                group(pe.snap(i + 0) if layer is None else pe.snap(layer * NGRP + i), True)
            group(base + (NGRP - 1), False)
            pe.wait_ge(S["y_added"], base * 4 + 4 * NGRP)

        @block.tensor
        def _(pe):
            pe.wait_ge(consts_loaded, 32)
            pe_attention(pe, ATT_A, SA, None)
            pe_mlp(pe, MLP_A, MA, None)
            with pe.Fori(0, LAYERS) as layer:
                pe_attention(pe, ATT_B, SB, layer)
                pe_mlp(pe, MLP_B, MB, layer)

        def piece(cols, i):
            w = -(-cols // SPLIT)
            return slice(i * w, min(cols, i * w + w))

        def pieces_of_step(c, j, e):
            if not isinstance(j, int) or j < ITERS - 1:
                return []
            n = 4 if c is ATT_A else 3
            return list(range(n * e, min(SPLIT, n * e + n)))

        def split_low(eng, engine, lo, hi, hi_done, done, cols, i, before):
            eng.wait_ge(hi_done, before * SPLIT + (i + 1))
            at = piece(cols, i)
            engine.tensor_tensor(lo[:, at], w_raw[:, at], hi[:, at].bitcast(F32), ALU.subtract).then_inc(done, 1)

        def dve_attention(v, c, S, layer, opening=False):
            def heads(ap, n=None):
                return ap.rearrange("p (h d) -> p h d", d=c.DH)

            def layer_norm_stats(m, slot):
                v.wait_ge(S[f"load{slot}"], load_count(c, m, slot))
                nc.vector.bn_stats(stats[:], x_in[:, slot, 0:2, :].rearrange("p a d -> p (a d)")).then_inc(S["ln_stats"], 1)
                wait_apart(v, (S["ln_stats"], m + 1))
                nc.vector.bn_aggr(mean_var[:], stats[:]).then_inc(S["ln_aggr"], 1)
                v.wait_ge(S["ln_aggr"], m + 1)
                nc.vector.tensor_scalar_add(var_eps[:], mean_var[:, 1:2], EPS).then_inc(S["ln_var"], 1)

            def normalize(m, slot):
                v.wait_ge(S["ln_rstd"], m + 1)
                nc.vector.tensor_scalar(z[:], x_in[:, slot, 0:2, :].rearrange("p a d -> p (a d)"), mean_var[:, 0:1], rstd[:], ALU.subtract,
                                        ALU.mult).then_inc(S["z_ready"], 1)

            def h_transposed(m):
                v.wait_ge(S["xt_ready"], m + 1)
                if c is ATT_A:
                    for k in range(KD):
                        ins = nc.vector.tensor_scalar(h32[:, k * P:k * P + P], work[1][:, k * P:k * P + P],
                                                      vec_a[:, k:k + 1], vec_a[:, 2 + k:3 + k], ALU.mult, ALU.add)
                    ins.then_inc(S["h32_ready"], 1)
                else:
                    v.wait_ge(S["h_hi"], m + 1)
                    nc.vector.tensor_tensor(h_lo[:], work[1][:, 0:D], h_hi[:].bitcast(F32),
                                            ALU.subtract).then_inc(S["h_lo"], 1)

            def h_low(m):
                v.wait_ge(S["h_hi"], m + 1)
                nc.vector.tensor_tensor(h_lo[:], h32[:], h_hi[:].bitcast(F32), ALU.subtract).then_inc(S["h_lo"], 1)

            def split_qk_low(n):
                v.wait_ge(S["qk_hi"], 2 * n + 2)
                q_src = work[1][:, 0:256].rearrange("p (h d) -> p h d", d=c.DH)
                k_src = work[1][:, 256:512].rearrange("p (h d) -> p h d", d=c.DH)
                nc.vector.scalar_tensor_tensor(q_stack[:, :, 2, :], q_src, c.DH ** -0.5, q_stack[:, :, 0, :].bitcast(F32),
                                               ALU.mult, ALU.subtract).then_inc(S["qk_lo"], 1)
                nc.vector.tensor_tensor(k_stack[:, :, 1, :], k_src, k_stack[:, :, 0, :].bitcast(F32),
                                        ALU.subtract).then_inc(S["qk_lo"], 1)

            def norms(n, i):
                v.wait_ge(S[["q_squared", "k_squared"][i]], n + 1)
                nc.vector.tensor_reduce(norm2[:, 8 * i:8 * i + 8], heads(squares[i][:]), AX.X,
                                        ALU.add).then_inc(S["norm2_part"], 1)
                if i == 1:
                    v.wait_ge(S["norm2_part"], 2 * n + 2)
                    nc.vector.tensor_scalar_max(norm2c[:], norm2[:], 1e-24).then_inc(S["norm2_ready"], 1)

            def rotate_q(n):
                v.wait_ge(S["rope_ready"], n + 1)
                v.wait_ge(S["q_squared"], n + 1)
                rotate(nc.vector, 0, S["q_parts"])
                v.wait_ge(S["q_parts"], 4 * n + 3)
                nc.vector.tensor_tensor(cos_part[0][:], cos_part[0][:], squares[0][:], ALU.add).then_inc(S["q_parts"], 1)

            def scale_rotated(n):
                for i, summed, done in ((0, "q_parts", "q_rot"), (1, "k_parts", "k_rot")):
                    v.wait_ge(S[summed], 4 * n + 4)
                    v.wait_ge(S["rnorm_ready"], n + 1)
                    r = rnorm[:, 8 * i:8 * i + 8].unsqueeze(2).to_broadcast([P, c.NH, c.DH])
                    nc.vector.tensor_tensor(heads(rot[i][:]), heads(cos_part[i][:]), r, ALU.mult).then_inc(S[done], 1)

            def qk_t_low(n, slot):
                v.wait_ge(S["kt_hi"], n + 1)
                src = work[2][:].rearrange("p (t q) -> p t q", q=P)
                cols = slice((slot + 1) * P, (slot + 2) * P)
                nc.vector.tensor_tensor(k_t_lo[:, :, cols], src, k_t_hi[:, :, cols].bitcast(F32),
                                        ALU.subtract).then_inc(S["kt_copied"], 1)
                v.wait_ge(S["qt_hi"], n + 1)
                nc.vector.tensor_tensor(q_t_lo[:], work[1][:].rearrange("p (t q) -> p t q", q=P), q_t_hi[:].bitcast(F32),
                                        ALU.subtract).then_inc(S["qt_copied"], 1)

            def copy_q_t(n, half=0):
                v.wait_ge(S["qt_ready"], n * c.TB + (half + 1))
                nc.vector.tensor_copy(q_t_a[:, 4 * half:4 * half + 4, :].rearrange("p t q -> p (t q)"),
                                      work[1 + half][:]).then_inc(S["qt_copied"], 1)

            def mask_pair(g, e, p, it=None, first=False):
                waits = [(S["scores_ready"], g * c.NP + (p + 1))]
                if p >= 2 or not first:
                    waits.append((S["probs_ready"], g * c.NP + (p - 1)))
                if e == 0 and p == 0:
                    waits.append((S["mask0_ready"], it))
                wait_apart(v, *waits)
                for hh in range(2):
                    h = c.head(p, hh)
                    cols = slice(hh * 256, hh * 256 + 256)
                    ins = nc.vector.tensor_tensor_reduce(masked[p % 2][:, cols], scores[p % 2][:, cols],
                                                         (mask0 if e == 0 else mask)[:], -1.0, BIG, ALU.add, ALU.min,
                                                         neg_max[:, h:h + 1])
                ins.then_inc(S["masked_ready"], 1)

            def copy_probs(g, p):
                by, k, per = evacuator(c, p)
                if by != "pt_dve":
                    return
                v.wait_ge(S["pt_ready"], g * c.NP + (p + 1))
                if p >= 2:
                    v.wait_ge(S["pv_done"], g * c.NP + (p - 1))
                nc.vector.tensor_copy(pt[p % 2][:], probs_t[p % 2][:]).then_inc(S["pt_dve"], 1)

            def normalize_heads(g, e):
                v.wait_ge(S["pv_done"], g * c.NP + c.NP)
                nc.vector.reciprocal(inv_sum[:, 0:c.NH], row_sum[:, e % 2, 0:c.NH]).then_inc(S["inv_ready"], 1)
                v.wait_ge(S["inv_ready"], g + 1)
                r = inv_sum[:, 0:c.NH].unsqueeze(2).to_broadcast([P, c.NH, c.DH])
                nc.vector.tensor_tensor(heads(o_tok[:, 0:c.OC]), heads(heads_out[:, 0:c.OC]), r,
                                        ALU.mult).then_inc(S["o_ready"], 1)

            def split_o(g):
                v.wait_ge(S["ot_ready"], g + 1)
                v.wait_ge(S["o_hi"], g + 1)
                nc.vector.tensor_tensor(o_lo[:, 0:c.OC], work[0][:, 0:c.OC], o_hi[:, 0:c.OC].bitcast(F32),
                                        ALU.subtract).then_inc(S["o_lo"], 1)

            def add_residual(g, e):
                v.wait_ge(S["wo_ready"], g + 1)
                per = 16 if c is ATT_A else 32
                v.wait_ge(S[f"store{e % 2}"], (g - e % 2) * (per // 2) + per)
                res = x_in[:, e, 0:2, :] if c is ATT_A else x_in[:, e, 0:3:2, :]
                nc.vector.tensor_tensor(y_out[:, e % 2, :].rearrange("p (a d) -> p a d", a=2),
                                        work[0][:, 0:D].rearrange("p (a d) -> p a d", a=2), res,
                                        ALU.add).then_inc(S["y_ready"], 1)

            def make_mask0(j):
                src = mask0_prev[:, j, :] if isinstance(j, int) else \
                    mask0_prev[:, bass.ds(j, 1), :].rearrange("p a k -> p (a k)")
                nc.vector.tensor_copy(mask0[:, 0:P], src).then_inc(S["mask0_ready"], 1)

            if opening:
                h_transposed(first_chunk(v, layer))
                return

            def prologue(base):
                if c is ATT_A:
                    layer_norm_stats(base, 0)
                    normalize(base, 0)
                    v.wait_ge(consts_loaded, 32)
                    h_transposed(base)
                    h_low(base)
                    for i in range(SPLIT):
                        split_low(v, nc.vector, wa_lo, wa_hi, wa_hi_done, wa_split, c.WCOLS, i, 0)
                v.wait_ge(S["params"], 48 if layer is None else layer * 64 + 64)
                make_mask0(0)
                if c is ATT_A:
                    layer_norm_stats(base + 1, 1)
                    normalize(base + 1, 1)
                    split_qk_low(base)
                    copy_q_t(base, 0)
                    copy_q_t(base, 1)
                else:
                    h_transposed(base + 1)
                    norms(base, 0)
                    norms(base, 1)
                    rotate_q(base)
                    scale_rotated(base)
                    norms(base + 1, 0)
                    norms(base + 1, 1)
                    rotate_q(base + 1)
                    qk_t_low(base, 0)
                it = 1 if layer is None else layer * ITERS + 1
                mask_pair(base, 0, 0, it, True)
                mask_pair(base, 0, 1, None, True)
                h_transposed(base + c.AHEAD)
                if c is ATT_A:
                    h_low(base + 1)

            def step_a(g, e, j, g_local, more):
                before, ms = (e - 1) % U, (e + 2) % U
                for p in range(c.NP):
                    copy_probs(g, p)
                    if p + 2 < c.NP:
                        mask_pair(g, e, p + 2)
                    elif more[1]:
                        it = None
                        if p == 6 and e == U - 1:
                            make_mask0(j + 1)
                            it = j + 2
                        mask_pair(g + 1, (e + 1) % U, p + 2 - c.NP, it)
                    if p == 0 and more[-1]:
                        normalize_heads(g - 1, before)
                    if p == 1 and more[1]:
                        split_qk_low(g + 1)
                    if p == 2 and more[2]:
                        layer_norm_stats(g + 2, ms)
                    if p == 3 and more[-1]:
                        split_o(g - 1)
                    if p == 4 and more[2]:
                        normalize(g + 2, ms)
                    if p == 5:
                        if more[1]:
                            copy_q_t(g + 1, 0)
                        if more[-1]:
                            add_residual(g - 1, before)
                    if p == 6:
                        if more[1]:
                            copy_q_t(g + 1, 1)
                        if more[2]:
                            h_transposed(g + 2)
                    if p == 7 and more[2]:
                        h_low(g + 2)
                    if not more[1] and p in (5, 7):
                        dve_mlp(v, next_mlp(c), MA, layer, opening=(p - 5) // 2)
                if not more[1]:
                    normalize_heads(g, e)
                    split_o(g)
                    dve_mlp(v, next_mlp(c), MA, layer, opening=2)
                    add_residual(g, e)

            def step(g, e, j, g_local, more):
                for p in range(c.NP):
                    if p == 0:
                        mask_pair(g, e, 2)
                        if more[1]:
                            scale_rotated(g + 1)
                        if more[-1]:
                            add_residual(g - 1, (e - 1) % U)
                        copy_probs(g, 0)
                    if p == 1:
                        mask_pair(g, e, 3)
                        if more[2]:
                            norms(g + 2, 0)
                    if p == 2:
                        if more[2]:
                            norms(g + 2, 1)
                        if more[1]:
                            qk_t_low(g + 1, (e + 1) % U)
                        if more[2]:
                            rotate_q(g + 2)
                    if p == 3 and more[1]:
                        it = None
                        if e == U - 1:
                            make_mask0(j + 1)
                            it = layer * ITERS + (j + 2)
                        mask_pair(g + 1, (e + 1) % U, 0, it)
                    if not more[1] and p in (0, 3):
                        dve_mlp(v, next_mlp(c), MB, layer, opening=p // 3)
                normalize_heads(g, e)
                if more[1]:
                    mask_pair(g + 1, (e + 1) % U, 1)
                if more[3]:
                    h_transposed(g + 3)
                split_o(g)
                if not more[1]:
                    dve_mlp(v, next_mlp(c), MB, layer, opening=2)
                    add_residual(g, e)

            attention_loop(v, c, layer, prologue, step_a if c is ATT_A else step)

        def rotate(engine, i, done):
            x = qk[i][:].rearrange("p (h d) -> p h d", d=64)
            half = 32
            def table(a, lo, hi):
                return rope[:, a, lo:hi].unsqueeze(1).to_broadcast([P, 8, hi - lo])
            engine.tensor_tensor(cos_part[i][:].rearrange("p (h d) -> p h d", d=64), x, table(2 * i, 0, 64),
                                 ALU.mult).then_inc(done, 1)
            s = squares[i][:].rearrange("p (h d) -> p h d", d=64)
            engine.tensor_tensor(s[:, :, 0:half], x[:, :, half:64], table(2 * i + 1, 0, half), ALU.mult).then_inc(done, 1)
            engine.tensor_tensor(s[:, :, half:64], x[:, :, 0:half], table(2 * i + 1, half, 64), ALU.mult).then_inc(done, 1)

        def m_load_count(c, t, slot):
            per = 16 if c is MLP_A else 48
            return (t - slot) * (per // 2) + per

        def dve_mlp(v, c, S, layer, opening=None):
            vec = vec_a if c is MLP_A else vec_b
            g0c = 4 if c is MLP_A else 0

            def ln_in(slot, i):
                return g_in[slot][:, i, 0:2, :].rearrange("p a d -> p (a d)")

            def norm_stats(t, slot):
                v.wait_ge(S[f"load{slot}"], m_load_count(c, t, slot))
                for i in range(4):
                    ins = nc.vector.bn_stats(g_stats[:, i, :], ln_in(slot, i))
                ins.then_inc(S["stats"], 1)
                wait_apart(v, (S["stats"], t + 1))
                for i in range(4):
                    ins = nc.vector.bn_aggr(g_mv[:, i, :], g_stats[:, i, :])
                ins.then_inc(S["aggr"], 1)
                v.wait_ge(S["aggr"], t + 1)
                nc.vector.tensor_scalar_add(g_ve[:], g_mv[:, :, 1], EPS).then_inc(S["var"], 1)

            def normalize(t, slot):
                v.wait_ge(S["rstd"], t + 1)
                for i in range(4):
                    ins = nc.vector.tensor_scalar(g_z[:, i, :], ln_in(slot, i), g_mv[:, i, 0:1],
                                                  g_rstd[:, i:i + 1], ALU.subtract, ALU.mult)
                ins.then_inc(S["z_ready"], 1)

            def gain_bias(t):
                v.wait_ge(S["xt_ready"], t + 1)
                for k in range(KD):
                    nc.vector.tensor_scalar(g_h32[:, k, :], bank[4 + k][:], vec[:, g0c + k:g0c + k + 1],
                                            vec[:, g0c + 2 + k:g0c + 3 + k], ALU.mult, ALU.add).then_inc(S["h32_ready"], 1)

            def h_low(t):
                v.wait_ge(S["h_hi"], t + 1)
                nc.vector.tensor_tensor(g_h_lo[:, 1, :], g_h32[:, 1, :], g_h_hi[:, 1, :].bitcast(F32),
                                        ALU.subtract).then_inc(S["h_lo"], 1)

            def value(t, f):
                r = c.rows[f]
                v.wait_ge(S["in_ready"], t * (2 * c.NF) + (2 * f + 2))
                v.wait_ge(S["gate_ready"], t * c.NF + (f + 1))
                if f >= RING:
                    v.wait_ge(S["u_hi"], t * c.NF + (f - RING + 1))
                    v.wait_ge(S[["u_lo_dve", "u_lo_pool"][f % 2]], t * 3 + ((f - RING) // 2 + 1))
                nc.vector.scalar_tensor_tensor(hid[f % RING][0:r, :], hidden_bank(c, f, 1)[0:r, :], vec[0:r, 4 + f:5 + f],
                                               gate[f % RING][0:r, :], ALU.add, ALU.mult).then_inc(S["hid_ready"], 1)

            def low(t, f):
                r = c.rows[f]
                src = hid if c.gated else gate
                v.wait_ge(S["u_hi"], t * c.NF + (f + 1))
                if c.gated:
                    v.wait_ge(S["hid_ready"], t * c.NF + (f + 1))
                nc.vector.tensor_tensor(u_lo[0:r, f, :], src[f % RING][0:r, :], u_hi[0:r, f, :].bitcast(F32),
                                        ALU.subtract).then_inc(S["u_lo_dve"], 1)

            def second_product(t, slot):
                v.wait_ge(S["res_ready"], t + 1)
                if c is MLP_B:
                    v.wait_ge(S["store"], t * 32 + 32)
                for i in range(4):
                    if i % 2 == 0:
                        v.wait_ge(S["y_ready"], t * 2 + (i // 2 + 1))
                    y = bank[(6, 7, 2, 3)[i]]
                    nc.vector.tensor_tensor(g_new[:, i, :], y[:, 0:D], g_sum[slot][:, i, :],
                                            ALU.add).then_inc(S["y_added"], 1)
                v.wait_ge(S["y_added"], t * 4 + 4)
                v.wait_ge(S[f"old{slot}"], (t - slot) * 8 + 16)
                nc.vector.tensor_tensor(g_sum[slot][:], g_new[:], g_old[slot][:], ALU.add).then_inc(S["f_sum"], 1)

            def finish_stats(t, slot):
                v.wait_ge(S["f_sum"], t + 1)
                for i in range(4):
                    ins = nc.vector.bn_stats(f_stats[:, i, :], g_sum[slot][:, i, :])
                ins.then_inc(S["f_stats"], 1)
                wait_apart(v, (S["f_stats"], t * 2 + 1))
                for i in range(4):
                    ins = nc.vector.bn_aggr(f_mv[:, i, :], f_stats[:, i, :])
                ins.then_inc(S["f_stats"], 1)
                v.wait_ge(S["f_stats"], t * 2 + 2)
                nc.vector.tensor_scalar_add(f_ve[:], f_mv[:, :, 1], EPS).then_inc(S["f_var"], 1)

            def finish(t, slot):
                if c is MLP_A:
                    v.wait_ge(S["store"], t * 32 + 32)
                else:
                    v.wait_ge(S["out_store"], t * 16 + 16)
                v.wait_ge(S["f_rstd"], t + 1)
                for i in range(4):
                    ins = nc.vector.tensor_scalar(g_fin[:, i, :], g_sum[slot][:, i, :], f_mv[:, i, 0:1],
                                                  f_rstd[:, i:i + 1], ALU.subtract, ALU.mult)
                ins.then_inc(S["fin_ready"], 1)

            def group(t, slot, more, steady=True):
                for f in range(c.NF):
                    if c.gated:
                        value(t, f)
                        if f % 2 == 0:
                            low(t, f)
                    else:
                        low(t, f)
                    if f == 1 and more:
                        norm_stats(t + 1, 1 - slot)
                    if f == 3 and more:
                        normalize(t + 1, 1 - slot)
                if more:
                    gain_bias(t + 1)
                if steady:
                    finish_stats(t - 1, 1 - slot)
                if more:
                    h_low(t + 1)
                if steady:
                    finish(t - 1, 1 - slot)
                if not more:
                    dve_attention(v, ATT_B, SB, next_layer(layer), opening=True)
                second_product(t, slot)

            base = 0 if layer is None else v.snap(layer * NGRP)
            if opening == 0:
                norm_stats(base, 0)
            if opening == 1:
                normalize(base, 0)
            if opening == 2:
                v.wait_ge(S["params"], 16 if layer is None else layer * 32 + 32)
                gain_bias(base)
            if opening is not None:
                return
            h_low(base)
            group(base, 0, True, False)
            with v.Fori(0, NGRP // 2 - 1) as i:
                t0 = v.snap(i * 2 + 1) if layer is None else v.snap(layer * NGRP + i * 2 + 1)
                for e in range(2):
                    group(t0 + e, 1 - e, True)
            group(base + (NGRP - 1), 1, False)
            finish_stats(base + (NGRP - 1), 1)
            finish(base + (NGRP - 1), 1)

        @block.vector
        def _(v):
            nc.vector.memset(zero_row[:], 0.0)
            nc.vector.memset(minus_half[:], -0.5).then_inc(consts_set, 1)
            dve_attention(v, ATT_A, SA, None)
            dve_mlp(v, MLP_A, MA, None)
            with v.Fori(0, LAYERS) as layer:
                dve_attention(v, ATT_B, SB, layer)
                dve_mlp(v, MLP_B, MB, layer)

        def split_high(a, hi, loaded, hi_done, cols, i, before):
            a.wait_ge(loaded, before * 16 + 16)
            at = piece(cols, i)
            nc.scalar.activation(hi[:, at], w_raw[:, at], ACT.Copy).then_inc(hi_done, 1)

        def act_attention(a, c, S, layer, opening=False):
            def split_mlp_high(i):
                split_high(a, wm_hi, wm_loaded, wm_hi_done, next_mlp(c).WCOLS, i,
                           0 if layer is None else layer + 1)

            def h_high(m):
                if c is ATT_A:
                    a.wait_ge(S["h32_ready"], m + 1)
                    nc.scalar.activation(h_hi[:], h32[:], ACT.Copy).then_inc(S["h_hi"], 1)
                else:
                    a.wait_ge(S["xt_ready"], m + 1)
                    nc.scalar.activation(h_hi[:], work[1][:, 0:D], ACT.Copy).then_inc(S["h_hi"], 1)

            def copy_qkv(n, slot, part, steady=True):
                if c is ATT_A:
                    if part == 0:
                        a.wait_ge(S["q_proj"], n + 1)
                        for i, scale, out in ((0, c.DH ** -0.5, q_stack[:, :, 0:2, :]), (1, 1.0, k_stack[:, :, 0:3:2, :])):
                            src = work[1][:, i * 256:i * 256 + 256].rearrange("p (h d) -> p h d", d=c.DH)
                            nc.scalar.activation(out, src.unsqueeze(2).to_broadcast([P, c.NH, 2, c.DH]), ACT.Copy,
                                                 scale=scale).then_inc(S["qk_hi"], 1)
                    elif part == 1:
                        a.wait_ge(S["v_proj"], n + 1)
                        nc.scalar.activation(v_tok[slot][:, 0:c.OC], work[2][:, 0:c.OC], ACT.Copy).then_inc(S["v_copied"], 1)
                    return
                if part < 2:
                    if steady:
                        a.wait_ge(S[["q_parts", "k_parts"][part]], 4 * n)
                    proj, squared = (("q_proj", "q_squared"), ("k_proj", "k_squared"))[part]
                    a.wait_ge(S[proj], n + 1)
                    nc.scalar.activation(qk[part][:], work[1 + part][:], ACT.Copy)
                    nc.scalar.activation(squares[part][:], work[1 + part][:], ACT.Square).then_inc(S[squared], 1)
                else:
                    a.wait_ge(S["v_proj"], n + 1)
                    nc.scalar.activation(v_tok[slot][:], work[0][:], ACT.Copy).then_inc(S["v_copied"], 1)

            def copy_k_t(n, slot, half=0):
                a.wait_ge(S["kt_ready"], n * c.TB + (half + 1))
                src = work[(1 + half) if c is ATT_A else 2][:].rearrange("p (t q) -> p t q", q=P)
                rows = slice(4 * half, 4 * half + 4)
                k_t = k_t_a if c is ATT_A else k_t_hi
                if slot == U - 1 and c is ATT_A:
                    nc.scalar.activation(k_t[:, rows, 0:P], src, ACT.Copy)
                nc.scalar.activation(k_t[:, rows, (slot + 1) * P:(slot + 2) * P], src, ACT.Copy).then_inc(
                    S["kt_copied" if c is ATT_A else "kt_hi"], 1)

            def k_t_to_front(n):
                a.wait_ge(S["kt_copied"], n + 1)
                a.wait_ge(S["kt_hi"], n + 1)
                for k_t in (k_t_hi, k_t_lo):
                    nc.scalar.activation(k_t[:, :, 0:P], k_t[:, :, U * P:(U + 1) * P].bitcast(F32), ACT.Copy)

            def q_t_high(n):
                a.wait_ge(S["qt_ready"], n + 1)
                nc.scalar.activation(q_t_hi[:], work[1][:].rearrange("p (t q) -> p t q", q=P), ACT.Copy).then_inc(
                    S["qt_hi"], 1)

            def exponentials(g, e, p, first=False):
                a.wait_ge(S["masked_ready"], g * c.NP + (p + 1))
                if p >= 2 or not first:
                    a.wait_ge(S["pt_ready"], g * c.NP + (p - 1))
                for hh in range(2):
                    h = c.head(p, hh)
                    cols = slice(hh * 256, hh * 256 + 256)
                    ins = nc.scalar.activation(probs[p % 2][:, cols], masked[p % 2][:, cols], ACT.Exp,
                                               bias=neg_max[:, h:h + 1], scale=-1.0, accum_out=row_sum[:, e % 2, h:h + 1])
                ins.then_inc(S["probs_ready"], 1)

            def copy_probs(g, p):
                by, k, per = evacuator(c, p)
                if by != "pt_act":
                    return
                a.wait_ge(S["pt_ready"], g * c.NP + (p + 1))
                if p >= 2:
                    a.wait_ge(S["pv_done"], g * c.NP + (p - 1))
                nc.scalar.activation(pt[p % 2][:], probs_t[p % 2][:], ACT.Copy).then_inc(S["pt_act"], 1)

            def o_high(g):
                a.wait_ge(S["ot_ready"], g + 1)
                nc.scalar.activation(o_hi[:, 0:c.OC], work[0][:, 0:c.OC], ACT.Copy).then_inc(S["o_hi"], 1)

            if opening:
                h_high(first_chunk(a, layer))
                return

            def prologue(base):
                if c is ATT_A:
                    h_high(base)
                    for i in range(SPLIT):
                        split_high(a, wa_hi, wa_loaded, wa_hi_done, c.WCOLS, i, 0)
                a.wait_ge(S["phase_set"], 2 if layer is None else layer * 2 + 2)
                for part in range(3):
                    copy_qkv(base, 0, part, False)
                if c is ATT_B:
                    h_high(base + 1)
                    for part in range(3):
                        copy_qkv(base + 1, 1, part)
                    a.wait_ge(zero_rows_stored, layer * 32 + 16)
                for k_t in (k_t_a,) if c is ATT_A else (k_t_hi, k_t_lo):
                    nc.scalar.activation(k_t[:, :, 0:P], zero_row[:, 0:1, :].to_broadcast([P, c.NT, P]), ACT.Copy)
                for half in range(c.TB):
                    copy_k_t(base, 0, half)
                if c is ATT_B:
                    q_t_high(base)
                exponentials(base, 0, 0, True)
                if c is ATT_B:
                    h_high(base + 2)
                exponentials(base, 0, 1, True)
                if c is ATT_A:
                    h_high(base + 1)

            def step_a(g, e, j, g_local, more):
                ns = (e + 1) % U
                for p in range(c.NP):
                    copy_probs(g, p)
                    if p + 2 < c.NP:
                        exponentials(g, e, p + 2)
                    elif more[1]:
                        exponentials(g + 1, ns, p + 2 - c.NP)
                    if more[1]:
                        if p < 2:
                            copy_qkv(g + 1, ns, p)
                        elif p < 4:
                            copy_k_t(g + 1, ns, p - 2)
                    if p == 2 and more[-1]:
                        o_high(g - 1)
                    if 2 <= p < 2 + len(pieces_of_step(c, j, e)):
                        split_mlp_high(pieces_of_step(c, j, e)[p - 2])
                    if p == 6 and more[2]:
                        h_high(g + 2)
                if not more[1]:
                    o_high(g)
                    act_mlp(a, next_mlp(c), MA, layer, opening=True)

            def step(g, e, j, g_local, more):
                n, ns = g + 2, (e + 2) % U
                for p in range(c.NP):
                    copy_probs(g, p)
                    if p + 2 < c.NP:
                        exponentials(g, e, p + 2)
                    if p == 0 and e == U - 1 and more[1]:
                        k_t_to_front(g)
                    if p == 2 and more[1]:
                        copy_k_t(g + 1, (e + 1) % U)
                        q_t_high(g + 1)
                    if more[2] and p < 3:
                        copy_qkv(n, ns, p)
                    if p < len(pieces_of_step(c, j, e)):
                        split_mlp_high(pieces_of_step(c, j, e)[p])
                if more[1]:
                    exponentials(g + 1, e + 1, 0)
                if more[3]:
                    h_high(g + 3)
                o_high(g)
                if more[1]:
                    exponentials(g + 1, e + 1, 1)
                else:
                    act_mlp(a, next_mlp(c), MB, layer, opening=True)

            attention_loop(a, c, layer, prologue, step_a if c is ATT_A else step)

        def act_mlp(a, c, S, layer, opening=False):
            vec, b0 = (vec_a, 8) if c is MLP_A else (vec_b, 10)

            def h_high(t):
                a.wait_ge(S["h32_ready"], t * KD + KD)
                nc.scalar.activation(g_h_hi[:], g_h32[:], ACT.Copy).then_inc(S["h_hi"], 1)

            def gates(t, f):
                r = c.rows[f]
                if c.gated:
                    a.wait_ge(S["in_ready"], t * (2 * c.NF) + (2 * f + 1))
                    if f >= RING:
                        a.wait_ge(S["hid_ready"], t * c.NF + (f - RING + 1))
                else:
                    a.wait_ge(S["in_ready"], t * c.NF + (f + 1))
                    if f >= RING:
                        a.wait_ge(S["u_lo_dve"], t * c.NF + (f - RING + 1))
                src = hidden_bank(c, f)
                nc.scalar.activation(gate[f % RING][0:r, :], src[0:r, :], ACT.Gelu,
                                     bias=vec[0:r, b0 + f:b0 + f + 1]).then_inc(S["gate_ready"], 1)

            def high(t, f):
                r = c.rows[f]
                src = hid if c.gated else gate
                a.wait_ge(S["hid_ready"] if c.gated else S["gate_ready"], t * c.NF + (f + 1))
                nc.scalar.activation(u_hi[0:r, f, :], src[f % RING][0:r, :], ACT.Copy).then_inc(S["u_hi"], 1)

            def group(t, more, splits=False):
                gates(t, 0)
                for f in range(c.NF):
                    if f + 1 < c.NF:
                        gates(t, f + 1)
                    high(t, f)
                    for i in range(2 * f, min(SPLIT, 2 * f + 2)) if splits else []:
                        split_high(a, wa_hi, wa_loaded, wa_hi_done, ATT_B.WCOLS, i, 1 if layer is None else layer + 2)
                if more:
                    h_high(t + 1)
                else:
                    act_attention(a, ATT_B, SB, next_layer(layer), opening=True)

            base = 0 if layer is None else a.snap(layer * NGRP)
            if opening:
                h_high(base)
                return
            with a.Fori(0, NGRP - 2) as i:
                group(a.snap(i + 0) if layer is None else a.snap(layer * NGRP + i), True)
            group(base + (NGRP - 2), True, True)
            group(base + (NGRP - 1), False)

        @block.scalar
        def _(a):
            act_attention(a, ATT_A, SA, None)
            act_mlp(a, MLP_A, MA, None)
            with a.Fori(0, LAYERS) as layer:
                act_attention(a, ATT_B, SB, layer)
                act_mlp(a, MLP_B, MB, layer)

        def pool_attention(pool, c, S, layer):
            def set_start(base):
                wait_apart(pool, (S["load0"], 16 if layer is None else layer * (48 * ITERS) + 48))
                if c is ATT_A:
                    nc.gpsimd.memset(q_stack[:].rearrange("p h s d -> p (h s d)").bitcast(F32), 0.0)
                    nc.gpsimd.memset(k_stack[:].rearrange("p h s d -> p (h s d)").bitcast(F32), 0.0).then_inc(
                        S["phase_set"], 1)
                nc.gpsimd.memset(v_tok[U - 1][:], 0.0).then_inc(S["phase_set"], 1 if c is ATT_A else 2)

            def inverse_std(m):
                pool.wait_ge(S["ln_var"], m + 1)
                nc.gpsimd.tensor_tensor(rstd[:], var_eps[:], minus_half[:, 0:1], ALU.pow).then_inc(S["ln_rstd"], 1)

            def tables(n, slot, steady):
                pool.wait_ge(S[f"load{slot}"], load_count(c, n, slot))
                if steady:
                    pool.wait_ge(S["q_parts"], 4 * n)
                    pool.wait_ge(S["k_parts"], 4 * n)
                nc.gpsimd.tensor_tensor(rope[:].rearrange("p a d -> p (a d)"), rope_in[:, slot, :],
                                        rope_scale[:].rearrange("p a d -> p (a d)"), ALU.mult).then_inc(S["rope_ready"], 1)

            def rotate_k(n, steady):
                if steady:
                    pool.wait_ge(S["k_rot"], n)
                pool.wait_ge(S["rope_ready"], n + 1)
                pool.wait_ge(S["k_squared"], n + 1)
                pool.wait_ge(S["norm2_part"], 2 * n + 2)
                rotate(nc.gpsimd, 1, S["k_parts"])
                pool.wait_ge(S["norm2_ready"], n + 1)
                nc.gpsimd.tensor_tensor(rnorm[:], norm2c[:], minus_half[:], ALU.pow).then_inc(S["rnorm_ready"], 1)
                pool.wait_ge(S["k_parts"], 4 * n + 3)
                nc.gpsimd.tensor_tensor(cos_part[1][:], cos_part[1][:], squares[1][:], ALU.add).then_inc(S["k_parts"], 1)

            def prologue(base):
                set_start(base)
                if c is ATT_A:
                    inverse_std(base)
                    inverse_std(base + 1)
                else:
                    pool.wait_ge(S["params"], layer * 64 + 64)
                    tables(base, 0, False)
                    rotate_k(base, False)
                    tables(base + 1, 1, True)
                    rotate_k(base + 1, True)

            def step(g, e, j, g_local, more):
                if c is ATT_A:
                    if more[2]:
                        inverse_std(g + 2)
                elif more[2]:
                    tables(g + 2, (e + 2) % U, True)
                    rotate_k(g + 2, True)
                for i in pieces_of_step(c, j, e):
                    split_low(pool, nc.gpsimd, wm_lo, wm_hi, wm_hi_done, wm_split,
                              next_mlp(c).WCOLS, i, 0 if layer is None else layer + 1)

            attention_loop(pool, c, layer, prologue, step)

        def pool_mlp(pool, c, S, layer):
            def inverse_std(t):
                pool.wait_ge(S["var"], t + 1)
                nc.gpsimd.tensor_tensor(g_rstd[:], g_ve[:], minus_half[:, 0:4], ALU.pow).then_inc(S["rstd"], 1)

            def h_low(t):
                pool.wait_ge(S["h_hi"], t + 1)
                nc.gpsimd.tensor_tensor(g_h_lo[:, 0, :], g_h32[:, 0, :], g_h_hi[:, 0, :].bitcast(F32),
                                        ALU.subtract).then_inc(S["h_lo_pool"], 1)

            def residual(t, slot, steady):
                pool.wait_ge(S[f"load{slot}"], m_load_count(c, t, slot))
                if steady:
                    pool.wait_ge(S["fin_ready"], t - 1)
                src = g_in[slot][:, :, 0:2, :] if c is MLP_A else g_in[slot][:, :, 0:3:2, :]
                for i in range(2):
                    half = slice(i * P, i * P + P)
                    ins = nc.gpsimd.tensor_tensor(g_sum[slot][:, :, half], src[:, :, i, :],
                                                  row_b2[:, half].unsqueeze(1).to_broadcast([P, 4, P]), ALU.add)
                ins.then_inc(S["res_ready"], 1)

            def low(t, f):
                r = c.rows[f]
                pool.wait_ge(S["u_hi"], t * c.NF + (f + 1))
                nc.gpsimd.tensor_tensor(u_lo[0:r, f, :], hid[f % RING][0:r, :], u_hi[0:r, f, :].bitcast(F32),
                                        ALU.subtract).then_inc(S["u_lo_pool"], 1)

            def inverse_std_behind(t):
                pool.wait_ge(S["f_var"], t + 1)
                nc.gpsimd.tensor_tensor(f_rstd[:], f_ve[:], minus_half[:, 0:4], ALU.pow).then_inc(S["f_rstd"], 1)

            def group(t, slot, more, before=True, steady=True):
                if c.gated:
                    low(t, 1)
                if more:
                    inverse_std(t + 1)
                if c.gated:
                    low(t, 3)
                residual(t, slot, steady)
                if c.gated:
                    low(t, 5)
                if more:
                    h_low(t + 1)
                if before:
                    inverse_std_behind(t - 1)

            base = 0 if layer is None else pool.snap(layer * NGRP)
            inverse_std(base)
            h_low(base)
            pool.wait_ge(S["params"], 16 if layer is None else layer * 32 + 32)
            group(base, 0, True, False, False)
            group(base + 1, 1, True, True, False)
            with pool.Fori(0, NGRP // 2 - 2) as i:
                t0 = pool.snap(i * 2 + 2) if layer is None else pool.snap(layer * NGRP + i * 2 + 2)
                for e in range(2):
                    group(t0 + e, e, True)
            group(base + (NGRP - 2), 0, True)
            for i in range(SPLIT):
                split_low(pool, nc.gpsimd, wa_lo, wa_hi, wa_hi_done, wa_split, ATT_B.WCOLS, i,
                          1 if layer is None else layer + 2)
            group(base + (NGRP - 1), 1, False)
            inverse_std_behind(base + (NGRP - 1))
            pool.wait_ge(S["y_ready"], base * 2 + 2 * NGRP)

        @block.gpsimd
        def _(pool):
            pool_attention(pool, ATT_A, SA, None)
            pool_mlp(pool, MLP_A, MA, None)
            with pool.Fori(0, LAYERS) as layer:
                pool_attention(pool, ATT_B, SB, layer)
                pool_mlp(pool, MLP_B, MB, layer)


def contraction_tiles(w, tile=P):
    k, n = w.shape
    tiles = -(-k // tile)
    out = np.zeros((P, tiles, n), np.float32)
    for i in range(tiles):
        part = w[i * tile:(i + 1) * tile]
        out[:part.shape[0], i] = part
    return out.reshape(P, tiles * n)


def columns(*vectors_and_tiles):
    cols = []
    for vec, tile in vectors_and_tiles:
        for i in range(0, len(vec), tile):
            col = np.zeros(P, np.float32)
            col[:len(vec[i:i + tile])] = vec[i:i + tile]
            cols.append(col)
    out = np.zeros((P, 16), np.float32)
    out[:, :len(cols)] = np.stack(cols, 1)
    return out


def window_masks(first_key):
    q, k = np.arange(P)[:, None], np.arange(2 * P)[None, :]
    full = np.where((k >= q + first_key) & (k <= q + P), 0.0, MASKED).astype(np.float32)
    first = np.repeat(full[:, None, :P], ITERS, 1)
    first[:, ::ITERS // B] = MASKED
    return full, np.ascontiguousarray(first)


def rope_tables():
    dim, window, qk_scale = ATT_B.DH, P, 8.0
    half = np.arange(0, dim, 2, dtype=np.float32)
    inv_freq = (np.float32(1.0) / np.float32(10000.0) ** (half / np.float32(dim))).astype(np.float32)
    t = np.arange(SEQ, dtype=np.float32)
    freqs = t[:, None] * inv_freq[None, :]
    cos, sin = np.cos(freqs), np.sin(freqs)
    base = ((half + np.float32(0.4 * dim)) / np.float32(1.4 * dim)).astype(np.float32)
    power = ((t - SEQ // 2) / np.float32(window // 2)).astype(np.float32)
    scale = np.power(base[None, :], power[:, None]).astype(np.float32)
    parts = []
    for s in (scale * np.float32(qk_scale), np.float32(1.0) / scale):
        parts += [np.concatenate([cos * s, cos * s], 1), np.concatenate([-sin * s, sin * s], 1)]
    return np.tile(np.concatenate(parts, 1).astype(np.float32), (B, 1))


def kernel(L0_attn_x, L0_attn_w_qkv, L0_attn_w_o, L0_attn_ln1_g, L0_attn_ln1_b, L0_attn_ln2_g, L0_attn_ln2_b,
           L0_attn_mlp_w1, L0_attn_mlp_b1, L0_attn_mlp_w2, L0_attn_mlp_b2, L0_ffn_wqkv, L0_ffn_q_scale,
           L0_ffn_k_scale, L0_ffn_wo, L0_ffn_ln_g, L0_ffn_ln_b, L0_ffn_w1, L0_ffn_b1, L0_ffn_w2, L0_ffn_b2):
    import concourse.bacc as bacc
    from concourse.bass_utils import run_bass_kernel_spmd

    a = [np.asarray(t) for t in (L0_attn_x, L0_attn_w_qkv, L0_attn_w_o, L0_attn_mlp_w1, L0_attn_mlp_w2)]
    x, w_qkv, w_o, w1, w2 = a
    wqkv_b, wo_b, w1_b, w2_b = (np.asarray(t) for t in (L0_ffn_wqkv, L0_ffn_wo, L0_ffn_w1, L0_ffn_w2))
    qs, ks = np.asarray(L0_ffn_q_scale), np.asarray(L0_ffn_k_scale)
    lg, lb, b1, b2 = (np.asarray(t) for t in (L0_ffn_ln_g, L0_ffn_ln_b, L0_ffn_b1, L0_ffn_b2))
    mask_a, mask_a0 = window_masks(1)
    mask_b, mask_b0 = window_masks(0)

    def swap(s):
        return np.concatenate([s[ATT_B.DH // 2:], s[:ATT_B.DH // 2]])

    H = MLP_B.H
    data = {
        "x": x.reshape(TOK, D),
        "w_att_a": np.concatenate([contraction_tiles(w_qkv.T), contraction_tiles(w_o.T)], 1),
        "w_mlp_a": np.concatenate([contraction_tiles(w1.T), contraction_tiles(w2.T)], 1),
        "w_att_b": np.concatenate([np.concatenate([contraction_tiles(wqkv_b[l]), contraction_tiles(wo_b[l])], 1)
                                   for l in range(LAYERS)], 0),
        "w_mlp_b": np.concatenate([np.concatenate([contraction_tiles(w1_b[l]), contraction_tiles(w2_b[l], MLP_B.FT)], 1)
                                   for l in range(LAYERS)], 0),
        "vec_a": columns((np.asarray(L0_attn_ln1_g), P), (np.asarray(L0_attn_ln1_b), P), (np.asarray(L0_attn_ln2_g), P),
                         (np.asarray(L0_attn_ln2_b), P), (np.asarray(L0_attn_mlp_b1), P)),
        "vec_b": np.concatenate([columns((lg[l], P), (lb[l], P), (b1[l][:H], MLP_B.FT), (b1[l][H:], MLP_B.FT))
                                 for l in range(LAYERS)], 0),
        "b2_a": np.broadcast_to(np.asarray(L0_attn_mlp_b2), (P, D)),
        "b2_b": np.concatenate([np.broadcast_to(b2[l], (P, D)) for l in range(LAYERS)], 0),
        "rope": rope_tables(),
        "rope_scale": np.concatenate([np.broadcast_to(np.concatenate([qs[l], swap(qs[l]), ks[l], swap(ks[l])]), (P, D))
                                      for l in (*range(LAYERS), 0)], 0),
        "mask_a": mask_a, "mask_a0": mask_a0, "mask_b": mask_b, "mask_b0": mask_b0,
        "ident": np.eye(P, dtype=np.float32),
    }
    nc = bacc.Bacc("TRN2", target_bir_lowering=False, num_devices=1)
    arrays, io = {}, {}
    for name, arr in data.items():
        arrays[f"in_{name}"] = np.ascontiguousarray(arr)
        io[name] = nc.dram_tensor(f"in_{name}", arrays[f"in_{name}"].shape, F32, kind="ExternalInput").ap()
    io["out"] = nc.dram_tensor("out_x", (TOK, D), F32, kind="ExternalOutput").ap()
    build(nc, io)
    r = run_bass_kernel_spmd(nc, [arrays], core_ids=[0])
    return r.results[0]["out_x"].reshape(B, SEQ, D)
```
